# Optimizing a Trainium2 kernel written in Bass

```python
import numpy as np
import jax
import jax.numpy as jnp

def _softmax(x, axis=-1):
    return jax.nn.softmax(x, axis=axis)

def _gelu(x):
    return jax.nn.gelu(x, approximate=True)

def _silu(x):
    return jax.nn.silu(x)

def _sigmoid(x):
    return jax.nn.sigmoid(x)

def _layernorm(x, axis=-1, eps=1e-05):
    m = jnp.mean(x, axis=axis, keepdims=True)
    v = jnp.var(x, axis=axis, keepdims=True)
    return (x - m) / jnp.sqrt(v + eps)

def _scatter_add(tgt, idx, src, axis=0):
    return tgt.at[idx].add(src)

def _segment_sum(src, seg, n):
    return jax.ops.segment_sum(src, seg, n)
kernel_name = 'mk_recurrent_d4_jaxref_r8_16ce2c'

def setup_inputs(seed: int=0):
    np.random.seed(seed)
    _w = jnp.asarray

    def _L0_attn_setup():
        import jax, jax.numpy as jnp
        import numpy as np
        DIM = 128
        HEADS = 16
        HEAD_DIM = DIM // HEADS
        B, N = (2, 256)
        SCALE = 1.0 / np.float32(np.sqrt(DIM))

        def _split_heads(t):
            b, n, _ = t.shape
            return jnp.moveaxis(t.reshape(b, n, HEADS, HEAD_DIM), 2, 0)
        key = jax.random.key(seed)
        ks = jax.random.split(key, 9)
        s = 0.02
        return {'x': jax.random.normal(ks[0], (B, N, DIM), dtype=jnp.float32), 'Wq': jax.random.normal(ks[1], (DIM, DIM), dtype=jnp.float32) * s, 'bq': jax.random.normal(ks[2], (DIM,), dtype=jnp.float32) * s, 'Wk': jax.random.normal(ks[3], (DIM, DIM), dtype=jnp.float32) * s, 'bk': jax.random.normal(ks[4], (DIM,), dtype=jnp.float32) * s, 'Wv': jax.random.normal(ks[5], (DIM, DIM), dtype=jnp.float32) * s, 'bv': jax.random.normal(ks[6], (DIM,), dtype=jnp.float32) * s, 'Wo': jax.random.normal(ks[7], (DIM, DIM), dtype=jnp.float32) * s, 'bo': jax.random.normal(ks[8], (DIM,), dtype=jnp.float32) * s}
    _L0_attn_in = _L0_attn_setup()

    def _L0_ffn_setup():
        import jax, jax.numpy as jnp
        import numpy as np
        DIM = 128
        HIDDEN = 384
        SCALE = 1.0 / 127.0

        def _dequant(w_int, dtype):
            return w_int.astype(dtype) * jnp.asarray(SCALE, dtype)
        key = jax.random.key(seed)
        k_x, k_g, k_u, k_d = jax.random.split(key, 4)
        x = jax.random.normal(k_x, (4, 256, DIM), dtype=jnp.float32)
        w_gate = jax.random.randint(k_g, (HIDDEN, DIM), -127, 128, dtype=jnp.int32)
        w_up = jax.random.randint(k_u, (HIDDEN, DIM), -127, 128, dtype=jnp.int32)
        w_down = jax.random.randint(k_d, (DIM, HIDDEN), -127, 128, dtype=jnp.int32)
        return {'x': x, 'w_gate': w_gate, 'w_up': w_up, 'w_down': w_down}
    _L0_ffn_in = _L0_ffn_setup()

    def _L1_attn_setup():
        import jax, jax.numpy as jnp
        import numpy as np
        from jax import lax
        D_MODEL = 128
        DIFF_STEPS = 1
        DIFF_INIT = 0.1

        def _binary_operator_diag(q_i, q_j):
            a_i, b_i = q_i
            a_j, b_j = q_j
            return (a_i * a_j, a_j * b_i + b_j)

        def _parallel_scan(a, b):
            a = jnp.moveaxis(a, 1, 0)
            b = jnp.moveaxis(b, 1, 0)
            _, h = lax.associative_scan(_binary_operator_diag, (a, b))
            return jnp.moveaxis(h, 0, 1)
        key = jax.random.key(seed)
        ks = jax.random.split(key, 5)
        B, T, D = (4, 512, D_MODEL)
        x = jax.random.normal(ks[0], (B, T, D), dtype=jnp.float32)
        s = 1.0 / np.sqrt(D)
        Wz = jax.random.normal(ks[1], (D, D), dtype=jnp.float32) * s
        bz = jnp.zeros((D,), dtype=jnp.float32)
        Wh = jax.random.normal(ks[2], (D, D), dtype=jnp.float32) * s
        bh = jnp.zeros((D,), dtype=jnp.float32)
        log_D = jnp.full((D,), np.log(DIFF_INIT), dtype=jnp.float32)
        return {'x': x, 'Wz': Wz, 'bz': bz, 'Wh': Wh, 'bh': bh, 'log_D': log_D}
    _L1_attn_in = _L1_attn_setup()

    def _L1_ffn_setup():
        import jax, jax.numpy as jnp
        import numpy as np
        B, S, D, H, M, E, K = (4, 256, 128, 256, 64, 8, 2)

        def _layernorm(x, g, b, eps=1e-05):
            mu = x.mean(-1, keepdims=True)
            var = ((x - mu) ** 2).mean(-1, keepdims=True)
            return (x - mu) * jax.lax.rsqrt(var + eps) * g + b

        def _forward(inputs_embeds, enc_W, enc_b, s2c_W, s2c_b, rW1, rb1, rW2, rb2, We1, be1, We2, be2, c2s_W, c2s_b, dec_W, dec_b, ln_g, ln_b):
            b, s, _ = inputs_embeds.shape
            spikes_enc = jax.nn.sigmoid(inputs_embeds @ enc_W + enc_b)
            flat = spikes_enc.reshape(b * s, H)
            cont = flat @ s2c_W + s2c_b
            logits = jnp.tanh(cont @ rW1 + rb1) @ rW2 + rb2
            probs = jax.nn.softmax(logits, axis=-1)
            topw, topi = jax.lax.top_k(probs, K)
            w = topw / topw.sum(-1, keepdims=True)
            gates = (jax.nn.one_hot(topi, E, dtype=cont.dtype) * w[..., None]).sum(1)
            h = jax.nn.relu(jnp.einsum('nm,emh->enh', cont, We1) + be1[:, None, :])
            expert_out = jnp.einsum('enh,ehm->enm', h, We2) + be2[:, None, :]
            output_flat = jnp.einsum('enm,ne->nm', expert_out, gates)
            spikes_moe = jax.nn.sigmoid(output_flat @ c2s_W + c2s_b).reshape(b, s, H)
            decoded = jax.nn.sigmoid(spikes_moe @ dec_W + dec_b)
            return _layernorm(decoded, ln_g, ln_b)
        key = jax.random.key(seed)
        ks = jax.random.split(key, 10)
        r = lambda k, shape: jax.random.normal(k, shape, dtype=jnp.float32) * 0.02
        return {'inputs_embeds': jax.random.normal(ks[0], (B, S, D), dtype=jnp.float32), 'enc_W': r(ks[1], (D, H)), 'enc_b': jnp.zeros((H,), jnp.float32), 's2c_W': r(ks[2], (H, M)), 's2c_b': jnp.zeros((M,), jnp.float32), 'rW1': r(ks[3], (M, 64)), 'rb1': jnp.zeros((64,), jnp.float32), 'rW2': r(ks[4], (64, E)), 'rb2': jnp.zeros((E,), jnp.float32), 'We1': r(ks[5], (E, M, H // 2)), 'be1': jnp.zeros((E, H // 2), jnp.float32), 'We2': r(ks[6], (E, H // 2, M)), 'be2': jnp.zeros((E, M), jnp.float32), 'c2s_W': r(ks[7], (M, H)), 'c2s_b': jnp.zeros((H,), jnp.float32), 'dec_W': r(ks[8], (H, D)), 'dec_b': jnp.zeros((D,), jnp.float32), 'ln_g': jnp.ones((D,), jnp.float32), 'ln_b': jnp.zeros((D,), jnp.float32)}
    _L1_ffn_in = _L1_ffn_setup()

    def _L2_attn_setup():
        import math
        import jax, jax.numpy as jnp
        import numpy as np
        N_HEAD = 16

        def _reference_tuple_inner(x, W_dq, W_uq, W_dkv, W_uk, W_uv, W_o):
            B, T, C = x.shape
            nh = N_HEAD
            hs = C // nh
            kvl = W_dkv.shape[0]
            k_eff = (W_dq.T @ W_uq.T @ W_uk).reshape(nh, hs, kvl)
            v_eff = (W_uv.T @ W_o.T).reshape(kvl, nh, hs).transpose(1, 0, 2)
            c_kv = x @ W_dkv.T
            q = (x @ W_dq.T @ W_uq.T).reshape(B, T, nh, hs).transpose(0, 2, 1, 3)
            q_lat = jnp.einsum('bhtd,hdl->bhtl', q, k_eff)
            attn = jnp.einsum('bhtl,bsl->bhts', q_lat, c_kv) / math.sqrt(hs)
            causal_mask = jnp.triu(jnp.ones((T, T), bool), k=1)
            attn = jnp.where(causal_mask[None, None], -jnp.inf, attn)
            attn = jax.nn.softmax(attn, axis=-1)
            ctx = jnp.einsum('bhts,bsl->bhtl', attn, c_kv)
            y = jnp.einsum('bhtl,hld->bhtd', ctx, v_eff).transpose(0, 2, 1, 3).reshape(B, T, C)
            return (y, c_kv)
        key = jax.random.key(seed)
        ks = jax.random.split(key, 7)
        B, T, C = (4, 256, 128)
        QL, KVL = (32, 32)
        s = 0.02
        return {'x': jax.random.normal(ks[0], (B, T, C), jnp.float32), 'W_dq': jax.random.normal(ks[1], (QL, C), jnp.float32) * s, 'W_uq': jax.random.normal(ks[2], (C, QL), jnp.float32) * s, 'W_dkv': jax.random.normal(ks[3], (KVL, C), jnp.float32) * s, 'W_uk': jax.random.normal(ks[4], (C, KVL), jnp.float32) * s, 'W_uv': jax.random.normal(ks[5], (C, KVL), jnp.float32) * s, 'W_o': jax.random.normal(ks[6], (C, C), jnp.float32) * s}
    _L2_attn_in = _L2_attn_setup()

    def _L2_ffn_setup():
        import jax, jax.numpy as jnp
        import numpy as np
        B, T, C = (2, 128, 128)
        H = 512
        E_R, E_S, K = (8, 2, 2)

        def _rmsnorm(x, g):
            eps = jnp.finfo(x.dtype).eps
            return x * jax.lax.rsqrt(jnp.mean(x * x, axis=-1, keepdims=True) + eps) * g

        def _experts_mlp(x, g, W1, b1, W2, b2):
            xn = _rmsnorm(x, g)
            h = jnp.einsum('btc,ech->bteh', xn, W1) + b1
            h = jax.nn.gelu(h, approximate=False)
            return jnp.einsum('bteh,ehc->btec', h, W2) + b2
        key = jax.random.key(seed)
        ks = jax.random.split(key, 12)
        s = 0.02
        return {'u': jax.random.normal(ks[0], (B, T, C), dtype=jnp.float32), 'g_shared': jnp.ones((C,), jnp.float32), 'W1_s': jax.random.normal(ks[1], (E_S, C, H), jnp.float32) * s, 'b1_s': jax.random.normal(ks[2], (E_S, H), jnp.float32) * s, 'W2_s': jax.random.normal(ks[3], (E_S, H, C), jnp.float32) * s, 'b2_s': jax.random.normal(ks[4], (E_S, C), jnp.float32) * s, 'g_routed': jnp.ones((C,), jnp.float32), 'W1_r': jax.random.normal(ks[5], (E_R, C, H), jnp.float32) * s, 'b1_r': jax.random.normal(ks[6], (E_R, H), jnp.float32) * s, 'W2_r': jax.random.normal(ks[7], (E_R, H, C), jnp.float32) * s, 'b2_r': jax.random.normal(ks[8], (E_R, C), jnp.float32) * s, 'centroids': jax.random.normal(ks[9], (C, E_R), jnp.float32) * s}
    _L2_ffn_in = _L2_ffn_setup()

    def _L3_attn_setup():
        import jax, jax.numpy as jnp
        import numpy as np
        D_MODEL = 128
        NUM_HEADS = 16
        D_K = D_MODEL // NUM_HEADS
        ROPE_THETA = 10000.0
        MAX_SEQ_LEN = 256

        def _rope_tables():
            dim_index = jnp.arange(D_K // 2, dtype=jnp.float32)
            pos = jnp.arange(MAX_SEQ_LEN, dtype=jnp.float32)
            theta_inv = ROPE_THETA ** (-2.0 * dim_index / D_K)
            ang = pos[:, None] * theta_inv[None, :]
            return (jnp.sin(ang), jnp.cos(ang))

        def _apply_rope(x, positions, sin, cos):
            s = sin[positions]
            c = cos[positions]
            x_even = x[..., ::2]
            x_odd = x[..., 1::2]
            y_even = x_even * c - x_odd * s
            y_odd = x_even * s + x_odd * c
            y = jnp.stack([y_even, y_odd], axis=-1)
            return y.reshape(x.shape)
        key = jax.random.key(seed)
        k0, k1, k2, k3, k4 = jax.random.split(key, 5)
        std = np.sqrt(2.0 / (D_MODEL + D_MODEL))
        in_features = jax.random.normal(k0, (2, 256, D_MODEL), dtype=jnp.float32)
        W_q = jax.random.normal(k1, (D_MODEL, D_MODEL), dtype=jnp.float32) * std
        W_k = jax.random.normal(k2, (D_MODEL, D_MODEL), dtype=jnp.float32) * std
        W_v = jax.random.normal(k3, (D_MODEL, D_MODEL), dtype=jnp.float32) * std
        W_o = jax.random.normal(k4, (D_MODEL, D_MODEL), dtype=jnp.float32) * std
        return {'in_features': in_features, 'W_q': W_q, 'W_k': W_k, 'W_v': W_v, 'W_o': W_o}
    _L3_attn_in = _L3_attn_setup()

    def _L3_ffn_setup():
        import math
        import jax, jax.numpy as jnp
        import numpy as np
        B, L, D, FF, E, K = (4, 256, 128, 512, 8, 2)
        CAPACITY_FACTOR = 1.25
        T = B * L
        CAP = math.ceil(CAPACITY_FACTOR * T * K / E)
        key = jax.random.key(seed)
        ks = jax.random.split(key, 7)
        return {'h': jax.random.normal(ks[0], (B, L, D), dtype=jnp.float32), 'gate_w': 0.02 * jax.random.normal(ks[1], (E, D), dtype=jnp.float32), 'gate_b': jnp.zeros((E,), dtype=jnp.float32), 'W1': 0.02 * jax.random.normal(ks[2], (E, D, FF), dtype=jnp.float32), 'b1': jnp.zeros((E, FF), dtype=jnp.float32), 'W2': 0.02 * jax.random.normal(ks[3], (E, FF, D), dtype=jnp.float32), 'b2': jnp.zeros((E, D), dtype=jnp.float32)}
    _L3_ffn_in = _L3_ffn_setup()
    _d = {'L0_attn_x': _L0_attn_in['x'], 'L0_attn_Wq': _L0_attn_in['Wq'], 'L0_attn_bq': _L0_attn_in['bq'], 'L0_attn_Wk': _L0_attn_in['Wk'], 'L0_attn_bk': _L0_attn_in['bk'], 'L0_attn_Wv': _L0_attn_in['Wv'], 'L0_attn_bv': _L0_attn_in['bv'], 'L0_attn_Wo': _L0_attn_in['Wo'], 'L0_attn_bo': _L0_attn_in['bo'], 'L0_ffn_w_gate': _L0_ffn_in['w_gate'], 'L0_ffn_w_up': _L0_ffn_in['w_up'], 'L0_ffn_w_down': _L0_ffn_in['w_down'], 'L1_attn_Wz': _L1_attn_in['Wz'], 'L1_attn_bz': _L1_attn_in['bz'], 'L1_attn_Wh': _L1_attn_in['Wh'], 'L1_attn_bh': _L1_attn_in['bh'], 'L1_attn_log_D': _L1_attn_in['log_D'], 'L1_ffn_enc_W': _L1_ffn_in['enc_W'], 'L1_ffn_enc_b': _L1_ffn_in['enc_b'], 'L1_ffn_s2c_W': _L1_ffn_in['s2c_W'], 'L1_ffn_s2c_b': _L1_ffn_in['s2c_b'], 'L1_ffn_rW1': _L1_ffn_in['rW1'], 'L1_ffn_rb1': _L1_ffn_in['rb1'], 'L1_ffn_rW2': _L1_ffn_in['rW2'], 'L1_ffn_rb2': _L1_ffn_in['rb2'], 'L1_ffn_We1': _L1_ffn_in['We1'], 'L1_ffn_be1': _L1_ffn_in['be1'], 'L1_ffn_We2': _L1_ffn_in['We2'], 'L1_ffn_be2': _L1_ffn_in['be2'], 'L1_ffn_c2s_W': _L1_ffn_in['c2s_W'], 'L1_ffn_c2s_b': _L1_ffn_in['c2s_b'], 'L1_ffn_dec_W': _L1_ffn_in['dec_W'], 'L1_ffn_dec_b': _L1_ffn_in['dec_b'], 'L1_ffn_ln_g': _L1_ffn_in['ln_g'], 'L1_ffn_ln_b': _L1_ffn_in['ln_b'], 'L2_attn_W_dq': _L2_attn_in['W_dq'], 'L2_attn_W_uq': _L2_attn_in['W_uq'], 'L2_attn_W_dkv': _L2_attn_in['W_dkv'], 'L2_attn_W_uk': _L2_attn_in['W_uk'], 'L2_attn_W_uv': _L2_attn_in['W_uv'], 'L2_attn_W_o': _L2_attn_in['W_o'], 'L2_ffn_g_shared': _L2_ffn_in['g_shared'], 'L2_ffn_W1_s': _L2_ffn_in['W1_s'], 'L2_ffn_b1_s': _L2_ffn_in['b1_s'], 'L2_ffn_W2_s': _L2_ffn_in['W2_s'], 'L2_ffn_b2_s': _L2_ffn_in['b2_s'], 'L2_ffn_g_routed': _L2_ffn_in['g_routed'], 'L2_ffn_W1_r': _L2_ffn_in['W1_r'], 'L2_ffn_b1_r': _L2_ffn_in['b1_r'], 'L2_ffn_W2_r': _L2_ffn_in['W2_r'], 'L2_ffn_b2_r': _L2_ffn_in['b2_r'], 'L2_ffn_centroids': _L2_ffn_in['centroids'], 'L3_attn_W_q': _L3_attn_in['W_q'], 'L3_attn_W_k': _L3_attn_in['W_k'], 'L3_attn_W_v': _L3_attn_in['W_v'], 'L3_attn_W_o': _L3_attn_in['W_o'], 'L3_ffn_gate_w': _L3_ffn_in['gate_w'], 'L3_ffn_gate_b': _L3_ffn_in['gate_b'], 'L3_ffn_W1': _L3_ffn_in['W1'], 'L3_ffn_b1': _L3_ffn_in['b1'], 'L3_ffn_W2': _L3_ffn_in['W2'], 'L3_ffn_b2': _L3_ffn_in['b2']}
    _x0 = _d['L0_attn_x']
    _d['L0_attn_x'] = jax.random.normal(jax.random.fold_in(jax.random.key(seed), 1), (16, 256, 128), dtype=_x0.dtype)
    del _x0
    return _d

def reference(L0_attn_x, L0_attn_Wq, L0_attn_bq, L0_attn_Wk, L0_attn_bk, L0_attn_Wv, L0_attn_bv, L0_attn_Wo, L0_attn_bo, L0_ffn_w_gate, L0_ffn_w_up, L0_ffn_w_down, L1_attn_Wz, L1_attn_bz, L1_attn_Wh, L1_attn_bh, L1_attn_log_D, L1_ffn_enc_W, L1_ffn_enc_b, L1_ffn_s2c_W, L1_ffn_s2c_b, L1_ffn_rW1, L1_ffn_rb1, L1_ffn_rW2, L1_ffn_rb2, L1_ffn_We1, L1_ffn_be1, L1_ffn_We2, L1_ffn_be2, L1_ffn_c2s_W, L1_ffn_c2s_b, L1_ffn_dec_W, L1_ffn_dec_b, L1_ffn_ln_g, L1_ffn_ln_b, L2_attn_W_dq, L2_attn_W_uq, L2_attn_W_dkv, L2_attn_W_uk, L2_attn_W_uv, L2_attn_W_o, L2_ffn_g_shared, L2_ffn_W1_s, L2_ffn_b1_s, L2_ffn_W2_s, L2_ffn_b2_s, L2_ffn_g_routed, L2_ffn_W1_r, L2_ffn_b1_r, L2_ffn_W2_r, L2_ffn_b2_r, L2_ffn_centroids, L3_attn_W_q, L3_attn_W_k, L3_attn_W_v, L3_attn_W_o, L3_ffn_gate_w, L3_ffn_gate_b, L3_ffn_W1, L3_ffn_b1, L3_ffn_W2, L3_ffn_b2):

    def _L0_attn_ref(x, Wq, bq, Wk, bk, Wv, bv, Wo, bo):
        import jax, jax.numpy as jnp
        import numpy as np
        DIM = 128
        HEADS = 16
        HEAD_DIM = DIM // HEADS
        B, N = (2, 256)
        SCALE = 1.0 / np.float32(np.sqrt(DIM))

        def _split_heads(t):
            b, n, _ = t.shape
            return jnp.moveaxis(t.reshape(b, n, HEADS, HEAD_DIM), 2, 0)
        q = _split_heads(x @ Wq.T + bq)
        k = _split_heads(x @ Wk.T + bk)
        v = _split_heads(x @ Wv.T + bv)
        scores = jnp.einsum('hbnd,hbmd->hbnm', k, q) * SCALE
        attn = jax.nn.softmax(scores, axis=-1)
        out = jnp.einsum('hbnm,hbmd->hbnd', attn, v)
        out = jnp.moveaxis(out, 0, 2).reshape(x.shape[0], x.shape[1], DIM)
        return out @ Wo.T + bo

    def _L0_ffn_ref(x, w_gate, w_up, w_down):
        import jax, jax.numpy as jnp
        import numpy as np
        DIM = 128
        HIDDEN = 384
        SCALE = 1.0 / 127.0

        def _dequant(w_int, dtype):
            return w_int.astype(dtype) * jnp.asarray(SCALE, dtype)
        wg = _dequant(w_gate, x.dtype)
        wu = _dequant(w_up, x.dtype)
        wd = _dequant(w_down, x.dtype)
        gate = jnp.einsum('bsd,hd->bsh', x, wg)
        up = jnp.einsum('bsd,hd->bsh', x, wu)
        h = jax.nn.silu(gate) * up
        return jnp.einsum('bsh,dh->bsd', h, wd)

    def _L1_attn_ref(x, Wz, bz, Wh, bh, log_D):
        import jax, jax.numpy as jnp
        import numpy as np
        from jax import lax
        D_MODEL = 128
        DIFF_STEPS = 1
        DIFF_INIT = 0.1

        def _binary_operator_diag(q_i, q_j):
            a_i, b_i = q_i
            a_j, b_j = q_j
            return (a_i * a_j, a_j * b_i + b_j)

        def _parallel_scan(a, b):
            a = jnp.moveaxis(a, 1, 0)
            b = jnp.moveaxis(b, 1, 0)
            _, h = lax.associative_scan(_binary_operator_diag, (a, b))
            return jnp.moveaxis(h, 0, 1)
        z = jax.nn.sigmoid(x @ Wz + bz)
        h_tilde = x @ Wh + bh
        a = 1.0 - z
        b = z * h_tilde
        h = _parallel_scan(a, b)
        Dcoef = jnp.exp(log_D)
        for _ in range(DIFF_STEPS):
            h_left = jnp.roll(h, 1, axis=-1)
            h_right = jnp.roll(h, -1, axis=-1)
            h = h + Dcoef * (h_left - 2.0 * h + h_right)
        return h

    def _L1_ffn_ref(inputs_embeds, enc_W, enc_b, s2c_W, s2c_b, rW1, rb1, rW2, rb2, We1, be1, We2, be2, c2s_W, c2s_b, dec_W, dec_b, ln_g, ln_b):
        import jax, jax.numpy as jnp
        import numpy as np
        B, S, D, H, M, E, K = (4, 256, 128, 256, 64, 8, 2)

        def _layernorm(x, g, b, eps=1e-05):
            mu = x.mean(-1, keepdims=True)
            var = ((x - mu) ** 2).mean(-1, keepdims=True)
            return (x - mu) * jax.lax.rsqrt(var + eps) * g + b

        def _forward(inputs_embeds, enc_W, enc_b, s2c_W, s2c_b, rW1, rb1, rW2, rb2, We1, be1, We2, be2, c2s_W, c2s_b, dec_W, dec_b, ln_g, ln_b):
            b, s, _ = inputs_embeds.shape
            spikes_enc = jax.nn.sigmoid(inputs_embeds @ enc_W + enc_b)
            flat = spikes_enc.reshape(b * s, H)
            cont = flat @ s2c_W + s2c_b
            logits = jnp.tanh(cont @ rW1 + rb1) @ rW2 + rb2
            probs = jax.nn.softmax(logits, axis=-1)
            topw, topi = jax.lax.top_k(probs, K)
            w = topw / topw.sum(-1, keepdims=True)
            gates = (jax.nn.one_hot(topi, E, dtype=cont.dtype) * w[..., None]).sum(1)
            h = jax.nn.relu(jnp.einsum('nm,emh->enh', cont, We1) + be1[:, None, :])
            expert_out = jnp.einsum('enh,ehm->enm', h, We2) + be2[:, None, :]
            output_flat = jnp.einsum('enm,ne->nm', expert_out, gates)
            spikes_moe = jax.nn.sigmoid(output_flat @ c2s_W + c2s_b).reshape(b, s, H)
            decoded = jax.nn.sigmoid(spikes_moe @ dec_W + dec_b)
            return _layernorm(decoded, ln_g, ln_b)
        return _forward(inputs_embeds, enc_W, enc_b, s2c_W, s2c_b, rW1, rb1, rW2, rb2, We1, be1, We2, be2, c2s_W, c2s_b, dec_W, dec_b, ln_g, ln_b)

    def _L2_attn_ref(x, W_dq, W_uq, W_dkv, W_uk, W_uv, W_o):
        import math
        import jax, jax.numpy as jnp
        import numpy as np
        N_HEAD = 16

        def _reference_tuple_inner(x, W_dq, W_uq, W_dkv, W_uk, W_uv, W_o):
            B, T, C = x.shape
            nh = N_HEAD
            hs = C // nh
            kvl = W_dkv.shape[0]
            k_eff = (W_dq.T @ W_uq.T @ W_uk).reshape(nh, hs, kvl)
            v_eff = (W_uv.T @ W_o.T).reshape(kvl, nh, hs).transpose(1, 0, 2)
            c_kv = x @ W_dkv.T
            q = (x @ W_dq.T @ W_uq.T).reshape(B, T, nh, hs).transpose(0, 2, 1, 3)
            q_lat = jnp.einsum('bhtd,hdl->bhtl', q, k_eff)
            attn = jnp.einsum('bhtl,bsl->bhts', q_lat, c_kv) / math.sqrt(hs)
            causal_mask = jnp.triu(jnp.ones((T, T), bool), k=1)
            attn = jnp.where(causal_mask[None, None], -jnp.inf, attn)
            attn = jax.nn.softmax(attn, axis=-1)
            ctx = jnp.einsum('bhts,bsl->bhtl', attn, c_kv)
            y = jnp.einsum('bhtl,hld->bhtd', ctx, v_eff).transpose(0, 2, 1, 3).reshape(B, T, C)
            return (y, c_kv)
        return _reference_tuple_inner(x, W_dq, W_uq, W_dkv, W_uk, W_uv, W_o)[0]

    def _L2_ffn_ref(u, g_shared, W1_s, b1_s, W2_s, b2_s, g_routed, W1_r, b1_r, W2_r, b2_r, centroids):
        import jax, jax.numpy as jnp
        import numpy as np
        B, T, C = (2, 128, 128)
        H = 512
        E_R, E_S, K = (8, 2, 2)

        def _rmsnorm(x, g):
            eps = jnp.finfo(x.dtype).eps
            return x * jax.lax.rsqrt(jnp.mean(x * x, axis=-1, keepdims=True) + eps) * g

        def _experts_mlp(x, g, W1, b1, W2, b2):
            xn = _rmsnorm(x, g)
            h = jnp.einsum('btc,ech->bteh', xn, W1) + b1
            h = jax.nn.gelu(h, approximate=False)
            return jnp.einsum('bteh,ehc->btec', h, W2) + b2
        h_s = _experts_mlp(u, g_shared, W1_s, b1_s, W2_s, b2_s).sum(axis=-2)
        scores = jax.nn.sigmoid(u @ centroids)
        gpk, i_topk = jax.lax.top_k(scores, K)
        gk = gpk / scores.sum(axis=-1, keepdims=True)
        routed_all = _experts_mlp(u, g_routed, W1_r, b1_r, W2_r, b2_r)
        routed_topk = jnp.take_along_axis(routed_all, i_topk[..., None], axis=2)
        h_r = (gk[..., None] * routed_topk).sum(axis=-2)
        return u + h_s + h_r

    def _L3_attn_ref(in_features, W_q, W_k, W_v, W_o):
        import jax, jax.numpy as jnp
        import numpy as np
        D_MODEL = 128
        NUM_HEADS = 16
        D_K = D_MODEL // NUM_HEADS
        ROPE_THETA = 10000.0
        MAX_SEQ_LEN = 256

        def _rope_tables():
            dim_index = jnp.arange(D_K // 2, dtype=jnp.float32)
            pos = jnp.arange(MAX_SEQ_LEN, dtype=jnp.float32)
            theta_inv = ROPE_THETA ** (-2.0 * dim_index / D_K)
            ang = pos[:, None] * theta_inv[None, :]
            return (jnp.sin(ang), jnp.cos(ang))

        def _apply_rope(x, positions, sin, cos):
            s = sin[positions]
            c = cos[positions]
            x_even = x[..., ::2]
            x_odd = x[..., 1::2]
            y_even = x_even * c - x_odd * s
            y_odd = x_even * s + x_odd * c
            y = jnp.stack([y_even, y_odd], axis=-1)
            return y.reshape(x.shape)
        B, S, _ = in_features.shape
        sin, cos = _rope_tables()
        positions = jnp.arange(S)

        def proj(W):
            y = jnp.einsum('bsd,od->bso', in_features, W)
            return y.reshape(B, S, NUM_HEADS, D_K).transpose(0, 2, 1, 3)
        Q = _apply_rope(proj(W_q), positions, sin, cos)
        K = _apply_rope(proj(W_k), positions, sin, cos)
        V = proj(W_v)
        scores = jnp.einsum('bhnd,bhmd->bhnm', Q, K) / jnp.sqrt(jnp.float32(D_K))
        causal = jnp.tril(jnp.ones((S, S), dtype=bool))
        scores = jnp.where(causal[None, None], scores, -jnp.inf)
        attn = jax.nn.softmax(scores, axis=-1)
        head = jnp.einsum('bhnm,bhmd->bhnd', attn, V)
        head = head.transpose(0, 2, 1, 3).reshape(B, S, D_MODEL)
        return jnp.einsum('bso,do->bsd', head, W_o.T.T) if False else jnp.einsum('bsi,oi->bso', head, W_o)

    def _L3_ffn_ref(h, gate_w, gate_b, W1, b1, W2, b2):
        import math
        import jax, jax.numpy as jnp
        import numpy as np
        B, L, D, FF, E, K = (4, 256, 128, 512, 8, 2)
        CAPACITY_FACTOR = 1.25
        T = B * L
        CAP = math.ceil(CAPACITY_FACTOR * T * K / E)
        Bb, Ll, Dm = h.shape
        Tt = Bb * Ll
        x = h.reshape(Tt, Dm)
        logits = x @ gate_w.T + gate_b
        probs = jax.nn.softmax(logits, axis=-1)
        topk_prob, topk_idx = jax.lax.top_k(probs, K)
        y = jnp.zeros((Tt, Dm), dtype=h.dtype)
        n_slots = E * CAP
        for c in range(K):
            idx = topk_idx[:, c]
            prb = topk_prob[:, c]
            oh = jax.nn.one_hot(idx, E, dtype=jnp.int32)
            pos = jnp.take_along_axis(jnp.cumsum(oh, axis=0) - 1, idx[:, None], axis=1)[:, 0]
            keep = pos < CAP
            buf_idx = jnp.where(keep, idx * CAP + pos, n_slots)
            xbuf = jnp.zeros((n_slots, Dm), x.dtype).at[buf_idx].set(x, mode='drop')
            xb = xbuf.reshape(E, CAP, Dm)
            hmid = jax.nn.relu(jnp.einsum('ecd,edf->ecf', xb, W1) + b1[:, None, :])
            yb = jnp.einsum('ecf,efd->ecd', hmid, W2) + b2[:, None, :]
            ytok = yb.reshape(n_slots, Dm)[jnp.clip(buf_idx, 0, n_slots - 1)]
            y = y + ytok * (prb * keep.astype(prb.dtype))[:, None]
        return y.reshape(Bb, Ll, Dm)
    x = L0_attn_x
    xn = _layernorm(x, axis=-1)
    s = _L0_attn_ref(xn, L0_attn_Wq, L0_attn_bq, L0_attn_Wk, L0_attn_bk, L0_attn_Wv, L0_attn_bv, L0_attn_Wo, L0_attn_bo)
    g = _silu(_L0_ffn_ref(xn, L0_ffn_w_gate, L0_ffn_w_up, L0_ffn_w_down))
    x = x + s * g
    xn = _layernorm(x, axis=-1)
    s = _L1_attn_ref(xn, L1_attn_Wz, L1_attn_bz, L1_attn_Wh, L1_attn_bh, L1_attn_log_D)
    g = _silu(_L1_ffn_ref(xn, L1_ffn_enc_W, L1_ffn_enc_b, L1_ffn_s2c_W, L1_ffn_s2c_b, L1_ffn_rW1, L1_ffn_rb1, L1_ffn_rW2, L1_ffn_rb2, L1_ffn_We1, L1_ffn_be1, L1_ffn_We2, L1_ffn_be2, L1_ffn_c2s_W, L1_ffn_c2s_b, L1_ffn_dec_W, L1_ffn_dec_b, L1_ffn_ln_g, L1_ffn_ln_b))
    x = x + s * g
    xn = _layernorm(x, axis=-1)
    s = _L2_attn_ref(xn, L2_attn_W_dq, L2_attn_W_uq, L2_attn_W_dkv, L2_attn_W_uk, L2_attn_W_uv, L2_attn_W_o)
    g = _silu(_L2_ffn_ref(xn, L2_ffn_g_shared, L2_ffn_W1_s, L2_ffn_b1_s, L2_ffn_W2_s, L2_ffn_b2_s, L2_ffn_g_routed, L2_ffn_W1_r, L2_ffn_b1_r, L2_ffn_W2_r, L2_ffn_b2_r, L2_ffn_centroids))
    x = x + s * g
    xn = _layernorm(x, axis=-1)
    s = _L3_attn_ref(xn, L3_attn_W_q, L3_attn_W_k, L3_attn_W_v, L3_attn_W_o)
    g = _silu(_L3_ffn_ref(xn, L3_ffn_gate_w, L3_ffn_gate_b, L3_ffn_W1, L3_ffn_b1, L3_ffn_W2, L3_ffn_b2))
    x = x + s * g
    return x

_drawn_inputs = setup_inputs


def setup_inputs(seed=0):
    import zlib

    import numpy as np

    out = dict(_drawn_inputs(seed))
    spreads = {'L1_attn_bz': (0.0, 0.8),
     'L1_attn_bh': (0.0, 0.641),
     'L1_attn_log_D': (-2.3025851249694824, 0.6),
     'L1_ffn_enc_b': (0.0, 0.8),
     'L1_ffn_s2c_b': (0.0, 0.8),
     'L1_ffn_rb1': (0.0, 0.8),
     'L1_ffn_rb2': (0.0, 0.8),
     'L1_ffn_be1': (0.0, 0.8),
     'L1_ffn_be2': (0.0, 0.8),
     'L1_ffn_c2s_b': (0.0, 0.8),
     'L1_ffn_dec_b': (0.0, 0.1),
     'L1_ffn_ln_g': (1.0, 0.6),
     'L1_ffn_ln_b': (0.0, 0.8),
     'L2_ffn_g_shared': (1.0, 0.6),
     'L2_ffn_g_routed': (1.0, 0.6),
     'L3_ffn_gate_b': (0.0, 0.8),
     'L3_ffn_b1': (0.0, 0.8),
     'L3_ffn_b2': (0.0, 0.8)}
    factors = {'L0_attn_Wq': 8.0,
     'L0_attn_bq': 8.0,
     'L0_attn_Wk': 8.0,
     'L0_attn_bk': 8.0,
     'L1_ffn_enc_W': 8.0,
     'L1_ffn_s2c_W': 8.0,
     'L1_ffn_rW1': 8.0,
     'L1_ffn_rW2': 8.0,
     'L1_ffn_We1': 8.0,
     'L1_ffn_We2': 8.0,
     'L1_ffn_c2s_W': 8.0,
     'L2_attn_W_dq': 8.0,
     'L2_attn_W_uq': 8.0,
     'L2_attn_W_dkv': 8.0,
     'L2_attn_W_uk': 8.0,
     'L2_attn_W_uv': 8.0,
     'L2_attn_W_o': 8.0,
     'L2_ffn_W1_s': 8.0,
     'L2_ffn_b1_s': 8.0,
     'L2_ffn_W2_s': 8.0,
     'L2_ffn_b2_s': 8.0,
     'L2_ffn_W1_r': 8.0,
     'L2_ffn_b1_r': 8.0,
     'L2_ffn_W2_r': 8.0,
     'L2_ffn_b2_r': 8.0,
     'L2_ffn_centroids': 8.0,
     'L3_attn_W_q': 8.0,
     'L3_attn_W_k': 8.0,
     'L3_attn_W_v': 8.0,
     'L3_attn_W_o': 8.0,
     'L3_ffn_gate_w': 8.0,
     'L3_ffn_W1': 8.0,
     'L3_ffn_W2': 8.0}
    for name, (base, spread) in spreads.items():
        noise = np.random.default_rng([zlib.crc32(name.encode()), seed]).standard_normal(out[name].shape)
        drawn = base * np.exp(spread * noise) if base else spread * noise
        out[name] = jnp.asarray(drawn.astype(out[name].dtype))
    for name, factor in factors.items():
        out[name] = (out[name] * factor).astype(out[name].dtype)
    return out
```

```python
from contextlib import ExitStack

import numpy as np
import concourse.bass as bass
from concourse import mybir

F32 = mybir.dt.float32
BF16 = mybir.dt.bfloat16
I32 = mybir.dt.int32
U32 = mybir.dt.uint32
ACT = mybir.ActivationFunctionType
ALU = mybir.AluOpType
AX = mybir.AxisListType

P = 128
B, N, D = 16, 256, 128
TT = N // P
HEADS, HD = 16, 8
GROUPS = HEADS // 4
SLOTS = 6
ROWS = SLOTS * HD
SHIFT_ROW = 64
SLICES = 8
SHIFT_SLICE = (6, 2)
PRING = 8
PART_RUNS = (((0, 0, 3, True), (3, 1, 2, True), (5, 2, 1, False)),
             ((0, 0, 3, False), (3, 0, 2, False), (5, 0, 1, False)))
MASKED = -1e30
CAPACITY = 320


class Steps:

    def __init__(self, sem, names, by=1):
        self.sem, self.names, self.by = sem, names.split() if isinstance(names, str) else names, by

    def at(self, b, name):
        return (b * len(self.names) + self.names.index(name) + 1) * self.by


def exists(b):
    return not isinstance(b, int) or b >= 0


class Body:

    def __init__(self, t, parity, inside):
        self.t, self.parity, self.inside = t, parity, inside

    def batch(self, ahead):
        b = self.t + ahead
        return b if self.inside or 0 <= b < B else None


FIRST_LOOPED, LOOPS = 2, 6


def turns(eng, body):
    for t in range(-2, FIRST_LOOPED):
        body(Body(t, t % 2, False))
    with eng.Fori(0, LOOPS) as i:
        body(Body(2 * i + FIRST_LOOPED, 0, True))
        body(Body(2 * i + FIRST_LOOPED + 1, 1, True))
    for t in range(FIRST_LOOPED + 2 * LOOPS, B + 1):
        body(Body(t, t % 2, False))


class BankJobs:

    def __init__(self, ready, order):
        self.ready, self.order = ready, order
        self.names = [name for name, *_ in order]

    def freed(self, body, name):
        t, i = body.t, self.names.index(name)
        while True:
            i -= 1
            if i < 0:
                t, i = t - 1, len(self.order) - 1
            if isinstance(t, int) and t < -2:
                return None
            _, ahead, steps, step = self.order[i]
            if body.inside or 0 <= t + ahead < B:
                return steps.sem, steps.at(t + ahead, step)

    def filled(self, body, name):
        t, i = body.t, self.names.index(name)
        first = FIRST_LOOPED if body.inside else t
        n = sum(0 <= s + ahead < B for s in range(-2, first) for _, ahead, *_ in self.order)
        if body.inside:
            return n + (t - FIRST_LOOPED) * len(self.order) + i + 1
        return n + sum(0 <= t + ahead < B for _, ahead, *_ in self.order[:i + 1])


def own_wait(eng):
    eng.nop(nofuse=True)


def xtile(X, b, k=0, n=TT):
    return X[:, bass.ds(TT * b + k, n), :]


def attention_layer(nc, m, L, tag, causal, scale, bias, rope, project, ffn, store, prefetch=None):
    ctx = ExitStack()
    with ctx:
        def sem(name):
            return ctx.enter_context(nc.semaphore(f"{tag}_{name}"))

        W = 384 if causal else 512
        ln_dve = Steps(sem("ln_dve"), "stats0 stats1 mean0 mean1 xn0 xn1")
        ln_pool = Steps(sem("ln_pool"), "var rstd")
        xnT_act = Steps(sem("xnT_act"), "xnT")
        proj_act = Steps(sem("proj_act"), "rows cols" if bias else "both")
        rope_dve = Steps(sem("rope_dve"), "rows cols")
        rope_pool = Steps(sem("rope_pool"), "rows cols")
        split_act = Steps(sem("split_act"), "high middle")
        split_dve = Steps(sem("split_dve"), "rest low")
        parts_out = Steps(sem("parts_out"), "high middle low", 16 * 2)
        split = 5 if rope else 4
        stacks_in = Steps(sem("stacks_in"), ["loaded"], 16 * sum(len(r) for r in PART_RUNS))
        v_act = Steps(sem("v_act"), "v")
        score_pe = Steps(sem("score_pe"), [f"h{h}" for h in range(HEADS)])
        max_dve = Steps(sem("max_dve"), [f"h{h}" for h in range(HEADS)])
        shift_act = Steps(sem("shift_act"), "half0 half1")
        shift_dve = Steps(sem("shift_dve"), "half0 half1")
        shift_in = [Steps(sem(f"shift_in{i}"), ["half"], 32) for i in range(2)]
        scoreT_pe = Steps(sem("scoreT_pe"), [f"h{h}" for h in range(HEADS)])
        exp_act = Steps(sem("exp_act"), [f"h{h}" for h in range(HEADS)])
        av_pe = Steps(sem("av_pe"), [f"g{g}" for g in range(GROUPS)])
        av_act = Steps(sem("av_act"), [f"g{g}" for g in range(GROUPS)])
        norm_dve = Steps(sem("norm_dve"), "recip0 mul0 recip1 mul1")
        oT_act = Steps(sem("oT_act"), "oT")
        fin_dve = Steps(sem("fin_dve"), "gated")
        fin_pool = Steps(sem("fin_pool"), "x" if project else "gated x")
        out_sp = Steps(sem("out_sp"), ["stored"], 16)
        jobs = [("v", 1, v_act, "v"), ("turn0", -1, norm_dve, "mul0"), ("shift1", 0, shift_dve, "half1"),
                ("turn1", -1, norm_dve, "mul1"), ("xnT", 2, xnT_act, "xnT")]
        jobs += [("proj", 2, rope_dve, "rows"), ("projc", 2, rope_dve, "cols")] if rope else \
            [("proj", 2, proj_act, proj_act.names[-1])]
        if project:
            jobs += [("turnO", -1, oT_act, "oT")]
        jobs += [("shift0", 1, shift_dve, "half0")]
        if project:
            jobs += [("out", -1, fin_dve, "gated")]
        M = BankJobs(sem("m_ready"), jobs)
        F = ffn.open(nc, sem, m, xnT_act)

        block = ctx.enter_context(nc.Block())

        @block.sync
        def _(sp):
            if prefetch is not None:
                prefetch(sp)

            def send_shifts(b, u, half):
                sp.wait_ge(shift_dve.sem, shift_dve.at(b, f"half{half}"))
                hs = HEADS // 2 * half
                for r in range(2):
                    sp.dma_start(m.stack[0][u][SHIFT_ROW + r:SHIFT_ROW + r + 1, hs:hs + HEADS // 2, :],
                                 m.shift[half][:, r, :]).then_inc(shift_in[half].sem, 16)

            def body(t):
                b = t.batch(1)
                if b is not None:
                    u = (t.parity + 1) % 2
                    sp.wait_ge(parts_out.sem, parts_out.at(b, "low"))
                    if exists(b - 2):
                        sp.wait_ge(scoreT_pe.sem, scoreT_pe.at(b - 2, f"h{HEADS - 1}"))
                    for o, runs in enumerate(PART_RUNS):
                        for slot, part, n, same in runs:
                            src = m.parts_dram[u, o, part:part + (1 if same else n)]
                            if same:
                                src = src.broadcast_to([n, HD, HEADS * N])
                            sp.dma_start(m.stack[o][u][HD * slot:HD * (slot + n), :, :], src)\
                              .then_inc(stacks_in.sem, 16)
                b = t.batch(0)
                if b is not None:
                    send_shifts(b, t.parity, 1)
                b = t.batch(2)
                if b is not None:
                    u = t.parity
                    for part, made, step in ((0, split_act, "high"), (1, split_act, "middle"), (2, split_dve, "low")):
                        sp.wait_ge(made.sem, made.at(b, step))
                        for o in range(2):
                            sp.dma_start(m.parts_dram[u, o, part].rearrange("d (h n) -> h d n", n=N),
                                         m.parts[:, part, o, :]).then_inc(parts_out.sem, 16)
                b = t.batch(1)
                if b is not None:
                    send_shifts(b, (t.parity + 1) % 2, 0)
                b = t.batch(-1)
                if store is not None and b is not None:
                    sp.wait_ge(fin_pool.sem, fin_pool.at(b, "x"))
                    sp.dma_start(store[:, bass.ds(TT * b, TT), :], xtile(m.X, b)).then_inc(out_sp.sem, 16)
            turns(sp, body)
            if store is not None:
                if exists(B - 1):
                    sp.wait_ge(out_sp.sem, out_sp.at(B - 1, "stored"))

        @block.tensor
        def _(pe):

            def score_mask(bank, tri):
                pe.matmul(bank[:, 0:384].rearrange("p (a c) -> p a c", a=3)[:, 0:3:2, :], m.ident_b[:, :],
                          m.tri2[:, tri, :, :],
                          start=True, stop=False, skip_group_check=True)

            def scores(t, b, u, h):
                if h == 0:
                    pe.wait_ge(stacks_in.sem, stacks_in.at(b, "loaded"))
                if h >= 2:
                    pe.wait_ge(max_dve.sem, max_dve.at(b, f"h{h - 2}"))
                else:
                    if exists(b - 1):
                        pe.wait_ge(max_dve.sem, max_dve.at(b - 1, f"h{HEADS - 2 + h}"))
                S, k = m.S[h % 2], SHIFT_ROW
                rows, cols = m.stack[0][u][0:k, h, :], m.stack[1][u][0:k, h, :]
                if causal:
                    score_mask(S, 0)
                    pe.matmul(S[:, 0:128], rows[:, 0:128], cols[:, 0:128], start=False, stop=False,
                              skip_group_check=True)
                    pe.matmul(S[:, 128:384], rows[:, 128:256], cols, start=False, stop=True,
                              skip_group_check=True).then_inc(score_pe.sem, 1)
                else:
                    pe.matmul(S[:, 0:256], rows[:, 0:128], cols, start=True, stop=True)
                    pe.matmul(S[:, 256:512], rows[:, 128:256], cols, start=True, stop=True)\
                      .then_inc(score_pe.sem, 1)

            def scoresT(t, b, u, h):
                if h % 8 == 0:
                    pe.wait_ge(shift_in[h // 8].sem, shift_in[h // 8].at(b, "half"))
                if h >= 2:
                    pe.wait_ge(exp_act.sem, exp_act.at(b, f"h{h - 2}"))
                else:
                    if exists(b - 1):
                        pe.wait_ge(exp_act.sem, exp_act.at(b - 1, f"h{HEADS - 2 + h}"))
                T = m.T[h % 2]
                rows, cols = m.stack[0][u][:, h, :], m.stack[1][u][:, h, :]
                if causal:
                    score_mask(T, 1)
                    pe.matmul(T[:, 0:256], cols[:, 0:128], rows, start=False, stop=False,
                              skip_group_check=True)
                    pe.matmul(T[:, 256:384], cols[:, 128:256], rows[:, 128:256], start=False, stop=True,
                              skip_group_check=True).then_inc(scoreT_pe.sem, 1)
                else:
                    pe.matmul(T[:, 0:256], cols[:, 0:128], rows, start=True, stop=True)
                    pe.matmul(T[:, 256:512], cols[:, 128:256], rows, start=True, stop=True)\
                      .then_inc(scoreT_pe.sem, 1)

            def values(t, b, u, g):
                pe.wait_ge(exp_act.sem, exp_act.at(b, f"h{4 * g + 3}"))
                if g == 0:
                    pe.wait_ge(v_act.sem, v_act.at(b, "v"))
                    if exists(b - 1):
                        pe.wait_ge(av_act.sem, av_act.at(b - 1, f"g{GROUPS - 1}"))
                else:
                    pe.wait_ge(av_act.sem, av_act.at(b, f"g{g - 1}"))
                c = N * (g % 2)
                for k in range(TT):
                    lo = P * k if causal else 0
                    for j in range(4):
                        h = 4 * g + j
                        p = m.prob[:, h % PRING, P * (2 * k):P * (2 * k) + N - lo]
                        mm = pe.matmul(m.O[32 * j:32 * j + 32, c + lo:c + N], m.vaug[u][:, k, h, :], p,
                                       start=(k == 0), stop=(k == TT - 1), skip_group_check=True)
                mm.then_inc(av_pe.sem, 1)

            def turn_back(t, b, u, k):
                if k == 0:
                    pe.wait_ge(av_act.sem, av_act.at(b, f"g{GROUPS - 1}"))
                free = M.freed(t, f"turn{k}")
                if free:
                    pe.wait_ge(*free)
                for g in range(GROUPS):
                    mm = pe.transpose(m.M[:, P * g:P * g + P], m.oTn[u][:, g, P * k:P * k + P], m.ident[:, :])
                mm.then_inc(M.ready, 1)

            def body(t):
                p = t.parity
                q = (p + 1) % 2
                prev, cur, nxt, new = (t.batch(a) for a in (-1, 0, 1, 2))
                for s in range(SLICES):
                    if cur is not None:
                        scoresT(t, cur, p, 2 * s)
                        scoresT(t, cur, p, 2 * s + 1)
                    for b, half in ((cur, 1), (nxt, 0)):
                        if b is None or s != SHIFT_SLICE[half]:
                            continue
                        hs = HEADS // 2 * half
                        pe.wait_ge(max_dve.sem, max_dve.at(b, f"h{hs + HEADS // 2 - 1}"))
                        free = M.freed(t, f"shift{half}")
                        if free:
                            pe.wait_ge(*free)
                        for k in range(TT):
                            mm = pe.transpose(m.M[0:8, P * k:P * k + P], m.rowmax[:, k, hs:hs + 8], m.ident[:, :])
                        mm.then_inc(M.ready, 1)
                    if nxt is not None:
                        F.tensor(pe, nxt, q, s)
                    for b, u, pair in ((cur, p, s + 6), (nxt, q, s - 2)):
                        if b is not None and 0 <= pair < HEADS // 2:
                            scores(t, b, u, 2 * pair)
                            scores(t, b, u, 2 * pair + 1)
                    if s == 0 and prev is not None:
                        values(t, prev, q, 3)
                    if s in (2, 4, 6) and cur is not None:
                        values(t, cur, p, s // 2 - 1)
                    if s == 0 and nxt is not None:
                        free = M.freed(t, "v")
                        if free:
                            pe.wait_ge(*free)
                        pe.wait_ge(xnT_act.sem, xnT_act.at(nxt, "xnT"))
                        for k in range(TT):
                            mm = pe.matmul(m.M[:, P * k:P * k + P], m.xnT[q][:, P * k:P * k + P], L.w["V"],
                                           start=True, stop=True)
                        mm.then_inc(M.ready, 1)
                    if s == 1 and prev is not None:
                        turn_back(t, prev, q, 0)
                    if s == 2 and prev is not None:
                        turn_back(t, prev, q, 1)
                    if s == 3 and new is not None:
                        pe.wait_ge(ln_dve.sem, ln_dve.at(new, "xn1"))
                        free = M.freed(t, "xnT")
                        if free:
                            pe.wait_ge(*free)
                        for k in range(TT):
                            mm = pe.transpose(m.M[:, P * k:P * k + P], m.xn[:, k, :], m.ident[:, :])
                        mm.then_inc(M.ready, 1)
                    if s == 4 and new is not None:
                        pe.wait_ge(xnT_act.sem, xnT_act.at(new, "xnT"))
                        if rope:
                            free = M.freed(t, "proj")
                            if free:
                                pe.wait_ge(*free)
                            pe.matmul(m.M[:, 0:N], L.w["A"], m.xnT[p][:, :], start=True, stop=True)
                            pe.matmul(m.M[:, N:2 * N], L.w["Ar"], m.xnT[p][:, :], start=True, stop=True)\
                              .then_inc(M.ready, 1)
                            free = M.freed(t, "projc")
                            if free:
                                pe.wait_ge(*free)
                            pe.matmul(m.M[:, 0:N], L.w["B"], m.xnT[p][:, :], start=True, stop=True)
                            pe.matmul(m.M[:, N:2 * N], L.w["Br"], m.xnT[p][:, :], start=True, stop=True)\
                              .then_inc(M.ready, 1)
                        else:
                            free = M.freed(t, "proj")
                            if free:
                                pe.wait_ge(*free)
                            pe.matmul(m.M[:, 0:N], L.w["A"], m.xnT[p][:, :], start=True, stop=True)
                            pe.matmul(m.M[:, N:2 * N], L.w["B"], m.xnT[p][:, :], start=True, stop=True)\
                              .then_inc(M.ready, 1)
                    if s == 5 and prev is not None and project:
                        pe.wait_ge(norm_dve.sem, norm_dve.at(prev, "mul1"))
                        free = M.freed(t, "turnO")
                        if free:
                            pe.wait_ge(*free)
                        for k in range(TT):
                            mm = pe.transpose(m.M[:, P * k:P * k + P], m.o[:, k, :], m.ident[:, :])
                        mm.then_inc(M.ready, 1)
                    if s == 7 and prev is not None and project:
                        pe.wait_ge(oT_act.sem, oT_act.at(prev, "oT"))
                        free = M.freed(t, "out")
                        if free:
                            pe.wait_ge(*free)
                        for k in range(TT):
                            mm = pe.matmul(m.M[:, P * k:P * k + P], m.oT[:, P * k:P * k + P], L.w["O"],
                                           start=True, stop=not bias)
                            if bias:
                                mm = pe.matmul(m.M[:, P * k:P * k + P], m.ones[0:1, 0:P], L.w["bo"],
                                               start=False, stop=True)
                        mm.then_inc(M.ready, 1)
            turns(pe, body)

        @block.scalar
        def _(act):

            def body(t):
                p = t.parity
                q = (p + 1) % 2
                prev, cur, nxt, new = (t.batch(a) for a in (-1, 0, 1, 2))

                def copy_values(b, u, g):
                    act.wait_ge(av_pe.sem, av_pe.at(b, f"g{g}"))
                    if g == 0:
                        if exists(b - 2):
                            act.wait_ge(norm_dve.sem, norm_dve.at(b - 2, "mul1"))
                    c = N * (g % 2)
                    act.activation(m.oTn[u][:, g, :], m.O[:, c:c + N], ACT.Copy).then_inc(av_act.sem, 1)

                for s in range(SLICES):
                    if cur is not None:
                        for h in (2 * s, 2 * s + 1):
                            act.wait_ge(scoreT_pe.sem, scoreT_pe.at(cur, f"h{h}"))
                            if h >= PRING:
                                act.wait_ge(av_pe.sem, av_pe.at(cur, f"g{(h - PRING) // 4}"))
                            else:
                                if exists(cur - 1):
                                    act.wait_ge(av_pe.sem, av_pe.at(cur - 1, f"g{(h + PRING) // 4}"))
                            act.activation(m.prob[:, h % PRING, 0:W], m.T[h % 2][:, 0:W], ACT.Exp, scale=scale)\
                               .then_inc(exp_act.sem, 1)
                    for b, half in ((cur, 1), (nxt, 0)):
                        if b is None or s != SHIFT_SLICE[half]:
                            continue
                        act.wait_ge(M.ready, M.filled(t, f"shift{half}"))
                        if exists(b - 1):
                            act.wait_ge(shift_in[half].sem, shift_in[half].at(b - 1, "half"))
                        act.activation(m.shift[half][:, 0, :], m.M[0:8, 0:N], ACT.Copy, scale=-1.0)\
                           .then_inc(shift_act.sem, 1)
                    if s == 0 and prev is not None:
                        copy_values(prev, q, 3)
                    if s in (2, 4, 6) and cur is not None:
                        copy_values(cur, p, s // 2 - 1)
                    if nxt is not None:
                        F.scalar(act, nxt, q, s)
                    if s == 0 and nxt is not None:
                        act.wait_ge(M.ready, M.filled(t, "v"))
                        if exists(nxt - 2):
                            act.wait_ge(av_pe.sem, av_pe.at(nxt - 2, f"g{GROUPS - 1}"))
                        for k in range(TT):
                            a = act.activation(m.vaug[q][:, k, :, 0:HD],
                                               m.M[:, P * k:P * k + P].rearrange("p (h d) -> p h d", d=HD), ACT.Copy)
                        a.then_inc(v_act.sem, 1)
                    if s == 3 and new is not None:
                        act.wait_ge(M.ready, M.filled(t, "xnT"))
                        act.activation(m.xnT[p][:, :], m.M[:, 0:N], ACT.Copy).then_inc(xnT_act.sem, 1)
                    if s == 4 and new is not None and not rope:
                        act.wait_ge(M.ready, M.filled(t, "proj"))
                        if exists(new - 1):
                            act.wait_ge(split_dve.sem, split_dve.at(new - 1, "rest"))
                        if bias:
                            act.activation(m.rc[:, 0:N], m.M[:, 0:N], ACT.Identity, bias=L.w["bA"])\
                               .then_inc(proj_act.sem, 1)
                            act.activation(m.rc[:, N:2 * N], m.M[:, N:2 * N], ACT.Identity, bias=L.w["bB"])\
                               .then_inc(proj_act.sem, 1)
                        else:
                            act.activation(m.rc[:, :], m.M[:, :], ACT.Copy).then_inc(proj_act.sem, 1)
                    if s == 5 and prev is not None and project:
                        act.wait_ge(M.ready, M.filled(t, "turnO"))
                        act.activation(m.oT[:, :], m.M[:, 0:N], ACT.Copy).then_inc(oT_act.sem, 1)
                    if s == split and new is not None:
                        ready = rope_pool if rope else proj_act
                        act.wait_ge(ready.sem, ready.at(new, ready.names[-1]))
                        if exists(new - 1):
                            act.wait_ge(parts_out.sem, parts_out.at(new - 1, "high"))
                        act.activation(m.parts[:, 0, :, :], m.rc[:, :].rearrange("p (o n) -> p o n", o=2), ACT.Copy)\
                           .then_inc(split_act.sem, 1)
                    if s == split + 1 and new is not None:
                        act.wait_ge(split_dve.sem, split_dve.at(new, "rest"))
                        if exists(new - 1):
                            act.wait_ge(parts_out.sem, parts_out.at(new - 1, "middle"))
                        act.activation(m.parts[:, 1, :, :], m.rest[:, :, :], ACT.Copy).then_inc(split_act.sem, 1)
            turns(act, body)

        @block.vector
        def _(dve):

            def body(t):
                p = t.parity
                q = (p + 1) % 2
                prev, cur, nxt, new = (t.batch(a) for a in (-1, 0, 1, 2))
                for s in range(SLICES):
                    if s == split + 1 and new is not None:
                        dve.wait_ge(split_act.sem, split_act.at(new, "high"))
                        if exists(new - 1):
                            dve.wait_ge(split_dve.sem, split_dve.at(new - 1, "low"))
                        dve.tensor_tensor(m.rest[:, :, :], m.rc[:, :].rearrange("p (o n) -> p o n", o=2),
                                          m.parts[:, 0, :, :], ALU.subtract).then_inc(split_dve.sem, 1)
                    if s == split + 2 and new is not None:
                        dve.wait_ge(split_act.sem, split_act.at(new, "middle"))
                        if exists(new - 1):
                            dve.wait_ge(parts_out.sem, parts_out.at(new - 1, "low"))
                        dve.tensor_tensor(m.parts[:, 2, :, :], m.rest[:, :, :], m.parts[:, 1, :, :], ALU.subtract)\
                           .then_inc(split_dve.sem, 1)
                    if s == 0 and new is not None:
                        if exists(new - 1):
                            dve.wait_ge(ln_pool.sem, ln_pool.at(new - 1, "rstd"))
                        for k in range(TT):
                            dve.bn_stats(m.stats[:, k, :], xtile(m.X, new, k, 1)).then_inc(ln_dve.sem, 1)
                        for k in range(TT):
                            dve.wait_ge(ln_dve.sem, ln_dve.at(new, f"stats{k}"))
                            own_wait(dve)
                            dve.bn_aggr(m.mean_var[:, k, :], m.stats[:, k, :]).then_inc(ln_dve.sem, 1)
                    if s == 1 and new is not None:
                        dve.wait_ge(ln_pool.sem, ln_pool.at(new, "rstd"))
                        if exists(new - 1):
                            dve.wait_ge(xnT_act.sem, xnT_act.at(new - 1, "xnT"))
                        for k in range(TT):
                            dve.tensor_scalar(m.xn[:, k, :], xtile(m.X, new, k, 1), m.mean_var[:, k, 0:1],
                                              m.rstd[:, k:k + 1], ALU.subtract, ALU.mult).then_inc(ln_dve.sem, 1)
                    for b, half in ((cur, 1), (nxt, 0)):
                        if b is None or s != SHIFT_SLICE[half]:
                            continue
                        dve.wait_ge(shift_act.sem, shift_act.at(b, f"half{half}"))
                        dve.scalar_tensor_tensor(m.shift[half][:, 1, :], m.M[0:8, 0:N], -1.0, m.shift[half][:, 0, :],
                                                 ALU.mult, ALU.subtract).then_inc(shift_dve.sem, 1)
                    for b, pair in ((cur, s + 6), (nxt, s - 2)):
                        if b is None or not 0 <= pair < HEADS // 2:
                            continue
                        for h in (2 * pair, 2 * pair + 1):
                            dve.wait_ge(score_pe.sem, score_pe.at(b, f"h{h}"))
                            if h % 8 == 0:
                                if exists(b - 1):
                                    dve.wait_ge(shift_dve.sem, shift_dve.at(b - 1, f"half{h // 8}"))
                            S = m.S[h % 2]
                            if causal:
                                dve.tensor_reduce(m.rowmax[:, 0, h:h + 1], S[:, 0:128], AX.X, ALU.max)
                                r = dve.tensor_reduce(m.rowmax[:, 1, h:h + 1], S[:, 128:384], AX.X, ALU.max)
                            else:
                                r = dve.tensor_reduce(m.rowmax[:, :, h:h + 1],
                                                      S[:, :].rearrange("p (k c) -> p k c", k=TT), AX.X, ALU.max)
                            r.then_inc(max_dve.sem, 1)
                    if nxt is not None:
                        F.vector(dve, nxt, q, s)
                    if s in (1, 2) and prev is not None:
                        k = s - 1
                        dve.wait_ge(M.ready, M.filled(t, f"turn{k}"))
                        if k == 0:
                            if exists(prev - 1) and project:
                                dve.wait_ge(oT_act.sem, oT_act.at(prev - 1, "oT"))
                            elif exists(prev - 1):
                                dve.wait_ge(fin_pool.sem, fin_pool.at(prev - 1, "gated"))
                        heads = m.M[:, :].rearrange("p (h w) -> p h w", w=32)
                        dve.reciprocal(m.rsum[:, k, :].unsqueeze(2), heads[:, :, HD:HD + 1]).then_inc(norm_dve.sem, 1)
                        dve.wait_ge(norm_dve.sem, norm_dve.at(prev, f"recip{k}"))
                        dve.tensor_tensor(m.o[:, k, :].rearrange("p (h d) -> p h d", d=HD), heads[:, :, 0:HD],
                                          m.rsum[:, k, :].unsqueeze(2).broadcast_to([P, HEADS, HD]), ALU.mult)\
                           .then_inc(norm_dve.sem, 1)
                    if s == 4 and new is not None and rope:
                        for i, job in enumerate(("proj", "projc")):
                            dve.wait_ge(M.ready, M.filled(t, job))
                            if exists(new - 1):
                                dve.wait_ge(rope_pool.sem, rope_pool.at(new - 1, rope_pool.names[i]))
                            dve.tensor_tensor(m.turned[:, i, :], m.M[:, :], m.cossin[:, :], ALU.mult)\
                               .then_inc(rope_dve.sem, 1)
                    if s == 7 and prev is not None and project:
                        dve.wait_ge(M.ready, M.filled(t, "out"))
                        if exists(prev - 1):
                            dve.wait_ge(fin_pool.sem, fin_pool.at(prev - 1, "x"))
                        F.gate_ready(dve, prev)
                        dve.scalar_tensor_tensor(m.gated[:, :, :], m.M[:, 0:N].rearrange("p (k c) -> p k c", k=TT),
                                                 0.5, F.gate(prev, q), ALU.mult, ALU.mult)\
                           .then_inc(fin_dve.sem, 1)
            turns(dve, body)

        @block.gpsimd
        def _(pool):

            def body(t):
                prev, cur, nxt, new = (t.batch(a) for a in (-1, 0, 1, 2))
                if new is not None:
                    pool.wait_ge(ln_dve.sem, ln_dve.at(new, "mean1"))
                    own_wait(pool)
                    pool.tensor_scalar(m.var_eps[:, :], m.mean_var[:, :, 1], 1e-5, None, ALU.add)\
                        .then_inc(ln_pool.sem, 1)
                    pool.wait_ge(ln_pool.sem, ln_pool.at(new, "var"))
                    pool.tensor_tensor(m.rstd[:, :], m.var_eps[:, :], m.minus_half[:, 0:TT], ALU.pow)\
                        .then_inc(ln_pool.sem, 1)
                F.gpsimd(pool, nxt, (t.parity + 1) % 2)
                if new is not None and rope:
                    for i in range(2):
                        pool.wait_ge(rope_dve.sem, rope_dve.at(new, rope_dve.names[i]))
                        if i == 0 and exists(new - 1):
                            pool.wait_ge(split_dve.sem, split_dve.at(new - 1, "rest"))
                        pool.tensor_tensor(m.rc[:, N * i:N * i + N], m.turned[:, i, 0:N], m.turned[:, i, N:2 * N],
                                           ALU.add).then_inc(rope_pool.sem, 1)
                if prev is not None:
                    X = xtile(m.X, prev)
                    if project:
                        pool.wait_ge(fin_dve.sem, fin_dve.at(prev, "gated"))
                    else:
                        pool.wait_ge(norm_dve.sem, norm_dve.at(prev, "mul1"))
                        F.gate_ready(pool, prev)
                        if exists(prev - 1):
                            pool.wait_ge(fin_pool.sem, fin_pool.at(prev - 1, "x"))
                        pool.tensor_tensor(m.gated[:, :, :], m.o[:, :, :], F.gate(prev, (t.parity + 1) % 2), ALU.mult)\
                            .then_inc(fin_pool.sem, 1)
                        pool.wait_ge(fin_pool.sem, fin_pool.at(prev, "gated"))
                    pool.tensor_tensor(X, X, m.gated[:, :, :], ALU.add).then_inc(fin_pool.sem, 1)
            turns(pool, body)


def moe_layer(nc, m, w, tag):
    ctx = ExitStack()
    with ctx:
        def sem(name):
            return ctx.enter_context(nc.semaphore(f"{tag}_{name}"))

        E, K = w.experts, 8
        first = E - K
        capped = w.capacity is not None
        ln_dve = Steps(sem("ln_dve"), "stats0 stats1 mean0 mean1 xn0 xn1" + (" xr0 xr1" if w.rms else ""))
        ln_pool = Steps(sem("ln_pool"), "var rstd" + (" sq mean2 meps r2" if w.rms else ""))
        xT_act = Steps(sem("xT_act"), "xnT xrT" if w.rms else "xnT")
        route_act = Steps(sem("route_act"), "act gT")
        route_dve = Steps(sem("route_dve"), (["v"] if w.sigmoid else ["logit", "max", "shift"]) +
                          "vsum vrec max1 eq1 key1 top1 one1 less max2 eq2 key2 top2 one2".split() +
                          (["keep", "chosen"] if capped else []) + ["onehots", "gates", "weight"] +
                          (["counts"] if capped else []))
        in_pe = Steps(sem("in_pe"), [f"e{e}c{c}" for e in range(E) for c in range(2)])
        hid = [Steps(sem(f"hid_{n}"), [f"e{e}c{c}" for e in range(E) for c in ((0, 1) if not w.relu else (i,))])
               for i, n in enumerate(("act", "dve"))]
        outs = ["base"] + [f"e{e}" for e in range(first, E)]
        out_pe = Steps(sem("out_pe"), outs)
        acc_dve = Steps(sem("acc_dve"), ["base"] + [f"e{e}" for e in range(first, E)] + ["gate"])
        tanh_act = Steps(sem("tanh_act"), "tanh")
        jobs = [("xnT", 1, xT_act, "xnT")] + ([("xrT", 1, xT_act, "xrT")] if w.rms else [])
        jobs += [("logit", 1, *((route_act, "act") if w.sigmoid else (route_dve, "logit")))]
        jobs += [("count", 1, route_dve, "keep")] if capped else []
        jobs += [("gT", 1, route_act, "gT")]
        M = BankJobs(sem("m_ready"), jobs)
        IN = [m.S[0], m.S[1], m.T[0], m.T[1]]
        HR = 4

        def hidden_done(eng, b, e, c):
            done = hid[c] if w.relu else hid[0]
            if exists(b):
                eng.wait_ge(done.sem, done.at(b, f"e{e}c{c}"))

        def hid_free(eng, b, e):
            x = e - HR
            bb, x = (b, x) if x >= 0 else (b - 1, max(y for y in range(E) if y % HR == e % HR))
            if exists(bb):
                eng.wait_ge(out_pe.sem, out_pe.at(bb, "base" if x < first else f"e{x}"))

        block = ctx.enter_context(nc.Block())

        @block.tensor
        def _(pe):
            def experts_in(b, u, e):
                if e == 0:
                    pe.wait_ge(xT_act.sem, xT_act.at(b, xT_act.names[-1]))
                for c in range(2):
                    hidden_done(pe, b if e >= 2 else b - 1, (e - 2) % E, c)
                    bank = IN[(2 * e + c) % 4]
                    for i in range(2):
                        mm = pe.matmul(bank[:, N * i:N * i + N], w.W1[:, e, P * (2 * c + i):P * (2 * c + i) + P],
                                       w.xT[u], start=True, stop=True)
                    mm.then_inc(in_pe.sem, 1)

            def products_out(bank, e, start, stop):
                for k in range(TT):
                    for c in range(4):
                        mm = pe.matmul(bank[:, P * k:P * k + P], w.hT[e % HR][:, c, P * k:P * k + P],
                                       w.W2[:, e, c, :], start=(start and c == 0), stop=(stop and c == 3),
                                       skip_group_check=True)
                return mm

            def experts_out(b, u, i):
                prev = i - 2
                if exists(b if prev >= 0 else b - 1):
                    pe.wait_ge(acc_dve.sem, acc_dve.at(b if prev >= 0 else b - 1, (["base"] + [f"e{e}" for e in range(first, E)])[prev]))
                bank = m.F[(i + u) % 2]
                if i == 0:
                    pe.wait_ge(route_act.sem, route_act.at(b, "gT"))
                    for k in range(TT):
                        mm = pe.matmul(bank[:, P * k:P * k + P], w.gT[u][:, P * k:P * k + P], w.b2[:, :],
                                       start=True, stop=not first, skip_group_check=True)
                        if first:
                            for e in range(first):
                                mm = pe.matmul(bank[:, P * k:P * k + P], m.ones[0:1, 0:P], w.b2s[:, e, :],
                                               start=False, stop=False, skip_group_check=True)
                            if k == 0:
                                hidden_done(pe, b, first - 1, 1)
                            for e in range(first):
                                for c in range(4):
                                    mm = pe.matmul(bank[:, P * k:P * k + P], w.hT[e % HR][:, c, P * k:P * k + P],
                                                   w.W2[:, e, c, :], start=False, stop=(e == first - 1 and c == 3),
                                                   skip_group_check=True)
                else:
                    e = first + i - 1
                    if w.relu:
                        hidden_done(pe, b, e, 0)
                    hidden_done(pe, b, e, 1)
                    mm = products_out(bank, e, True, True)
                mm.then_inc(out_pe.sem, 1)

            def misc(t, b, u, i):
                if i == 0:
                    pe.wait_ge(ln_dve.sem, ln_dve.at(b, "xn1"))
                    free = M.freed(t, "xnT")
                    if free:
                        pe.wait_ge(*free)
                    for k in range(TT):
                        mm = pe.transpose(m.M[:, P * k:P * k + P], m.xn[:, k, :], m.ident[:, :])
                    mm.then_inc(M.ready, 1)
                if i == 1 and w.rms:
                    pe.wait_ge(ln_dve.sem, ln_dve.at(b, "xr1"))
                    free = M.freed(t, "xrT")
                    if free:
                        pe.wait_ge(*free)
                    for k in range(TT):
                        mm = pe.transpose(m.M[:, P * k:P * k + P], w.xr[:, k, :], m.ident[:, :])
                    mm.then_inc(M.ready, 1)
                if i == 2:
                    free = M.freed(t, "logit")
                    if free:
                        pe.wait_ge(*free)
                    for k in range(TT):
                        mm = pe.matmul(m.M[:, K * k:K * k + K], m.xnT[u][:, P * k:P * k + P], w.router[:, :],
                                       start=True, stop=True)
                    mm.then_inc(M.ready, 1)
                if i == 3 and capped:
                    pe.wait_ge(route_dve.sem, route_dve.at(b, "one2"))
                    free = M.freed(t, "count")
                    if free:
                        pe.wait_ge(*free)
                    for k in range(TT):
                        pe.matmul(m.M[:, 16 * k:16 * k + 16], m.upto[:, :], w.one[:, k, :], start=True, stop=False)
                        if k:
                            pe.matmul(m.M[:, 16 * k:16 * k + 16], m.ones[:, :], w.one[:, 0, :], start=False, stop=False)
                        mm = pe.matmul(m.M[:, 16 * k:16 * k + 16], m.ones[:, :], w.counts[:, :], start=False, stop=True)
                    mm.then_inc(M.ready, 1)
                if i == 4:
                    pe.wait_ge(route_dve.sem, route_dve.at(b, "weight"))
                    free = M.freed(t, "gT")
                    if free:
                        pe.wait_ge(*free)
                    for k in range(TT):
                        mm = pe.transpose(m.M[0:K, P * k:P * k + P], w.weight[u][:, k, :], m.ident[:, :])
                    mm.then_inc(M.ready, 1)

            def body(t):
                cur, nxt = t.batch(0), t.batch(1)
                u = t.parity
                for e in range(E + 2):
                    if cur is not None:
                        if e < E:
                            experts_in(cur, u, e)
                        i = e - first - 1 if first else e - 1
                        if 0 <= i <= K:
                            experts_out(cur, u, i)
                    if nxt is not None and e in (1, 2, 3, 5, 7):
                        misc(t, nxt, 1 - u, (1, 2, 3, 5, 7).index(e))
            turns(pe, body)

        @block.scalar
        def _(act):
            def body(t):
                cur, nxt = t.batch(0), t.batch(1)
                u = t.parity
                for e in range(E + 2):
                    if cur is not None and e < E:
                        for c in range(2):
                            if w.relu and c:
                                continue
                            act.wait_ge(in_pe.sem, in_pe.at(cur, f"e{e}c{c}"))
                            if c == 0:
                                hid_free(act, cur, e)
                            for i in range(2):
                                a = act.activation(w.hT[e % HR][:, 2 * c + i, :], IN[(2 * e + c) % 4][:, N * i:N * i + N],
                                                   ACT.Relu if w.relu else ACT.Gelu, bias=w.b1[:, e, 2 * c + i:2 * c + i + 1])
                            a.then_inc(hid[0].sem, 1)
                    if nxt is not None:
                        if e == 2:
                            act.wait_ge(M.ready, M.filled(t, "xnT"))
                            act.activation(m.xnT[1 - u][:, :], m.M[:, 0:N], ACT.Copy).then_inc(xT_act.sem, 1)
                        if e == 3 and w.rms:
                            act.wait_ge(M.ready, M.filled(t, "xrT"))
                            act.activation(w.xT[1 - u], m.M[:, 0:N], ACT.Copy).then_inc(xT_act.sem, 1)
                        if e == 4:
                            if w.sigmoid:
                                act.wait_ge(M.ready, M.filled(t, "logit"))
                                if exists(nxt - 1):
                                    act.wait_ge(route_dve.sem, route_dve.at(nxt - 1, "weight"))
                                act.activation(w.v0[:, :, :], m.M[:, 0:2 * K].rearrange("p (k e) -> p k e", k=TT),
                                               ACT.Tanh, scale=0.5).then_inc(route_act.sem, 1)
                            else:
                                act.wait_ge(route_dve.sem, route_dve.at(nxt, "shift"))
                                act.activation(w.v[:, :, :], w.v0[:, :, :], ACT.Exp).then_inc(route_act.sem, 1)
                        if e == 8:
                            act.wait_ge(M.ready, M.filled(t, "gT"))
                            act.activation(w.gT[1 - u][:, :], m.M[0:K, 0:N], ACT.Copy).then_inc(route_act.sem, 1)
                if cur is not None:
                    act.wait_ge(acc_dve.sem, acc_dve.at(cur, f"e{E - 1}"))
                    act.activation(w.th, w.acc, ACT.Tanh, scale=0.5).then_inc(tanh_act.sem, 1)

            turns(act, body)

        @block.vector
        def _(dve):
            def top(b, n):
                v = w.v if n == 1 else w.v2
                dve.tensor_reduce(w.mx[:, :, :], v[:, :, :], AX.X, ALU.max).then_inc(route_dve.sem, 1)
                dve.wait_ge(route_dve.sem, route_dve.at(b, f"max{n}"))
                dve.tensor_tensor(w.eq[:, :, :], v[:, :, :], w.mx[:, :, :].broadcast_to([P, TT, K]), ALU.is_ge)\
                   .then_inc(route_dve.sem, 1)
                dve.wait_ge(route_dve.sem, route_dve.at(b, f"eq{n}"))
                dve.tensor_tensor(w.eq[:, :, :], w.eq[:, :, :], m.rank[:, :, :], ALU.mult).then_inc(route_dve.sem, 1)
                dve.wait_ge(route_dve.sem, route_dve.at(b, f"key{n}"))
                dve.tensor_reduce(w.mx[:, :, :], w.eq[:, :, :], AX.X, ALU.max).then_inc(route_dve.sem, 1)
                dve.wait_ge(route_dve.sem, route_dve.at(b, f"top{n}"))
                dve.tensor_tensor(w.one[:, :, K * (n - 1):K * n], w.eq[:, :, :],
                                  w.mx[:, :, :].broadcast_to([P, TT, K]), ALU.is_equal).then_inc(route_dve.sem, 1)
                dve.wait_ge(route_dve.sem, route_dve.at(b, f"one{n}"))

            def body(t):
                cur, nxt = t.batch(0), t.batch(1)
                u = t.parity
                for e in range(E + 2):
                    if w.relu and cur is not None and e < E:
                        dve.wait_ge(in_pe.sem, in_pe.at(cur, f"e{e}c1"))
                        hid_free(dve, cur, e)
                        for i in range(2):
                            a = dve.tensor_scalar(w.hT[e % HR][:, 2 + i, :], IN[(2 * e + 1) % 4][:, N * i:N * i + N],
                                                  w.b1[:, e, 2 + i:3 + i], 0.0, ALU.add, ALU.max)
                        a.then_inc(hid[1].sem, 1)
                    i = e - first - 2 if first else e - 2
                    if cur is not None and 0 <= i <= K:
                        accumulate(cur, u, i)
                    if nxt is not None:
                        misc(t, nxt, 1 - u, e)
                if cur is not None:
                    accumulate(cur, u, K)
                    dve.wait_ge(tanh_act.sem, tanh_act.at(cur, "tanh"))
                    dve.scalar_tensor_tensor(xtile(m.gate, cur), w.th, 1.0, w.acc, ALU.add, ALU.mult)\
                       .then_inc(acc_dve.sem, 1)

            def accumulate(b, u, i):
                name = "base" if i == 0 else f"e{first + i - 1}"
                dve.wait_ge(out_pe.sem, out_pe.at(b, name))
                F = m.F[(i + u) % 2][:, 0:N].rearrange("p (k c) -> p k c", k=TT)
                if i == 0:
                    if exists(b - 1):
                        dve.wait_ge(acc_dve.sem, acc_dve.at(b - 1, "gate"))
                    if w.plus_x:
                        a = dve.tensor_tensor(w.acc, F, w.xk[u], ALU.add)
                    else:
                        a = dve.tensor_copy(w.acc, F)
                else:
                    dve.wait_ge(acc_dve.sem, acc_dve.at(b, "base" if i == 1 else f"e{first + i - 2}"))
                    for k in range(TT):
                        a = dve.scalar_tensor_tensor(w.acc[:, k, :], F[:, k, :], w.weight[u][:, k, i - 1:i],
                                                     w.acc[:, k, :], ALU.mult, ALU.add)
                a.then_inc(acc_dve.sem, 1)

            def misc(t, b, u, e):
                if e == 0:
                    if exists(b - 1):
                        dve.wait_ge(ln_pool.sem, ln_pool.at(b - 1, "rstd"))
                    for k in range(TT):
                        dve.bn_stats(m.stats[:, k, :], xtile(m.X, b, k, 1)).then_inc(ln_dve.sem, 1)
                    for k in range(TT):
                        dve.wait_ge(ln_dve.sem, ln_dve.at(b, f"stats{k}"))
                        own_wait(dve)
                        dve.bn_aggr(m.mean_var[:, k, :], m.stats[:, k, :]).then_inc(ln_dve.sem, 1)
                if e == 1:
                    dve.wait_ge(ln_pool.sem, ln_pool.at(b, "rstd"))
                    if exists(b - 1):
                        dve.wait_ge(xT_act.sem, xT_act.at(b - 1, "xnT"))
                    for k in range(TT):
                        dve.tensor_scalar(m.xn[:, k, :], xtile(m.X, b, k, 1), m.mean_var[:, k, 0:1],
                                          m.rstd[:, k:k + 1], ALU.subtract, ALU.mult).then_inc(ln_dve.sem, 1)
                if e == 2 and w.rms:
                    dve.wait_ge(ln_pool.sem, ln_pool.at(b, "r2"))
                    dve.wait_ge(ln_dve.sem, ln_dve.at(b, "xn1"))
                    if exists(b - 2):
                        dve.wait_ge(acc_dve.sem, acc_dve.at(b - 2, "base"))
                    if exists(b - 1):
                        dve.wait_ge(xT_act.sem, xT_act.at(b - 1, "xrT"))
                    for k in range(TT):
                        dve.tensor_copy(w.xk[u][:, k, :], m.xn[:, k, :])
                        dve.tensor_scalar(w.xr[:, k, :], m.xn[:, k, :], w.r2[:, k:k + 1], None, ALU.mult)\
                           .then_inc(ln_dve.sem, 1)
                if e == 4:
                    R = route_dve
                    logit = m.M[:, 0:2 * K].rearrange("p (k e) -> p k e", k=TT)
                    if exists(b - 1):
                        dve.wait_ge(R.sem, R.at(b - 1, R.names[-1]))
                    if w.sigmoid:
                        dve.wait_ge(route_act.sem, route_act.at(b, "act"))
                        dve.tensor_scalar(w.v[:, :, :], w.v0[:, :, :], 0.5, 0.5, ALU.mult, ALU.add).then_inc(R.sem, 1)
                        dve.wait_ge(R.sem, R.at(b, "v"))
                    else:
                        dve.wait_ge(M.ready, M.filled(t, "logit"))
                        dve.tensor_tensor(w.v0[:, :, :], logit, w.router_b[:, :, :], ALU.add).then_inc(R.sem, 1)
                        dve.wait_ge(R.sem, R.at(b, "logit"))
                        dve.tensor_reduce(w.mx[:, :, :], w.v0[:, :, :], AX.X, ALU.max).then_inc(R.sem, 1)
                        dve.wait_ge(R.sem, R.at(b, "max"))
                        if exists(b - 1):
                            dve.wait_ge(route_act.sem, route_act.at(b - 1, "act"))
                        dve.tensor_tensor(w.v0[:, :, :], w.v0[:, :, :], w.mx[:, :, :].broadcast_to([P, TT, K]),
                                          ALU.subtract).then_inc(R.sem, 1)
                        dve.wait_ge(route_act.sem, route_act.at(b, "act"))
                    dve.tensor_reduce(w.vsum[:, :, :], w.v[:, :, :], AX.X, ALU.add).then_inc(R.sem, 1)
                    dve.wait_ge(R.sem, R.at(b, "vsum"))
                    dve.reciprocal(w.vrec[:, :, :], w.vsum[:, :, :]).then_inc(R.sem, 1)
                    top(b, 1)
                    dve.scalar_tensor_tensor(w.v2[:, :, :], w.one[:, :, 0:K], -1e30, w.v[:, :, :], ALU.mult, ALU.add)\
                       .then_inc(R.sem, 1)
                    dve.wait_ge(R.sem, R.at(b, "less"))
                    top(b, 2)
                if e == 6:
                    R = route_dve
                    if capped:
                        dve.wait_ge(M.ready, M.filled(t, "count"))
                        dve.scalar_tensor_tensor(w.kept[:, :, :], m.M[:, 0:32].rearrange("p (k e) -> p k e", k=TT),
                                                 float(w.capacity) + 0.5, w.one[:, :, :], ALU.is_le, ALU.mult)\
                           .then_inc(R.sem, 1)
                        dve.wait_ge(R.sem, R.at(b, "keep"))
                        dve.tensor_tensor(w.cnt2[:, :], w.one[:, 0, :], w.one[:, 1, :], ALU.add).then_inc(R.sem, 1)
                    kept = w.kept if capped else w.one
                    dve.tensor_tensor(w.ohs[:, :, :], kept[:, :, 0:K], kept[:, :, K:2 * K], ALU.add).then_inc(R.sem, 1)
                    dve.wait_ge(R.sem, R.at(b, "onehots"))
                    dve.tensor_tensor(w.ohs[:, :, :], w.ohs[:, :, :], w.v[:, :, :], ALU.mult).then_inc(R.sem, 1)
                    dve.wait_ge(R.sem, R.at(b, "gates"))
                    if exists(b - 2):
                        dve.wait_ge(acc_dve.sem, acc_dve.at(b - 2, f"e{E - 1}"))
                    dve.tensor_tensor(w.weight[u][:, :, :], w.ohs[:, :, :], w.vrec[:, :, :].broadcast_to([P, TT, K]),
                                      ALU.mult).then_inc(R.sem, 1)
                    if capped:
                        dve.tensor_tensor(w.counts[:, :], w.counts[:, :], w.cnt2[:, :], ALU.add).then_inc(R.sem, 1)
            turns(dve, body)

        @block.gpsimd
        def _(pool):
            def body(t):
                b = t.batch(1)
                if b is None:
                    return
                pool.wait_ge(ln_dve.sem, ln_dve.at(b, "mean1"))
                own_wait(pool)
                pool.tensor_scalar(m.var_eps[:, :], m.mean_var[:, :, 1], 1e-5, None, ALU.add).then_inc(ln_pool.sem, 1)
                pool.wait_ge(ln_pool.sem, ln_pool.at(b, "var"))
                pool.tensor_tensor(m.rstd[:, :], m.var_eps[:, :], m.minus_half[:, 0:TT], ALU.pow).then_inc(ln_pool.sem, 1)
                if w.rms:
                    pool.wait_ge(ln_pool.sem, ln_pool.at(b, "rstd"))
                    pool.tensor_tensor(w.sq[:, :], m.rstd[:, :], m.rstd[:, :], ALU.mult).then_inc(ln_pool.sem, 1)
                    pool.wait_ge(ln_pool.sem, ln_pool.at(b, "sq"))
                    pool.tensor_tensor(w.sq2[:, :], w.sq[:, :], m.mean_var[:, :, 1], ALU.mult).then_inc(ln_pool.sem, 1)
                    pool.wait_ge(ln_pool.sem, ln_pool.at(b, "mean2"))
                    own_wait(pool)
                    pool.tensor_scalar(w.sq[:, :], w.sq2[:, :], float(np.finfo(np.float32).eps), None, ALU.add)\
                        .then_inc(ln_pool.sem, 1)
                    pool.wait_ge(ln_pool.sem, ln_pool.at(b, "meps"))
                    pool.tensor_tensor(w.r2[:, :], w.sq[:, :], m.minus_half[:, 0:TT], ALU.pow)\
                        .then_inc(ln_pool.sem, 1)
            turns(pool, body)


def recurrent_layer(nc, m, w, store=None):
    ctx = ExitStack()
    with ctx:
        def sem(name):
            return ctx.enter_context(nc.semaphore(f"l1_{name}"))

        E, C = 8, 64
        H = P
        ln_dve = Steps(sem("ln_dve"), "stats0 stats1 mean0 mean1 xn0 xn1")
        ln_pool = Steps(sem("ln_pool"), "var rstd")
        enc_act = Steps(sem("enc_act"), "xnT enc z cont r1 exp")
        enc_pool = Steps(sem("enc_pool"), "spikes keep take")
        scan_dve = Steps(sem("scan_dve"), "drive scan")
        route_dve = Steps(sem("route_dve"), "logit max shift max1 eq1 key1 top1 one1 less max2 eq2 key2 top2 one2 "
                          "onehots gates sum rec weight")
        gT_act = Steps(sem("gT_act"), "gT")
        in_pe = Steps(sem("in_pe"), [f"e{e}" for e in range(E)])
        hid = [Steps(sem(f"hid_{n}"), [f"e{e}" for e in range(i, E, 2)]) for i, n in enumerate(("act", "dve"))]
        out_pe = Steps(sem("out_pe"), [f"p{p}" for p in range(E // 2)])
        acc_dve = Steps(sem("acc_dve"), ["base"] + [f"e{e}" for e in range(E)])
        dec_act = Steps(sem("dec_act"), "outT spikes decoded tanh")
        dec_pool = Steps(sem("dec_pool"), "spikes var rstd x")
        dec_dve = Steps(sem("dec_dve"), "stats0 stats1 mean0 mean1 norm0 norm1 gain y gate gated")
        out_sp = Steps(sem("out_sp"), ["stored"], 16)
        M = BankJobs(sem("m_ready"), [("xnT", 1, enc_act, "xnT"), ("gT", 0, gT_act, "gT"), ("cont", 1, enc_act, "cont"),
                                      ("r1", 1, enc_act, "r1"), ("logit", 1, route_dve, "logit")])
        Z = BankJobs(sem("z_ready"), [("enc", 1, enc_act, "enc"), ("zh", 1, scan_dve, "drive")])
        Y = BankJobs(sem("y_ready"), [("outT", -1, dec_act, "outT"), ("c2s", -1, dec_act, "spikes"),
                                      ("dec", -1, dec_act, "decoded"), ("s", -1, dec_dve, "gated")])
        zb, yb, ob = m.S[0], m.T[0], m.O
        IN = [m.F[0], m.F[1], m.S[1], m.T[1]]

        block = ctx.enter_context(nc.Block())

        @block.sync
        def _(sp):
            if store is not None:
                def body(t):
                    b = t.batch(-1)
                    if b is not None:
                        sp.wait_ge(dec_pool.sem, dec_pool.at(b, "x"))
                        sp.dma_start(store[:, bass.ds(TT * b, TT), :], xtile(m.X, b)).then_inc(out_sp.sem, 16)
                turns(sp, body)
                if exists(B - 1):
                    sp.wait_ge(out_sp.sem, out_sp.at(B - 1, "stored"))

        @block.tensor
        def _(pe):
            def hidden(b, u, p):
                if p == 0:
                    pe.wait_ge(enc_act.sem, enc_act.at(b, "cont"))
                for e in (2 * p, 2 * p + 1):
                    if exists(b if e >= 4 else b - 1):
                        pe.wait_ge(hid[e % 2].sem, hid[e % 2].at(b if e >= 4 else b - 1, f"e{(e - 4) % E}"))
                    pe.matmul(IN[e % 4][:, 0:N], w.We1[:, e, :], w.contT[u], start=True, stop=True)\
                      .then_inc(in_pe.sem, 1)

            def outputs(b, u, p):
                pe.wait_ge(hid[0].sem, hid[0].at(b, f"e{2 * p}"))
                pe.wait_ge(hid[1].sem, hid[1].at(b, f"e{2 * p + 1}"))
                if exists(b if p else b - 1):
                    pe.wait_ge(acc_dve.sem, acc_dve.at(b if p else b - 1, f"e{(2 * p - 1) % E}"))
                if p == 0:
                    pe.wait_ge(gT_act.sem, gT_act.at(b, "gT"))
                    for k in range(TT):
                        pe.matmul(ob[:, 256 + C * k:256 + C * k + C], w.gT[:, P * k:P * k + P], w.be2[:, :],
                                  start=True, stop=True, skip_group_check=True)
                for k in range(TT):
                    for i in range(2):
                        c = C * (2 * k + i)
                        mm = pe.matmul(ob[:, c:c + C], w.hid[p % 2][:, i, P * k:P * k + P], w.We2[:, 2 * p + i, :],
                                       start=True, stop=True, skip_group_check=True)
                mm.then_inc(out_pe.sem, 1)

            def body(t):
                prev, cur, nxt = (t.batch(a) for a in (-1, 0, 1))
                u = t.parity
                q = 1 - u
                if prev is not None:
                    pe.wait_ge(acc_dve.sem, acc_dve.at(prev, f"e{E - 1}"))
                    free = Y.freed(t, "outT")
                    if free:
                        pe.wait_ge(*free)
                    own_wait(pe)
                    for k in range(TT):
                        mm = pe.transpose(yb[0:C, P * k:P * k + P], w.acc[q][:, C * k:C * k + C], m.ident[:, :])
                    mm.then_inc(Y.ready, 1)
                if cur is not None:
                    hidden(cur, u, 0)
                if nxt is not None:
                    pe.wait_ge(ln_dve.sem, ln_dve.at(nxt, "xn1"))
                    free = M.freed(t, "xnT")
                    if free:
                        pe.wait_ge(*free)
                    for k in range(TT):
                        mm = pe.transpose(m.M[:, P * k:P * k + P], m.xn[:, k, :], m.ident[:, :])
                    mm.then_inc(M.ready, 1)
                if cur is not None:
                    hidden(cur, u, 1)
                    pe.wait_ge(route_dve.sem, route_dve.at(cur, "weight"))
                    free = M.freed(t, "gT")
                    if free:
                        pe.wait_ge(*free)
                    for k in range(TT):
                        mm = pe.transpose(m.M[0:E, P * k:P * k + P], w.weight[u][:, k, :], m.ident[:, :])
                    mm.then_inc(M.ready, 1)
                if prev is not None:
                    pe.wait_ge(dec_act.sem, dec_act.at(prev, "outT"))
                    for c in range(2):
                        mm = pe.matmul(yb[:, N * c:N * c + N], w.c2s[:, P * c:P * c + P], w.outT[:, :],
                                       start=True, stop=True)
                    mm.then_inc(Y.ready, 1)
                if cur is not None:
                    outputs(cur, u, 0)
                    hidden(cur, u, 2)
                if nxt is not None:
                    free = Z.freed(t, "enc")
                    if free:
                        pe.wait_ge(*free)
                    pe.wait_ge(enc_act.sem, enc_act.at(nxt, "xnT"))
                    for c in range(2):
                        mm = pe.matmul(zb[:, N * c:N * c + N], w.enc[:, P * c:P * c + P], m.xnT[q][:, :],
                                       start=True, stop=True)
                    mm.then_inc(Z.ready, 1)
                if cur is not None:
                    outputs(cur, u, 1)
                    hidden(cur, u, 3)
                if nxt is not None:
                    free = Z.freed(t, "zh")
                    if free:
                        pe.wait_ge(*free)
                    for c, W in enumerate((w.Wz, w.Wh)):
                        mm = pe.matmul(zb[:, N * c:N * c + N], W[:, :], m.xnT[q][:, :], start=True, stop=True)
                    mm.then_inc(Z.ready, 1)
                if prev is not None:
                    pe.wait_ge(dec_pool.sem, dec_pool.at(prev, "spikes"))
                    free = Y.freed(t, "dec")
                    if free:
                        pe.wait_ge(*free)
                    for k in range(TT):
                        for c in range(2):
                            pe.matmul(yb[:, P * k:P * k + P], w.spikes2[:, c, P * k:P * k + P], w.dec[:, c, :],
                                      start=(c == 0), stop=False)
                        mm = pe.matmul(yb[:, P * k:P * k + P], m.ones[0:1, 0:P], w.dec_b[:, :], start=False, stop=True)
                    mm.then_inc(Y.ready, 1)
                if cur is not None:
                    outputs(cur, u, 2)
                if nxt is not None:
                    pe.wait_ge(enc_pool.sem, enc_pool.at(nxt, "spikes"))
                    free = M.freed(t, "cont")
                    if free:
                        pe.wait_ge(*free)
                    for c in range(2):
                        mm = pe.matmul(m.M[0:C, 0:N], w.s2c[:, c, :], w.spikes[:, c, :], start=(c == 0), stop=(c == 1))
                    mm.then_inc(M.ready, 1)
                if prev is not None:
                    pe.wait_ge(scan_dve.sem, scan_dve.at(prev, "scan"))
                    free = Y.freed(t, "s")
                    if free:
                        pe.wait_ge(*free)
                    for k in range(TT):
                        mm = pe.matmul(yb[:, P * k:P * k + P], w.hT[q][:, P * k:P * k + P], w.diffuse[:, :],
                                       start=True, stop=True)
                    mm.then_inc(Y.ready, 1)
                if cur is not None:
                    outputs(cur, u, 3)
                if nxt is not None:
                    free = M.freed(t, "r1")
                    if free:
                        pe.wait_ge(*free)
                    own_wait(pe)
                    pe.matmul(m.M[0:C, 0:N], w.rW1[:, :], w.contT[q], start=True, stop=True).then_inc(M.ready, 1)
                if nxt is not None:
                    free = M.freed(t, "logit")
                    if free:
                        pe.wait_ge(*free)
                    for k in range(TT):
                        mm = pe.matmul(m.M[:, E * k:E * k + E], w.r1T[:, P * k:P * k + P], w.rW2[:, :],
                                       start=True, stop=True)
                    mm.then_inc(M.ready, 1)
            turns(pe, body)

        @block.scalar
        def _(act):
            def relu(b, e):
                act.wait_ge(in_pe.sem, in_pe.at(b, f"e{e}"))
                if exists(b if e >= 4 else b - 1):
                    act.wait_ge(out_pe.sem, out_pe.at(b if e >= 4 else b - 1, f"p{(e // 2 - 2) % 4}"))
                act.activation(w.hid[e // 2 % 2][:, 0, :], IN[e % 4][:, 0:N], ACT.Relu, bias=w.be1[:, e:e + 1])\
                   .then_inc(hid[0].sem, 1)

            def body(t):
                prev, cur, nxt = (t.batch(a) for a in (-1, 0, 1))
                u, q = t.parity, 1 - t.parity
                if prev is not None:
                    act.wait_ge(Y.ready, Y.filled(t, "outT"))
                    act.activation(w.outT[:, :], yb[0:C, 0:N], ACT.Copy).then_inc(dec_act.sem, 1)
                if cur is not None:
                    relu(cur, 0)
                if nxt is not None:
                    act.wait_ge(M.ready, M.filled(t, "xnT"))
                    act.activation(m.xnT[q][:, :], m.M[:, 0:N], ACT.Copy).then_inc(enc_act.sem, 1)
                if cur is not None:
                    relu(cur, 2)
                    act.wait_ge(M.ready, M.filled(t, "gT"))
                    if exists(cur - 1):
                        act.wait_ge(out_pe.sem, out_pe.at(cur - 1, "p0"))
                    act.activation(w.gT[:, :], m.M[0:E, 0:N], ACT.Copy).then_inc(gT_act.sem, 1)
                if prev is not None:
                    act.wait_ge(Y.ready, Y.filled(t, "c2s"))
                    if exists(prev - 1):
                        act.wait_ge(dec_pool.sem, dec_pool.at(prev - 1, "spikes"))
                    for c in range(2):
                        a = act.activation(w.th2[:, c, :], yb[:, N * c:N * c + N], ACT.Tanh, scale=0.5,
                                           bias=w.c2s_b[:, c:c + 1])
                    a.then_inc(dec_act.sem, 1)
                if cur is not None:
                    relu(cur, 4)
                if nxt is not None:
                    act.wait_ge(Z.ready, Z.filled(t, "enc"))
                    if exists(nxt - 1):
                        act.wait_ge(enc_pool.sem, enc_pool.at(nxt - 1, "spikes"))
                    for c in range(2):
                        a = act.activation(w.th[:, c, :], zb[:, N * c:N * c + N], ACT.Tanh, scale=0.5,
                                           bias=w.enc_b[:, c:c + 1])
                    a.then_inc(enc_act.sem, 1)
                if cur is not None:
                    relu(cur, 6)
                if nxt is not None:
                    act.wait_ge(Z.ready, Z.filled(t, "zh"))
                    if exists(nxt - 1):
                        act.wait_ge(enc_pool.sem, enc_pool.at(nxt - 1, "take"))
                    act.activation(w.zth[:, :], zb[:, 0:N], ACT.Tanh, scale=0.5, bias=w.bz[:, :])\
                       .then_inc(enc_act.sem, 1)
                if prev is not None:
                    act.wait_ge(Y.ready, Y.filled(t, "dec"))
                    if exists(prev - 1):
                        act.wait_ge(dec_dve.sem, dec_dve.at(prev - 1, "norm1"))
                    act.activation(w.dth[:, :, :], yb[:, 0:N].rearrange("p (k c) -> p k c", k=TT), ACT.Tanh, scale=0.5)\
                       .then_inc(dec_act.sem, 1)
                if nxt is not None:
                    act.wait_ge(M.ready, M.filled(t, "cont"))
                    act.activation(w.contT[q], m.M[0:C, 0:N], ACT.Identity, bias=w.s2c_b[:, :])\
                       .then_inc(enc_act.sem, 1)
                    act.wait_ge(M.ready, M.filled(t, "r1"))
                    act.activation(w.r1T[:, :], m.M[0:C, 0:N], ACT.Tanh, bias=w.rb1[:, :]).then_inc(enc_act.sem, 1)
                if prev is not None:
                    act.wait_ge(dec_dve.sem, dec_dve.at(prev, "y"))
                    act.activation(w.gth[:, :, :], w.y[:, :, :], ACT.Tanh, scale=0.5).then_inc(dec_act.sem, 1)
                if nxt is not None:
                    act.wait_ge(route_dve.sem, route_dve.at(nxt, "shift"))
                    act.activation(w.v[:, :, :], w.v0[:, :, :], ACT.Exp).then_inc(enc_act.sem, 1)
            turns(act, body)

        @block.vector
        def _(dve):
            def relu(b, e):
                dve.wait_ge(in_pe.sem, in_pe.at(b, f"e{e}"))
                if exists(b if e >= 4 else b - 1):
                    dve.wait_ge(out_pe.sem, out_pe.at(b if e >= 4 else b - 1, f"p{(e // 2 - 2) % 4}"))
                dve.tensor_scalar(w.hid[e // 2 % 2][:, 1, :], IN[e % 4][:, 0:N], w.be1[:, e:e + 1], 0.0, ALU.add, ALU.max)\
                   .then_inc(hid[1].sem, 1)

            def accumulate(b, u, p):
                for i in range(2):
                    e = 2 * p + i
                    if i == 0:
                        dve.wait_ge(out_pe.sem, out_pe.at(b, f"p{p}"))
                    if e == 0:
                        dve.tensor_copy(w.acc[u][:, 0:TT * C], ob[:, 256:256 + TT * C]).then_inc(acc_dve.sem, 1)
                    dve.wait_ge(acc_dve.sem, acc_dve.at(b, f"e{e - 1}" if e else "base"))
                    for k in range(TT):
                        acc = w.acc[u][:, C * k:C * k + C]
                        a = dve.scalar_tensor_tensor(acc, ob[:, C * (2 * k + i):C * (2 * k + i) + C],
                                                     w.weight[u][:, k, e:e + 1], acc, ALU.mult, ALU.add)
                    a.then_inc(acc_dve.sem, 1)

            R = route_dve

            def top(b, n):
                v = w.v if n == 1 else w.v2
                dve.tensor_reduce(w.mx[:, :, :], v[:, :, :], AX.X, ALU.max).then_inc(R.sem, 1)
                dve.wait_ge(R.sem, R.at(b, f"max{n}"))
                dve.tensor_tensor(w.eq[:, :, :], v[:, :, :], w.mx[:, :, :].broadcast_to([P, TT, E]), ALU.is_ge)\
                   .then_inc(R.sem, 1)
                dve.wait_ge(R.sem, R.at(b, f"eq{n}"))
                dve.tensor_tensor(w.eq[:, :, :], w.eq[:, :, :], m.rank[:, :, :], ALU.mult).then_inc(R.sem, 1)
                dve.wait_ge(R.sem, R.at(b, f"key{n}"))
                dve.tensor_reduce(w.mx[:, :, :], w.eq[:, :, :], AX.X, ALU.max).then_inc(R.sem, 1)
                dve.wait_ge(R.sem, R.at(b, f"top{n}"))
                dve.tensor_tensor(w.one[:, :, E * (n - 1):E * n], w.eq[:, :, :],
                                  w.mx[:, :, :].broadcast_to([P, TT, E]), ALU.is_equal).then_inc(R.sem, 1)
                dve.wait_ge(R.sem, R.at(b, f"one{n}"))

            def route(b, u, t):
                dve.wait_ge(M.ready, M.filled(t, "logit"))
                if exists(b - 1):
                    dve.wait_ge(R.sem, R.at(b - 1, "weight"))
                dve.tensor_tensor(w.v0[:, :, :], m.M[:, 0:TT * E].rearrange("p (k e) -> p k e", k=TT), w.rb2[:, :, :],
                                  ALU.add).then_inc(R.sem, 1)
                dve.wait_ge(R.sem, R.at(b, "logit"))
                dve.tensor_reduce(w.mx[:, :, :], w.v0[:, :, :], AX.X, ALU.max).then_inc(R.sem, 1)
                dve.wait_ge(R.sem, R.at(b, "max"))
                dve.tensor_tensor(w.v0[:, :, :], w.v0[:, :, :], w.mx[:, :, :].broadcast_to([P, TT, E]), ALU.subtract)\
                   .then_inc(R.sem, 1)
                dve.wait_ge(enc_act.sem, enc_act.at(b, "exp"))
                top(b, 1)
                dve.scalar_tensor_tensor(w.v2[:, :, :], w.one[:, :, 0:E], MASKED, w.v[:, :, :], ALU.mult, ALU.add)\
                   .then_inc(R.sem, 1)
                dve.wait_ge(R.sem, R.at(b, "less"))
                top(b, 2)
                dve.tensor_tensor(w.ohs[:, :, :], w.one[:, :, 0:E], w.one[:, :, E:2 * E], ALU.add).then_inc(R.sem, 1)
                dve.wait_ge(R.sem, R.at(b, "onehots"))
                dve.tensor_tensor(w.ohs[:, :, :], w.ohs[:, :, :], w.v[:, :, :], ALU.mult).then_inc(R.sem, 1)
                dve.wait_ge(R.sem, R.at(b, "gates"))
                dve.tensor_reduce(w.mx[:, :, :], w.ohs[:, :, :], AX.X, ALU.add).then_inc(R.sem, 1)
                dve.wait_ge(R.sem, R.at(b, "sum"))
                dve.reciprocal(w.vrec[:, :, :], w.mx[:, :, :]).then_inc(R.sem, 1)
                dve.wait_ge(R.sem, R.at(b, "rec"))
                dve.tensor_tensor(w.weight[u][:, :, :], w.ohs[:, :, :], w.vrec[:, :, :].broadcast_to([P, TT, E]),
                                  ALU.mult).then_inc(R.sem, 1)

            def body(t):
                prev, cur, nxt, new = (t.batch(a) for a in (-1, 0, 1, 2))
                u, q = t.parity, 1 - t.parity
                if cur is not None:
                    relu(cur, 1)
                    relu(cur, 3)
                    accumulate(cur, u, 0)
                    relu(cur, 5)
                if new is not None:
                    if exists(new - 1):
                        dve.wait_ge(ln_pool.sem, ln_pool.at(new - 1, "rstd"))
                    if exists(new - 1):
                        dve.wait_ge(ln_dve.sem, ln_dve.at(new - 1, "xn1"))
                    for k in range(TT):
                        dve.bn_stats(m.stats[:, k, :], xtile(m.X, new, k, 1)).then_inc(ln_dve.sem, 1)
                    for k in range(TT):
                        dve.wait_ge(ln_dve.sem, ln_dve.at(new, f"stats{k}"))
                        own_wait(dve)
                        dve.bn_aggr(m.mean_var[:, k, :], m.stats[:, k, :]).then_inc(ln_dve.sem, 1)
                if cur is not None:
                    accumulate(cur, u, 1)
                    relu(cur, 7)
                if nxt is not None:
                    dve.wait_ge(Z.ready, Z.filled(t, "zh"))
                    dve.wait_ge(enc_pool.sem, enc_pool.at(nxt, "take"))
                    if exists(nxt - 1):
                        dve.wait_ge(scan_dve.sem, scan_dve.at(nxt - 1, "scan"))
                    dve.scalar_tensor_tensor(w.drive[:, :], zb[:, N:2 * N], w.bh[:, :], w.take[:, :], ALU.add, ALU.mult)\
                       .then_inc(scan_dve.sem, 1)
                if prev is not None:
                    D_ = dec_dve
                    dve.wait_ge(dec_act.sem, dec_act.at(prev, "decoded"))
                    if exists(prev - 1):
                        dve.wait_ge(dec_pool.sem, dec_pool.at(prev - 1, "rstd"))
                    for k in range(TT):
                        dve.bn_stats(w.stats[:, k, :], w.dth[:, k, :]).then_inc(D_.sem, 1)
                    for k in range(TT):
                        dve.wait_ge(D_.sem, D_.at(prev, f"stats{k}"))
                        own_wait(dve)
                        dve.bn_aggr(w.mean_var[:, k, :], w.stats[:, k, :]).then_inc(D_.sem, 1)
                if cur is not None:
                    accumulate(cur, u, 2)
                if nxt is not None:
                    if prev is not None:
                        dve.wait_ge(Y.ready, Y.filled(t, "s"))
                    dve.wait_ge(scan_dve.sem, scan_dve.at(nxt, "drive"))
                    dve.tensor_tensor_scan(w.hT[q], w.keep, w.drive, 0.0, ALU.mult, ALU.add)\
                       .then_inc(scan_dve.sem, 1)
                if new is not None:
                    dve.wait_ge(ln_pool.sem, ln_pool.at(new, "rstd"))
                    if nxt is not None:
                        dve.wait_ge(M.ready, M.filled(t, "xnT"))
                    for k in range(TT):
                        dve.tensor_scalar(m.xn[:, k, :], xtile(m.X, new, k, 1), m.mean_var[:, k, 0:1],
                                          m.rstd[:, k:k + 1], ALU.subtract, ALU.mult).then_inc(ln_dve.sem, 1)
                if prev is not None:
                    dve.wait_ge(dec_pool.sem, dec_pool.at(prev, "rstd"))
                    for k in range(TT):
                        dve.tensor_scalar(w.yn[:, k, :], w.dth[:, k, :], w.mean_var[:, k, 0:1], w.rstd[:, k:k + 1],
                                          ALU.subtract, ALU.mult).then_inc(D_.sem, 1)
                    dve.wait_ge(D_.sem, D_.at(prev, "norm1"))
                    dve.tensor_tensor(w.yn[:, :, :], w.yn[:, :, :], w.ln_g[:, :].unsqueeze(1).broadcast_to([P, TT, D]),
                                      ALU.mult).then_inc(D_.sem, 1)
                    dve.wait_ge(D_.sem, D_.at(prev, "gain"))
                    dve.tensor_tensor(w.y[:, :, :], w.yn[:, :, :], w.ln_b[:, :].unsqueeze(1).broadcast_to([P, TT, D]),
                                      ALU.add).then_inc(D_.sem, 1)
                if cur is not None:
                    accumulate(cur, u, 3)
                if prev is not None:
                    dve.wait_ge(dec_act.sem, dec_act.at(prev, "tanh"))
                    dve.scalar_tensor_tensor(w.gate[:, :, :], w.gth[:, :, :], 1.0, w.y[:, :, :], ALU.add, ALU.mult)\
                       .then_inc(D_.sem, 1)
                    dve.wait_ge(D_.sem, D_.at(prev, "gate"))
                    dve.wait_ge(Y.ready, Y.filled(t, "s"))
                    if exists(prev - 1):
                        dve.wait_ge(dec_pool.sem, dec_pool.at(prev - 1, "x"))
                    dve.scalar_tensor_tensor(m.gated[:, :, :], yb[:, 0:N].rearrange("p (k c) -> p k c", k=TT), 0.5,
                                             w.gate[:, :, :], ALU.mult, ALU.mult).then_inc(D_.sem, 1)
                if nxt is not None:
                    route(nxt, q, t)
            turns(dve, body)

        @block.gpsimd
        def _(pool):
            def body(t):
                prev, cur, nxt, new = (t.batch(a) for a in (-1, 0, 1, 2))
                if prev is not None:
                    pool.wait_ge(dec_act.sem, dec_act.at(prev, "spikes"))
                    own_wait(pool)
                    pool.tensor_scalar(w.spikes2[:, :, :], w.th2[:, :, :], 0.5, 0.5, ALU.mult, ALU.add)\
                        .then_inc(dec_pool.sem, 1)
                if nxt is not None:
                    pool.wait_ge(enc_act.sem, enc_act.at(nxt, "enc"))
                    own_wait(pool)
                    pool.tensor_scalar(w.spikes[:, :, :], w.th[:, :, :], 0.5, 0.5, ALU.mult, ALU.add)\
                        .then_inc(enc_pool.sem, 1)
                if new is not None:
                    pool.wait_ge(ln_dve.sem, ln_dve.at(new, "mean1"))
                    own_wait(pool)
                    pool.tensor_scalar(m.var_eps[:, :], m.mean_var[:, :, 1], 1e-5, None, ALU.add)\
                        .then_inc(ln_pool.sem, 1)
                    pool.wait_ge(ln_pool.sem, ln_pool.at(new, "var"))
                    pool.tensor_tensor(m.rstd[:, :], m.var_eps[:, :], m.minus_half[:, 0:TT], ALU.pow)\
                        .then_inc(ln_pool.sem, 1)
                if nxt is not None:
                    pool.wait_ge(enc_act.sem, enc_act.at(nxt, "z"))
                    if exists(nxt - 1):
                        pool.wait_ge(scan_dve.sem, scan_dve.at(nxt - 1, "scan"))
                    own_wait(pool)
                    pool.tensor_scalar(w.keep[:, :], w.zth[:, :], -0.5, 0.5, ALU.mult, ALU.add)\
                        .then_inc(enc_pool.sem, 1)
                    pool.tensor_scalar(w.take[:, :], w.zth[:, :], 0.5, 0.5, ALU.mult, ALU.add)\
                        .then_inc(enc_pool.sem, 1)
                if prev is not None:
                    pool.wait_ge(dec_dve.sem, dec_dve.at(prev, "mean1"))
                    own_wait(pool)
                    pool.tensor_scalar(w.var_eps[:, :], w.mean_var[:, :, 1], 4e-5, None, ALU.add)\
                        .then_inc(dec_pool.sem, 1)
                    pool.wait_ge(dec_pool.sem, dec_pool.at(prev, "var"))
                    pool.tensor_tensor(w.rstd[:, :], w.var_eps[:, :], m.minus_half[:, 0:TT], ALU.pow)\
                        .then_inc(dec_pool.sem, 1)
                    pool.wait_ge(dec_dve.sem, dec_dve.at(prev, "gated"))
                    X = xtile(m.X, prev)
                    pool.tensor_tensor(X, X, m.gated[:, :, :], ALU.add).then_inc(dec_pool.sem, 1)
            turns(pool, body)



class Memory:

    def __init__(self, nc, ctx):
        def sb(name, shape, dt=F32):
            return ctx.enter_context(nc.sbuf_tensor(name, shape, dt))

        def bank(name):
            return ctx.enter_context(nc.psum_tensor(name, [P, 512], F32))

        self.X = sb("X", [P, B * TT, D])
        self.xnT = [sb(f"xnT{u}", [P, N]) for u in range(2)]
        self.xn = sb("xn", [P, TT, D])
        self.stats = sb("stats", [P, TT, 6])
        self.mean_var = sb("mean_var", [P, TT, 2])
        self.var_eps = sb("var_eps", [P, TT])
        self.rstd = sb("rstd", [P, TT])
        self.rc = sb("rc", [P, 2 * N])
        self.turned = sb("turned", [P, 2, 2 * N])
        self.rest = sb("rest", [P, 2, N])
        self.parts = sb("parts", [P, 3, 2, N], BF16)
        self.parts_dram = nc.dram_tensor("parts_dram", [2, 2, 3, HD, HEADS * N], BF16, kind="Internal").ap()
        self.stack = [[sb(f"stack{o}{u}", [P, HEADS, N], BF16) for u in range(2)] for o in range(2)]
        self.rowmax = sb("rowmax", [P, TT, HEADS])
        self.shift = [sb(f"shift{i}", [HEADS // 2, 2, N], BF16) for i in range(2)]
        self.prob = sb("prob", [P, PRING, 512])
        self.vaug = [sb(f"vaug{u}", [P, TT, HEADS, 32]) for u in range(2)]
        self.oTn = [sb(f"oTn{u}", [P, GROUPS, N]) for u in range(2)]
        self.rsum = sb("rsum", [P, TT, HEADS])
        self.o = sb("o", [P, TT, D])
        self.oT = sb("oT", [P, N])
        self.gated = sb("gated", [P, TT, D])
        self.gate = sb("gate", [P, B * TT, D])
        self.W1 = sb("W1", [P, 10, 512])
        self.W2 = sb("W2", [P, 10, 4, P])
        self.ident = sb("ident", [P, P])
        self.ident_b = sb("ident_b", [P, P], BF16)
        self.tri = self.prob[:, 3, 0:2 * P].rearrange("p (k n) -> p k n", k=2)
        self.tri2 = sb("tri2", [P, 2, 2, P], BF16)
        self.cossin = sb("cossin", [P, 2 * N])
        self.upto = sb("upto", [P, P])
        self.rank = sb("rank", [P, TT, 8])
        self.ones = sb("ones", [P, P])
        self.minus_half = sb("minus_half", [P, 16])
        self.S = [bank(f"S{i}") for i in range(2)]
        self.T = [bank(f"T{i}") for i in range(2)]
        self.O = bank("O")
        self.M = bank("M")
        self.F = [bank(f"F{i}") for i in range(2)]


class Gated:

    def gate(self, b, u):
        return xtile(self.m.gate, b)


class SwigluFfn(Gated):

    CHUNKS = 3
    STAGE = {1: 0, 3: 1, 5: 2, 7: 3}

    def __init__(self, w):
        self.w = w

    def open(self, nc, sem, m, xnT_act):
        self.m, self.xnT_act = m, xnT_act
        c = range(self.CHUNKS)
        self.pe = Steps(sem("ffn_pe"), [f"in{i}" for i in c] + ["out"])
        self.act = Steps(sem("ffn_act"), [f"tanh{i}" for i in c] + ["tanh"])
        self.dve = Steps(sem("ffn_dve"), [f"{x}{i}" for i in c for x in ("silu", "hid")] + ["gate"])
        return self

    def bank_free(self, pe, b, i):
        steps = [f"hid{k}" for k in range(self.CHUNKS)] + ["gate"]
        if exists(b if i >= 2 else b - 1):
            pe.wait_ge(self.dve.sem, self.dve.at(b if i >= 2 else b - 1, steps[i - 2]))

    def tensor(self, pe, b, u, s):
        s = self.STAGE.get(s, -1)
        if s < 0:
            return
        m, n = self.m, self.CHUNKS
        if s == 0:
            pe.wait_ge(self.xnT_act.sem, self.xnT_act.at(b, "xnT"))
        if s < n:
            self.bank_free(pe, b, s)
            for i in range(2):
                mm = pe.matmul(m.F[s % 2][:, N * i:N * i + N], self.w.gate_up[:, i, P * s:P * s + P], m.xnT[u][:, :],
                               start=True, stop=True)
            mm.then_inc(self.pe.sem, 1)
        if s == n:
            self.bank_free(pe, b, n)
            pe.wait_ge(self.dve.sem, self.dve.at(b, f"hid{n - 1}"))
            for k in range(TT):
                for c in range(n):
                    mm = pe.matmul(m.F[n % 2][:, P * k:P * k + P], self.w.hid[:, c, P * k:P * k + P],
                                   self.w.down[:, c, :], start=(c == 0), stop=(c == n - 1))
            mm.then_inc(self.pe.sem, 1)

    def scalar(self, act, b, u, s):
        s = self.STAGE.get(s, -1)
        if s < 0:
            return
        m, n = self.m, self.CHUNKS
        if s < n:
            act.wait_ge(self.pe.sem, self.pe.at(b, f"in{s}"))
            if exists(b if s else b - 1):
                act.wait_ge(self.dve.sem, self.dve.at(b if s else b - 1, f"silu{s - 1}" if s else "gate"))
            act.activation(self.w.th[:, :], m.F[s % 2][:, 0:N], ACT.Tanh, scale=0.5).then_inc(self.act.sem, 1)
        if s == n:
            act.wait_ge(self.pe.sem, self.pe.at(b, "out"))
            act.wait_ge(self.dve.sem, self.dve.at(b, f"silu{n - 1}"))
            act.activation(self.w.th[:, :], m.F[n % 2][:, 0:N], ACT.Tanh, scale=0.5).then_inc(self.act.sem, 1)

    def vector(self, dve, b, u, s):
        s = self.STAGE.get(s, -1)
        if s < 0:
            return
        m, n = self.m, self.CHUNKS
        if s < n:
            F = m.F[s % 2]
            dve.wait_ge(self.act.sem, self.act.at(b, f"tanh{s}"))
            if exists(b if s else b - 1):
                dve.wait_ge(self.dve.sem, self.dve.at(b if s else b - 1, f"hid{(s - 1) % n}"))
            dve.scalar_tensor_tensor(self.w.silu[:, :], self.w.th[:, :], 1.0, F[:, 0:N], ALU.add, ALU.mult)\
               .then_inc(self.dve.sem, 1)
            dve.wait_ge(self.dve.sem, self.dve.at(b, f"silu{s}"))
            if s == 0:
                if exists(b - 1):
                    dve.wait_ge(self.pe.sem, self.pe.at(b - 1, "out"))
            dve.scalar_tensor_tensor(self.w.hid[:, s, :], self.w.silu[:, :], 0.5, F[:, N:2 * N], ALU.mult, ALU.mult)\
               .then_inc(self.dve.sem, 1)
        if s == n:
            dve.wait_ge(self.act.sem, self.act.at(b, "tanh"))
            dve.scalar_tensor_tensor(self.gate(b, u), self.w.th[:, :].rearrange("p (k c) -> p k c", k=TT), 1.0,
                                     m.F[n % 2][:, 0:N].rearrange("p (k c) -> p k c", k=TT), ALU.add, ALU.mult)\
               .then_inc(self.dve.sem, 1)

    def gpsimd(self, pool, b, u):
        pass

    def gate_ready(self, eng, b):
        eng.wait_ge(self.dve.sem, self.dve.at(b, "gate"))


class Holder:
    pass


def layer0(nc, ctx, load, m):
    def sb(name, shape, dt=F32):
        return ctx.enter_context(nc.sbuf_tensor(name, shape, dt))

    w = Holder()
    w.w = {}
    for key, src in (("A", "L0_attn_WkT"), ("B", "L0_attn_WqT"), ("V", "L0_attn_WvT"), ("O", "L0_attn_WoT")):
        t = sb(f"l0_{key}", [P, P])
        load(t[:, :], src)
        w.w[key] = t[:, :]
    w.bA, w.bB, w.bv = (sb(f"l0_{x}", [P, 1]) for x in ("bA", "bB", "bv"))
    load(w.bA[:, :], "L0_attn_bk", col=True)
    load(w.bB[:, :], "L0_attn_bq", col=True)
    load(w.bv[:, :], "L0_attn_bv", col=True)
    w.w["bA"], w.w["bB"] = w.bA[:, :], w.bB[:, :]
    w.bo = sb("l0_bo", [1, P])
    load(w.bo[:, :], "L0_attn_bo", row=True)
    w.w["bo"] = w.bo2 = sb("l0_bo2", [1, P])
    w.w["bo"] = w.bo2[:, :]
    w.ints = m.prob[:, 0:3, 0:384].bitcast(I32)
    load(w.ints[:, 0, :], "L0_ffn_w_gateT")
    load(w.ints[:, 1, :], "L0_ffn_w_upT")
    load(w.ints[:, 2, :].rearrange("p (c n) -> p c n", c=3), "L0_ffn_w_downT", chunks=3)
    w.gate_up = sb("l0_gate_up", [P, 2, 384])
    w.down = sb("l0_down", [P, 3, P])
    w.th, w.silu, w.hid = sb("l0_th", [P, N]), sb("l0_silu", [P, N]), sb("l0_hid", [P, 3, N])
    return w


def layer1(nc, ctx, load, m, w2):
    def sb(name, shape, src, **how):
        t = ctx.enter_context(nc.sbuf_tensor(f"l1_{name}", shape, F32))
        load(t[:, :] if len(shape) == 2 else t[:, :, :], src, **how)
        return t

    w = Holder()
    w.Wz, w.Wh = sb("Wz", [P, P], "L1_attn_Wz"), sb("Wh", [P, P], "L1_attn_Wh")
    w.bz, w.bh = sb("bz", [P, 1], "L1_attn_bz", col=True), sb("bh", [P, 1], "L1_attn_bh", col=True)
    w.diffuse = sb("diffuse", [P, P], "L1_attn_log_D", every=True)
    w.lap = sb("lap", [P, P], "const_lap")
    w.enc, w.enc_b = sb("enc", [P, N], "L1_ffn_enc_W"), sb("enc_b", [P, 2], "L1_ffn_enc_b")
    w.s2c, w.s2c_b = sb("s2c", [P, 2, 64], "L1_ffn_s2c_W"), sb("s2c_b", [64, 1], "L1_ffn_s2c_b", col=True)
    w.rW1, w.rb1 = sb("rW1", [64, 64], "L1_ffn_rW1"), sb("rb1", [64, 1], "L1_ffn_rb1", col=True)
    w.rW2 = sb("rW2", [64, 8], "L1_ffn_rW2")
    w.rb2 = ctx.enter_context(nc.sbuf_tensor("l1_rb2", [P, TT, 8], F32))
    for k in range(TT):
        load(w.rb2[:, k, :], "L1_ffn_rb2", every=True)
    w.We1, w.be1 = sb("We1", [64, 8, P], "L1_ffn_We1"), sb("be1", [P, 8], "L1_ffn_be1T")
    w.We2, w.be2 = sb("We2", [P, 8, 64], "L1_ffn_We2"), sb("be2", [8, 64], "L1_ffn_be2")
    w.c2s, w.c2s_b = sb("c2s", [64, N], "L1_ffn_c2s_W"), sb("c2s_b", [P, 2], "L1_ffn_c2s_b")
    w.dec, w.dec_b = sb("dec", [P, 2, P], "L1_ffn_dec_W"), sb("dec_b", [1, P], "L1_ffn_dec_b", row=True)
    w.ln_g, w.ln_b = sb("ln_g", [P, P], "L1_ffn_ln_g", every=True), sb("ln_b", [P, P], "L1_ffn_ln_b", every=True)
    w.v0, w.v, w.v2, w.eq, w.one, w.ohs = w2.v0, w2.v, w2.v2, w2.eq, w2.one, w2.ohs
    w.mx, w.vrec, w.weight = w2.mx, w2.vrec, w2.weight
    pair = [m.prob[:, i, :].rearrange("p (a n) -> p a n", a=2) for i in range(PRING)]
    w.th, w.spikes, w.th2, w.spikes2 = pair[0:4]
    w.hid = pair[4:6]
    w.zth, w.keep, w.take, w.drive = (m.prob[:, 6 + i // 2, N * (i % 2):N * (i % 2) + N] for i in range(4))
    w.hT = [m.oTn[u][:, 0, :] for u in range(2)]
    w.contT = [m.oTn[u][0:64, 1, :] for u in range(2)]
    w.r1T, w.outT = (m.oTn[u][0:64, 2, :] for u in range(2))
    w.acc = [m.rest[:, u, :] for u in range(2)]
    w.dth, w.yn, w.y, w.gth = (m.turned[:, i // 2, N * (i % 2):N * (i % 2) + N].rearrange("p (k c) -> p k c", k=TT)
                               for i in range(4))
    w.gate = m.oTn[0][:, 3, :].rearrange("p (k c) -> p k c", k=TT)
    w.gT = m.oT[0:8, :]
    w.stats, w.mean_var = w2.stats, w2.mean_var
    w.var_eps, w.rstd = w2.var_eps, w2.rstd
    return w


def layer1_weights(nc, ctx, m, w):
    s_exp = ctx.enter_context(nc.semaphore("l1w_exp"))
    s_mul = ctx.enter_context(nc.semaphore("l1w_mul"))
    with nc.Block() as block:
        @block.scalar
        def _(act):
            act.activation(m.xn[:, 0, :], w.diffuse[:, :], ACT.Exp).then_inc(s_exp, 1)

        @block.vector
        def _(dve):
            for b in (w.bz, w.enc_b, w.c2s_b):
                dve.tensor_scalar(b[:, :], b[:, :], 0.5, None, ALU.mult)
            dve.wait_ge(s_exp, 1)
            dve.tensor_tensor(m.xn[:, 1, :], m.xn[:, 0, :], w.lap[:, :], ALU.mult).then_inc(s_mul, 1)
            dve.wait_ge(s_mul, 1)
            dve.tensor_tensor(w.diffuse[:, :], m.xn[:, 1, :], m.ident[:, :], ALU.add)


class Precomputed(Gated):

    def open(self, nc, sem, m, xnT_act):
        self.m = m
        return self

    def tensor(self, pe, b, u, s):
        pass

    scalar = vector = tensor

    def gpsimd(self, pool, b, u):
        pass

    def gate_ready(self, eng, b):
        pass


def moe_weights(nc, ctx, load, m, tag, experts, capacity, sigmoid, rms, relu):
    def sb(name, shape, dt=F32):
        return ctx.enter_context(nc.sbuf_tensor(f"{tag}_{name}", shape, dt))

    w, K = Holder(), 8
    first = experts - K
    w.experts, w.capacity, w.sigmoid, w.rms, w.relu, w.plus_x = experts, capacity, sigmoid, rms, relu, rms
    w.W1, w.W2 = m.W1[:, 0:experts, :], m.W2[:, 0:experts, :, :]
    w.b1 = sb("b1", [P, experts, 4])
    w.router, w.b2 = sb("router", [P, K]), sb("b2", [K, P])
    w.v0, w.v, w.v2, w.eq = (sb(x, [P, TT, K]) for x in ("v0", "v", "v2", "eq"))
    w.mx, w.vsum, w.vrec = (sb(x, [P, TT, 1]) for x in ("mx", "vsum", "vrec"))
    w.one, w.kept, w.ohs = sb("one", [P, TT, 2 * K]), sb("kept", [P, TT, 2 * K]), sb("onehots", [P, TT, K])
    w.cnt2, w.counts = sb("chosen", [P, 2 * K]), sb("counts", [P, 2 * K])
    w.weight = [sb(f"weight{u}", [P, TT, K]) for u in range(2)]
    w.gT = [sb(f"gT{u}", [K, N]) for u in range(2)]
    w.hT = [m.prob[:, 2 * r:2 * r + 2, :].rearrange("p a (b n) -> p (a b) n", b=2) for r in range(4)]
    tiles = [m.rc[:, N * i:N * i + N] for i in range(2)] + [m.rest[:, 0, :]]
    w.acc, w.th, w.xr = (t.rearrange("p (k c) -> p k c", k=TT) for t in tiles)
    w.stats, w.mean_var = sb("stats", [P, TT, 6]), sb("mean_var", [P, TT, 2])
    w.var_eps, w.rstd = sb("var_eps", [P, TT]), sb("rstd", [P, TT])
    w.xT = [t[:, :] for t in m.xnT]
    if rms:
        w.xT = [m.turned[:, 0, N * u:N * u + N] for u in range(2)]
        w.xk = [m.turned[:, 1, N * u:N * u + N].rearrange("p (k c) -> p k c", k=TT) for u in range(2)]
        w.sq, w.sq2, w.r2 = sb("sq", [P, TT]), sb("sq2", [P, TT]), sb("r2", [P, TT])
        w.b2s = sb("b2s", [1, first, P])
        w.g = sb("g", [P, 2])
    else:
        w.router_b = sb("router_b", [P, TT, K])
    return w


def layer3(nc, ctx, load, m):
    w = moe_weights(nc, ctx, load, m, "l3", 8, CAPACITY, sigmoid=False, rms=False, relu=True)
    load(w.b1[:, :, :], "L3_ffn_b1")
    load(w.router[:, :], "L3_ffn_gate_wT")
    load(w.b2[:, :], "L3_ffn_b2")
    for k in range(TT):
        load(w.router_b[:, k, :], "L3_ffn_gate_b", every=True)
    w.w = {}
    for key, src in (("A", "L3_attn_W_qT"), ("Ar", "L3_attn_W_qTs"), ("B", "L3_attn_W_kT"), ("Br", "L3_attn_W_kTs"),
                     ("V", "L3_attn_W_vT"), ("O", "L3_attn_W_oT")):
        t = ctx.enter_context(nc.sbuf_tensor(f"l3_{key}", [P, P], F32))
        load(t[:, :], src)
        w.w[key] = t[:, :]
    return w


def layer2(nc, ctx, load, m):
    w = moe_weights(nc, ctx, load, m, "l2", 10, None, sigmoid=True, rms=True, relu=False)

    def sb(name, shape, dt=F32):
        return ctx.enter_context(nc.sbuf_tensor(f"l2_{name}", shape, dt))
    load(w.W1[:, 0:2, :], "L2_ffn_W1_s")
    load(w.W1[:, 2:10, :], "L2_ffn_W1_r")
    load(w.W2[:, 0:2, :, :], "L2_ffn_W2_s")
    load(w.W2[:, 2:10, :, :], "L2_ffn_W2_r")
    load(w.b1[:, 0:2, :], "L2_ffn_b1_s")
    load(w.b1[:, 2:10, :], "L2_ffn_b1_r")
    load(w.router[:, :], "L2_ffn_centroids")
    load(w.b2[:, :], "L2_ffn_b2_r")
    load(w.b2s[:, :, :].rearrange("a e n -> a (e n)"), "L2_ffn_b2_s", row=True)
    load(w.g[:, 0:1], "L2_ffn_g_shared", col=True)
    load(w.g[:, 1:2], "L2_ffn_g_routed", col=True)
    w.dq = m.prob[0:32, 4, 0:128]
    w.uqT = m.prob[0:32, 4, 128:256]
    w.dkv = m.prob[0:32, 4, 256:384]
    w.uk = m.prob[:, 5, 128:160]
    w.uv = m.prob[:, 5, 160:192]
    w.oT = m.prob[:, 5, 192:320]
    load(w.dq[:, :], "L2_attn_W_dq")
    load(w.uqT[:, :], "L2_attn_W_uqT")
    load(w.dkv[:, :], "L2_attn_W_dkv")
    load(w.uk[:, :], "L2_attn_W_uk")
    load(w.uv[:, :], "L2_attn_W_uv")
    load(w.oT[:, :], "L2_attn_W_oT")
    w.qT = m.prob[:, 5, 320:448]
    w.keffT = m.prob[0:32, 4, 384:512]
    w.veff = m.prob[0:32, 5, 0:128]
    w.w = {k: sb(k, [P, P]) for k in "ABV"}
    w.w = {k: t[:, :] for k, t in w.w.items()}
    return w


def layer2_weights(nc, ctx, m, w):
    def sem(name):
        return ctx.enter_context(nc.semaphore(f"l2w_{name}"))
    s_pe, s_dve = sem("pe"), sem("dve")
    with nc.Block() as block:
        @block.tensor
        def _(pe):
            pe.matmul(m.S[0][:, 0:P], w.dq[:, :], w.uqT[:, :], start=True, stop=True).then_inc(s_pe, 1)
            pe.matmul(m.S[1][:, 0:P], w.uqT[:, :], w.dq[:, :], start=True, stop=True).then_inc(s_pe, 1)
            pe.matmul(m.T[0][0:32, 0:P], w.uv[:, :], w.oT[:, :], start=True, stop=True).then_inc(s_pe, 1)
            pe.wait_ge(s_dve, 3)
            pe.matmul(m.T[1][0:32, 0:P], w.uk[:, :], w.qT[:, :], start=True, stop=True).then_inc(s_pe, 1)
            pe.matmul(m.F[0][:, 0:P], w.dkv[:, :], w.veff[:, :], start=True, stop=True).then_inc(s_pe, 1)
            pe.wait_ge(s_dve, 4)
            pe.matmul(m.F[1][:, 0:P], w.dkv[:, :], w.keffT[:, :], start=True, stop=True).then_inc(s_pe, 1)

        @block.vector
        def _(dve):
            moves = [(w.w["A"], m.S[0][:, 0:P]), (w.qT[:, :], m.S[1][:, 0:P]), (w.veff[:, :], m.T[0][0:32, 0:P]),
                     (w.keffT[:, :], m.T[1][0:32, 0:P]), (w.w["V"], m.F[0][:, 0:P]), (w.w["B"], m.F[1][:, 0:P])]
            for i, (dst, src) in enumerate(moves):
                dve.wait_ge(s_pe, i + 1)
                dve.tensor_scalar(dst, src, 0.5 if i == 4 else 1.0, None, ALU.mult).then_inc(s_dve, 1)
            dve.tensor_scalar(w.W1[:, 0:2, :], w.W1[:, 0:2, :], w.g[:, 0:1], None, ALU.mult)
            dve.tensor_scalar(w.W1[:, 2:10, :], w.W1[:, 2:10, :], w.g[:, 1:2], None, ALU.mult)


def build(nc, args, layers):
    ctx = ExitStack()
    with ctx:
        m = Memory(nc, ctx)
        pending = []

        def load(dst, name, col=False, row=False, every=False, chunks=None):
            src = args[name]
            if every:
                src = src.rearrange("(a p) -> a p", a=1).broadcast_to([P, src.shape[0]])
            if col:
                src = src.rearrange("(p a) -> p a", a=1)
            if row:
                src = src.rearrange("(a p) -> a p", a=1)
            if chunks:
                src = src.rearrange("(c p) n -> p c n", c=chunks)
            pending.append((dst, src))

        load(m.ident[:, :], "const_ident")
        load(m.tri[:, :, :], "const_tri")
        load(m.cossin[:, :], "const_cossin")
        load(m.upto[:, :], "const_upto")
        load(m.rank[:, :, :], "const_rank")
        load(m.X[:, :, :], "x_tiles")
        w0 = layer0(nc, ctx, load, m)
        w2 = layer2(nc, ctx, load, m)
        w1 = layer1(nc, ctx, load, m, w2)
        w3 = layer3(nc, ctx, load, m)
        s_load = ctx.enter_context(nc.semaphore("s_load"))
        s_prep = ctx.enter_context(nc.semaphore("s_prep"))
        s_bias = ctx.enter_context(nc.semaphore("s_bias"))
        s_l3 = ctx.enter_context(nc.semaphore("l3_weights"))

        def l3_weights(eng):
            eng.dma_start(w3.W1, args["L3_ffn_W1"]).then_inc(s_l3, 16)
            eng.dma_start(w3.W2, args["L3_ffn_W2"]).then_inc(s_l3, 16)

        with nc.Block() as block:
            @block.sync
            def _(sp):
                for dst, src in pending:
                    sp.dma_start(dst, src).then_inc(s_load, 16)

            @block.tensor
            def _(pe):
                pe.wait_ge(s_load, 16 * len(pending))
                pe.matmul(m.M[0:1, 0:P], w0.bv[:, :], w0.w["O"], start=True, stop=True).then_inc(s_bias, 1)

            @block.vector
            def _(dve):
                dve.wait_ge(s_load, 16 * len(pending))
                dve.tensor_scalar(w0.gate_up[:, :, :], w0.ints[:, 0:2, :], float(np.float32(1 / 127.0)), None, ALU.mult)
                dve.tensor_scalar(w0.down[:, :, :].rearrange("p c n -> p (c n)"), w0.ints[:, 2, :],
                                  float(np.float32(1 / 127.0)), None, ALU.mult)
                dve.tensor_copy(m.ident_b[:, :], m.ident[:, :])
                for k in range(2):
                    for i in range(2):
                        dve.tensor_copy(m.tri2[:, k, i, :], m.tri[:, k, :])
                dve.memset(m.ones[:, :], 1.0)
                dve.memset(m.minus_half[:, :], -0.5)
                dve.memset(w3.counts[:, :], 0.0)
                for u in range(2):
                    for o in range(2):
                        dve.memset(m.stack[o][u][:, :, :].rearrange("p h n -> p (h n)").bitcast(U32), 0)
                    dve.memset(m.vaug[u][:, :, :, :].rearrange("p a b c -> p (a b c)"), 0.0).then_inc(s_prep, 1)
                dve.wait_ge(s_prep, 2)
                for u in range(2):
                    dve.memset(m.stack[1][u][SHIFT_ROW:SHIFT_ROW + 2, :, :].rearrange("p h n -> p (h n)"), 1.0)
                    dve.memset(m.vaug[u][:, :, :, HD:HD + 1], 1.0)
                dve.wait_ge(s_bias, 1)
                dve.tensor_tensor(w0.bo2[:, :], m.M[0:1, 0:P], w0.bo[:, :], ALU.add).then_inc(s_prep, 1)
        layer1_weights(nc, ctx, m, w1)
        layer2_weights(nc, ctx, m, w2)
        if 0 in layers:
            attention_layer(nc, m, w0, "l0", causal=False, scale=float(1 / np.float32(np.sqrt(128))), bias=True,
                            rope=False, project=True, ffn=SwigluFfn(w0), store=args["out"] if layers[-1] == 0 else None)
        if 1 in layers:
            recurrent_layer(nc, m, w1, store=args["out"] if layers[-1] == 1 else None)
        if 2 in layers:
            moe_layer(nc, m, w2, "l2f")
            attention_layer(nc, m, w2, "l2", causal=True, scale=float(1 / np.sqrt(np.float32(HD))), bias=False,
                            rope=False, project=False, ffn=Precomputed(), store=args["out"] if layers[-1] == 2 else None,
                            prefetch=l3_weights)
        if 3 in layers:
            with nc.Block() as block:
                @block.sync
                def _(sp):
                    if 2 not in layers:
                        l3_weights(sp)
                    sp.wait_ge(s_l3, 32)
            moe_layer(nc, m, w3, "l3f")
            attention_layer(nc, m, w3, "l3", causal=True, scale=float(1 / np.sqrt(np.float32(HD))), bias=False,
                            rope=True, project=True, ffn=Precomputed(), store=args["out"])


_HOST = {
    "L0_attn_WqT": ("L0_attn_Wq", "T"), "L0_attn_WkT": ("L0_attn_Wk", "T"), "L0_attn_WvT": ("L0_attn_Wv", "T"),
    "L0_attn_WoT": ("L0_attn_Wo", "T"), "L0_attn_bq": ("L0_attn_bq", ""), "L0_attn_bk": ("L0_attn_bk", ""),
    "L0_attn_bv": ("L0_attn_bv", ""), "L0_attn_bo": ("L0_attn_bo", ""),
    "L0_ffn_w_gateT": ("L0_ffn_w_gate", "T"), "L0_ffn_w_upT": ("L0_ffn_w_up", "T"),
    "L0_ffn_w_downT": ("L0_ffn_w_down", "T"),
    **{n: (n, "") for n in "L1_attn_Wz L1_attn_Wh L1_attn_bz L1_attn_bh L1_attn_log_D L1_ffn_enc_W L1_ffn_s2c_b "
       "L1_ffn_rW1 L1_ffn_rb1 L1_ffn_rW2 L1_ffn_rb2 L1_ffn_be2 L1_ffn_c2s_W L1_ffn_dec_b L1_ffn_ln_g "
       "L1_ffn_ln_b".split()},
    **{n: (n, "chunks") for n in ("L1_ffn_enc_b", "L1_ffn_c2s_b", "L1_ffn_s2c_W", "L1_ffn_dec_W")},
    "L1_ffn_We1": ("L1_ffn_We1", "W1"), "L1_ffn_We2": ("L1_ffn_We2", "W1"), "L1_ffn_be1T": ("L1_ffn_be1", "T"),
    "L2_attn_W_dq": ("L2_attn_W_dq", ""), "L2_attn_W_uqT": ("L2_attn_W_uq", "T"),
    "L2_attn_W_dkv": ("L2_attn_W_dkv", ""), "L2_attn_W_uk": ("L2_attn_W_uk", ""),
    "L2_attn_W_uv": ("L2_attn_W_uv", ""), "L2_attn_W_oT": ("L2_attn_W_o", "T"),
    "L2_ffn_centroids": ("L2_ffn_centroids", ""), "L2_ffn_b2_r": ("L2_ffn_b2_r", ""),
    "L2_ffn_b2_s": ("L2_ffn_b2_s", "flat"), "L2_ffn_g_shared": ("L2_ffn_g_shared", ""),
    "L2_ffn_g_routed": ("L2_ffn_g_routed", ""),
    "L2_ffn_W1_s": ("L2_ffn_W1_s", "W1"), "L2_ffn_W1_r": ("L2_ffn_W1_r", "W1"),
    "L2_ffn_W2_s": ("L2_ffn_W2_s", "W2"), "L2_ffn_W2_r": ("L2_ffn_W2_r", "W2"),
    "L2_ffn_b1_s": ("L2_ffn_b1_s", "b1"), "L2_ffn_b1_r": ("L2_ffn_b1_r", "b1"),
    "L3_ffn_W1": ("L3_ffn_W1", "W1"), "L3_ffn_W2": ("L3_ffn_W2", "W2"), "L3_ffn_b1": ("L3_ffn_b1", "b1"),
    "L3_ffn_b2": ("L3_ffn_b2", ""), "L3_ffn_gate_wT": ("L3_ffn_gate_w", "T"), "L3_ffn_gate_b": ("L3_ffn_gate_b", ""),
    "L3_attn_W_qT": ("L3_attn_W_q", "T"), "L3_attn_W_qTs": ("L3_attn_W_q", "swap"),
    "L3_attn_W_kT": ("L3_attn_W_k", "T"), "L3_attn_W_kTs": ("L3_attn_W_k", "swap"),
    "L3_attn_W_vT": ("L3_attn_W_v", "T"), "L3_attn_W_oT": ("L3_attn_W_o", "T"),
}


def laid_out(a, how):
    if how == "T":
        return a.T
    if how == "swap":
        return a.reshape(P // 2, 2, P)[:, ::-1].reshape(P, P).T
    if how == "W1":
        return a.transpose(1, 0, 2)
    if how == "W2":
        return a.reshape(a.shape[0], 4, P, D).transpose(2, 0, 1, 3)
    if how == "b1":
        return a.reshape(a.shape[0], 4, P).transpose(2, 0, 1)
    if how == "chunks":
        return np.moveaxis(a.reshape((2, P) + a.shape[1:]), 0, 1)
    return a.reshape(-1) if how == "flat" else a


def constants():
    f = np.arange(P)
    tri = np.stack([np.where(f[None, :] > f[:, None], MASKED, 0.0), np.where(f[:, None] > f[None, :], MASKED, 0.0)], 1)
    inv = np.float32(10000.0) ** (np.float32(-2.0) * np.arange(HD // 2, dtype=np.float32) / np.float32(HD))
    ang = np.arange(N, dtype=np.float32)[None, :] * inv.astype(np.float32)[(f % HD) // 2][:, None]
    sign = np.where(f % 2 == 0, -1.0, 1.0)[:, None]
    return {
        "const_ident": np.eye(P, dtype=np.float32),
        "const_upto": (f[:, None] <= f[None, :]).astype(np.float32),
        "const_rank": np.ascontiguousarray(np.broadcast_to(8.0 - np.arange(8, dtype=np.float32), (P, TT, 8))),
        "const_lap": sum(np.roll(np.eye(P, dtype=np.float32), i, 1) for i in (1, -1))
        - np.float32(2.0) * np.eye(P, dtype=np.float32),
        "const_tri": tri.astype(np.float32),
        "const_cossin": np.concatenate([np.cos(ang), sign * np.sin(ang)], 1).astype(np.float32),
    }


def host_arrays(inputs):
    arrays = dict(constants())
    x = np.asarray(inputs["L0_attn_x"]).reshape(B * TT, P, D)
    arrays["x_tiles"] = np.ascontiguousarray(x.transpose(1, 0, 2))
    for name, (src, how) in _HOST.items():
        a = np.asarray(inputs[src])
        arrays[name] = np.ascontiguousarray(laid_out(a, how))
    return arrays


LAYERS = (0, 1, 2, 3)


def kernel(**inputs):
    import concourse.bacc as bacc
    from concourse.bass_utils import run_bass_kernel_spmd

    nc = bacc.Bacc("TRN2", target_bir_lowering=False, num_devices=1)
    arrays = host_arrays(inputs)
    args = {k: nc.dram_tensor(k, a.shape, mybir.dt.from_np(a.dtype), kind="ExternalInput").ap()
            for k, a in arrays.items()}
    args["out"] = nc.dram_tensor("out", [P, B * TT, D], F32, kind="ExternalOutput").ap()
    build(nc, args, LAYERS)
    got = run_bass_kernel_spmd(nc, [arrays], core_ids=[0]).results[0]["out"]
    return np.ascontiguousarray(got.transpose(1, 0, 2)).reshape(B, N, D)
```

```python
from contextlib import ExitStack

import numpy as np
import concourse.bass as bass
from concourse import mybir

F32 = mybir.dt.float32
BF16 = mybir.dt.bfloat16
I32 = mybir.dt.int32
U32 = mybir.dt.uint32
ACT = mybir.ActivationFunctionType
ALU = mybir.AluOpType
AX = mybir.AxisListType

P = 128
B, N, D = 16, 256, 128
TT = N // P
HEADS, HD = 16, 8
GROUPS = HEADS // 4
SLOTS = 6
ROWS = SLOTS * HD
SHIFT_ROW = 64
SLICES = 8
SHIFT_SLICE = (6, 2)
PRING = 8
PART_RUNS = (((0, 0, 3, True), (3, 1, 2, True), (5, 2, 1, False)),
             ((0, 0, 3, False), (3, 0, 2, False), (5, 0, 1, False)))
MASKED = -1e30
CAPACITY = 320


class Steps:

    def __init__(self, sem, names, by=1):
        self.sem, self.names, self.by = sem, names.split() if isinstance(names, str) else names, by

    def at(self, b, name):
        return (b * len(self.names) + self.names.index(name) + 1) * self.by


def exists(b):
    return not isinstance(b, int) or b >= 0


class Body:

    def __init__(self, t, parity, inside, count=B):
        self.t, self.parity, self.inside, self.count = t, parity, inside, count

    def batch(self, ahead):
        b = self.t + ahead
        return b if self.inside or 0 <= b < self.count else None


FIRST_LOOPED = 2


def turns(eng, body, count=B, start=-2):
    loops = (count - 4) // 2
    for t in range(start, FIRST_LOOPED):
        body(Body(t, t % 2, False, count))
    with eng.Fori(0, loops) as i:
        body(Body(2 * i + FIRST_LOOPED, 0, True, count))
        body(Body(2 * i + FIRST_LOOPED + 1, 1, True, count))
    for t in range(FIRST_LOOPED + 2 * loops, count + 1):
        body(Body(t, t % 2, False, count))


class BankJobs:

    def __init__(self, ready, order, count=B):
        self.ready, self.order, self.count = ready, order, count
        self.names = [name for name, *_ in order]

    def freed(self, body, name):
        t, i = body.t, self.names.index(name)
        while True:
            i -= 1
            if i < 0:
                t, i = t - 1, len(self.order) - 1
            if isinstance(t, int) and t < -2:
                return None
            _, ahead, steps, step = self.order[i]
            if body.inside or 0 <= t + ahead < self.count:
                return steps.sem, steps.at(t + ahead, step)

    def filled(self, body, name):
        t, i = body.t, self.names.index(name)
        first = FIRST_LOOPED if body.inside else t
        n = sum(0 <= s + ahead < self.count for s in range(-2, first) for _, ahead, *_ in self.order)
        if body.inside:
            return n + (t - FIRST_LOOPED) * len(self.order) + i + 1
        return n + sum(0 <= t + ahead < self.count for _, ahead, *_ in self.order[:i + 1])


def own_wait(eng):
    eng.nop(nofuse=True)


def xtile(X, b, k=0, n=TT):
    return X[:, bass.ds(TT * b + k, n), :]


def attention_layer(nc, m, L, tag, causal, scale, bias, rope, project, ffn, store, prefetch=None):
    ctx = ExitStack()
    with ctx:
        def sem(name):
            return ctx.enter_context(nc.semaphore(f"{tag}_{name}"))

        W = 384 if causal else 512
        ln_dve = Steps(sem("ln_dve"), "stats0 stats1 mean0 mean1 xn0 xn1")
        ln_pool = Steps(sem("ln_pool"), "var rstd")
        xnT_act = Steps(sem("xnT_act"), "xnT")
        proj_act = Steps(sem("proj_act"), "rows cols" if bias else "both")
        proj_pe = Steps(sem("proj_pe"), "rows cols")
        rope_dve = Steps(sem("rope_dve"), "rows cols")
        rope_pool = Steps(sem("rope_pool"), "rows cols")
        split_act = Steps(sem("split_act"), "high middle")
        split_dve = Steps(sem("split_dve"), "rest low")
        parts_out = Steps(sem("parts_out"), "high middle low", 16 * 2)
        turn_new = 3
        shifts_after = 1 if rope else 2 if causal else 3
        split = turn_new + (2 if rope else 1)
        stacks_in = Steps(sem("stacks_in"), ["loaded"], 16 * sum(len(r) for r in PART_RUNS))
        v_act = Steps(sem("v_act"), "v")
        score_pe = Steps(sem("score_pe"), [f"h{h}" for h in range(HEADS)])
        max_dve = Steps(sem("max_dve"), [f"h{h}" for h in range(HEADS)])
        shift_act = Steps(sem("shift_act"), "half0 half1")
        shift_dve = Steps(sem("shift_dve"), "half0 half1")
        shift_in = [Steps(sem(f"shift_in{i}"), ["half"], 32) for i in range(2)]
        scoreT_pe = Steps(sem("scoreT_pe"), [f"h{h}" for h in range(HEADS)])
        exp_act = Steps(sem("exp_act"), [f"h{h}" for h in range(HEADS)])
        av_pe = Steps(sem("av_pe"), [f"g{g}" for g in range(GROUPS)])
        av_act = Steps(sem("av_act"), [f"g{g}" for g in range(GROUPS)])
        norm_dve = Steps(sem("norm_dve"), "recip0 mul0 recip1 mul1")
        oT_act = Steps(sem("oT_act"), "oT")
        fin_dve = Steps(sem("fin_dve"), "gated")
        fin_pool = Steps(sem("fin_pool"), "x" if project else "gated x")
        out_sp = Steps(sem("out_sp"), ["stored"], 16)
        jobs = [("v", 1, v_act, "v"), ("turn0", -1, norm_dve, "mul0"), ("shift1", 0, shift_dve, "half1"),
                ("turn1", -1, norm_dve, "mul1"), ("xnT", 2, xnT_act, "xnT")]
        if not rope:
            jobs += [("proj", 2, proj_act, proj_act.names[-1])]
        if project:
            jobs += [("turnO", -1, oT_act, "oT")]
        jobs += [("shift0", 1, shift_dve, "half0")]
        if project:
            jobs += [("out", -1, fin_dve, "gated")]
        M = BankJobs(sem("m_ready"), jobs)
        F = ffn.open(nc, sem, m, xnT_act)

        block = ctx.enter_context(nc.Block())

        @block.sync
        def _(sp):
            if prefetch is not None:
                prefetch(sp)

            def send_shifts(b, u, half):
                sp.wait_ge(shift_dve.sem, shift_dve.at(b, f"half{half}"))
                hs = HEADS // 2 * half
                for r in range(2):
                    sp.dma_start(m.stack[0][u][SHIFT_ROW + r:SHIFT_ROW + r + 1, hs:hs + HEADS // 2, :],
                                 m.shift[half][:, r, :]).then_inc(shift_in[half].sem, 16)

            def body(t):
                b = t.batch(1)
                if b is not None:
                    u = (t.parity + 1) % 2
                    sp.wait_ge(parts_out.sem, parts_out.at(b, "low"))
                    if exists(b - 2):
                        sp.wait_ge(scoreT_pe.sem, scoreT_pe.at(b - 2, f"h{HEADS - 1}"))
                    for o, runs in enumerate(PART_RUNS):
                        for slot, part, n, same in runs:
                            src = m.parts_dram[u, o, part:part + (1 if same else n)]
                            if same:
                                src = src.broadcast_to([n, HD, HEADS * N])
                            sp.dma_start(m.stack[o][u][HD * slot:HD * (slot + n), :, :], src)\
                              .then_inc(stacks_in.sem, 16)
                b = t.batch(0)
                if b is not None:
                    send_shifts(b, t.parity, 1)
                b, nxt = t.batch(2), t.batch(1)
                for part, made, step in ((0, split_act, "high"), (1, split_act, "middle"), (2, split_dve, "low")):
                    if nxt is not None and part == shifts_after:
                        send_shifts(nxt, (t.parity + 1) % 2, 0)
                    if b is not None:
                        sp.wait_ge(made.sem, made.at(b, step))
                        for o in range(2):
                            sp.dma_start(m.parts_dram[t.parity, o, part].rearrange("d (h n) -> h d n", n=N),
                                         m.parts[:, part, o, :]).then_inc(parts_out.sem, 16)
                if nxt is not None and shifts_after == 3:
                    send_shifts(nxt, (t.parity + 1) % 2, 0)
                b = t.batch(-1)
                if store is not None and b is not None:
                    sp.wait_ge(fin_pool.sem, fin_pool.at(b, "x"))
                    sp.dma_start(store[:, bass.ds(TT * b, TT), :], xtile(m.X, b)).then_inc(out_sp.sem, 16)
            turns(sp, body)
            if store is not None:
                if exists(B - 1):
                    sp.wait_ge(out_sp.sem, out_sp.at(B - 1, "stored"))

        @block.tensor
        def _(pe):

            def score_mask(bank, tri):
                pe.matmul(bank[:, 0:384].rearrange("p (a c) -> p a c", a=3)[:, 0:3:2, :], m.ident_b[:, :],
                          m.tri2[:, tri, :, :],
                          start=True, stop=False, skip_group_check=True)

            def scores(t, b, u, h):
                if h == 0:
                    pe.wait_ge(stacks_in.sem, stacks_in.at(b, "loaded"))
                if h >= 2:
                    pe.wait_ge(max_dve.sem, max_dve.at(b, f"h{h - 2}"))
                else:
                    if exists(b - 1):
                        pe.wait_ge(max_dve.sem, max_dve.at(b - 1, f"h{HEADS - 2 + h}"))
                S, k = m.S[h % 2], SHIFT_ROW
                rows, cols = m.stack[0][u][0:k, h, :], m.stack[1][u][0:k, h, :]
                if causal:
                    score_mask(S, 0)
                    pe.matmul(S[:, 0:128], rows[:, 0:128], cols[:, 0:128], start=False, stop=False,
                              skip_group_check=True)
                    pe.matmul(S[:, 128:384], rows[:, 128:256], cols, start=False, stop=True,
                              skip_group_check=True).then_inc(score_pe.sem, 1)
                else:
                    pe.matmul(S[:, 0:256], rows[:, 0:128], cols, start=True, stop=True)
                    pe.matmul(S[:, 256:512], rows[:, 128:256], cols, start=True, stop=True)\
                      .then_inc(score_pe.sem, 1)

            def scoresT(t, b, u, h):
                if h % 8 == 0:
                    pe.wait_ge(shift_in[h // 8].sem, shift_in[h // 8].at(b, "half"))
                if h >= 2:
                    pe.wait_ge(exp_act.sem, exp_act.at(b, f"h{h - 2}"))
                else:
                    if exists(b - 1):
                        pe.wait_ge(exp_act.sem, exp_act.at(b - 1, f"h{HEADS - 2 + h}"))
                T = m.T[h % 2]
                rows, cols = m.stack[0][u][:, h, :], m.stack[1][u][:, h, :]
                if causal:
                    score_mask(T, 1)
                    pe.matmul(T[:, 0:256], cols[:, 0:128], rows, start=False, stop=False,
                              skip_group_check=True)
                    pe.matmul(T[:, 256:384], cols[:, 128:256], rows[:, 128:256], start=False, stop=True,
                              skip_group_check=True).then_inc(scoreT_pe.sem, 1)
                else:
                    pe.matmul(T[:, 0:256], cols[:, 0:128], rows, start=True, stop=True)
                    pe.matmul(T[:, 256:512], cols[:, 128:256], rows, start=True, stop=True)\
                      .then_inc(scoreT_pe.sem, 1)

            def values(t, b, u, g):
                pe.wait_ge(exp_act.sem, exp_act.at(b, f"h{4 * g + 3}"))
                if g == 0:
                    pe.wait_ge(v_act.sem, v_act.at(b, "v"))
                    if exists(b - 1):
                        pe.wait_ge(av_act.sem, av_act.at(b - 1, f"g{GROUPS - 1}"))
                else:
                    pe.wait_ge(av_act.sem, av_act.at(b, f"g{g - 1}"))
                c = N * (g % 2)
                for k in range(TT):
                    lo = P * k if causal else 0
                    for j in range(4):
                        h = 4 * g + j
                        p = m.prob[:, h % PRING, P * (2 * k):P * (2 * k) + N - lo]
                        mm = pe.matmul(m.O[32 * j:32 * j + 32, c + lo:c + N], m.vaug[u][:, k, h, :], p,
                                       start=(k == 0), stop=(k == TT - 1), skip_group_check=True)
                mm.then_inc(av_pe.sem, 1)

            def turn_back(t, b, u, k):
                if k == 0:
                    pe.wait_ge(av_act.sem, av_act.at(b, f"g{GROUPS - 1}"))
                free = M.freed(t, f"turn{k}")
                if free:
                    pe.wait_ge(*free)
                for g in range(GROUPS):
                    mm = pe.transpose(m.M[:, P * g:P * g + P], m.oTn[u][:, g, P * k:P * k + P], m.ident[:, :])
                mm.then_inc(M.ready, 1)

            def body(t):
                p = t.parity
                q = (p + 1) % 2
                prev, cur, nxt, new = (t.batch(a) for a in (-1, 0, 1, 2))
                for s in range(SLICES):
                    if cur is not None:
                        scoresT(t, cur, p, 2 * s)
                        scoresT(t, cur, p, 2 * s + 1)
                    for b, half in ((cur, 1), (nxt, 0)):
                        if b is None or s != SHIFT_SLICE[half]:
                            continue
                        hs = HEADS // 2 * half
                        pe.wait_ge(max_dve.sem, max_dve.at(b, f"h{hs + HEADS // 2 - 1}"))
                        free = M.freed(t, f"shift{half}")
                        if free:
                            pe.wait_ge(*free)
                        for k in range(TT):
                            mm = pe.transpose(m.M[0:8, P * k:P * k + P], m.rowmax[:, k, hs:hs + 8], m.ident[:, :])
                        mm.then_inc(M.ready, 1)
                    if nxt is not None:
                        F.tensor(pe, nxt, q, s)
                    for b, u, pair in ((cur, p, s + 6), (nxt, q, s - 2)):
                        if b is not None and 0 <= pair < HEADS // 2:
                            scores(t, b, u, 2 * pair)
                            scores(t, b, u, 2 * pair + 1)
                    if s == 0 and prev is not None:
                        values(t, prev, q, 3)
                    if s in (2, 4, 6) and cur is not None:
                        values(t, cur, p, s // 2 - 1)
                    if s == 0 and nxt is not None:
                        free = M.freed(t, "v")
                        if free:
                            pe.wait_ge(*free)
                        pe.wait_ge(xnT_act.sem, xnT_act.at(nxt, "xnT"))
                        for k in range(TT):
                            mm = pe.matmul(m.M[:, P * k:P * k + P], m.xnT[q][:, P * k:P * k + P], L.w["V"],
                                           start=True, stop=True)
                        mm.then_inc(M.ready, 1)
                    if s == 1 and prev is not None:
                        turn_back(t, prev, q, 0)
                    if s == 2 and prev is not None:
                        turn_back(t, prev, q, 1)
                    if s == turn_new and new is not None:
                        pe.wait_ge(ln_dve.sem, ln_dve.at(new, "xn1"))
                        free = M.freed(t, "xnT")
                        if free:
                            pe.wait_ge(*free)
                        for k in range(TT):
                            mm = pe.transpose(m.M[:, P * k:P * k + P], m.xn[:, k, :], m.ident[:, :])
                        mm.then_inc(M.ready, 1)
                    if s == turn_new + 1 and new is not None:
                        pe.wait_ge(xnT_act.sem, xnT_act.at(new, "xnT"))
                        if rope:
                            for i, W in enumerate(("A", "B")):
                                if exists(new - 1):
                                    pe.wait_ge(rope_dve.sem, rope_dve.at(new - 1, rope_dve.names[i]))
                                pe.matmul(m.F[i][:, 0:N], L.w[W], m.xnT[p][:, :], start=True, stop=True)
                                pe.matmul(m.F[i][:, N:2 * N], L.w[W + "r"], m.xnT[p][:, :], start=True, stop=True)\
                                  .then_inc(proj_pe.sem, 1)
                        else:
                            free = M.freed(t, "proj")
                            if free:
                                pe.wait_ge(*free)
                            pe.matmul(m.M[:, 0:N], L.w["A"], m.xnT[p][:, :], start=True, stop=True)
                            pe.matmul(m.M[:, N:2 * N], L.w["B"], m.xnT[p][:, :], start=True, stop=True)\
                              .then_inc(M.ready, 1)
                    if s == 5 and prev is not None and project:
                        pe.wait_ge(norm_dve.sem, norm_dve.at(prev, "mul1"))
                        free = M.freed(t, "turnO")
                        if free:
                            pe.wait_ge(*free)
                        for k in range(TT):
                            mm = pe.transpose(m.M[:, P * k:P * k + P], m.o[:, k, :], m.ident[:, :])
                        mm.then_inc(M.ready, 1)
                    if s == 7 and prev is not None and project:
                        pe.wait_ge(oT_act.sem, oT_act.at(prev, "oT"))
                        free = M.freed(t, "out")
                        if free:
                            pe.wait_ge(*free)
                        for k in range(TT):
                            mm = pe.matmul(m.M[:, P * k:P * k + P], m.oT[:, P * k:P * k + P], L.w["O"],
                                           start=True, stop=not bias)
                            if bias:
                                mm = pe.matmul(m.M[:, P * k:P * k + P], m.ones[0:1, 0:P], L.w["bo"],
                                               start=False, stop=True)
                        mm.then_inc(M.ready, 1)
            turns(pe, body)

        @block.scalar
        def _(act):

            def body(t):
                p = t.parity
                q = (p + 1) % 2
                prev, cur, nxt, new = (t.batch(a) for a in (-1, 0, 1, 2))

                def copy_values(b, u, g):
                    act.wait_ge(av_pe.sem, av_pe.at(b, f"g{g}"))
                    if g == 0:
                        if exists(b - 2):
                            act.wait_ge(norm_dve.sem, norm_dve.at(b - 2, "mul1"))
                    c = N * (g % 2)
                    act.activation(m.oTn[u][:, g, :], m.O[:, c:c + N], ACT.Copy).then_inc(av_act.sem, 1)

                for s in range(SLICES):
                    if cur is not None:
                        for h in (2 * s, 2 * s + 1):
                            act.wait_ge(scoreT_pe.sem, scoreT_pe.at(cur, f"h{h}"))
                            if h >= PRING:
                                act.wait_ge(av_pe.sem, av_pe.at(cur, f"g{(h - PRING) // 4}"))
                            else:
                                if exists(cur - 1):
                                    act.wait_ge(av_pe.sem, av_pe.at(cur - 1, f"g{(h + PRING) // 4}"))
                            act.activation(m.prob[:, h % PRING, 0:W], m.T[h % 2][:, 0:W], ACT.Exp, scale=scale)\
                               .then_inc(exp_act.sem, 1)
                    for b, half in ((cur, 1), (nxt, 0)):
                        if b is None or s != SHIFT_SLICE[half]:
                            continue
                        act.wait_ge(M.ready, M.filled(t, f"shift{half}"))
                        if exists(b - 1):
                            act.wait_ge(shift_in[half].sem, shift_in[half].at(b - 1, "half"))
                        act.activation(m.shift[half][:, 0, :], m.M[0:8, 0:N], ACT.Copy, scale=-1.0)\
                           .then_inc(shift_act.sem, 1)
                    if s == 0 and prev is not None:
                        copy_values(prev, q, 3)
                    if s in (2, 4, 6) and cur is not None:
                        copy_values(cur, p, s // 2 - 1)
                    if nxt is not None:
                        F.scalar(act, nxt, q, s)
                    if s == 0 and nxt is not None:
                        act.wait_ge(M.ready, M.filled(t, "v"))
                        if exists(nxt - 2):
                            act.wait_ge(av_pe.sem, av_pe.at(nxt - 2, f"g{GROUPS - 1}"))
                        for k in range(TT):
                            a = act.activation(m.vaug[q][:, k, :, 0:HD],
                                               m.M[:, P * k:P * k + P].rearrange("p (h d) -> p h d", d=HD), ACT.Copy)
                        a.then_inc(v_act.sem, 1)
                    if s == turn_new and new is not None:
                        act.wait_ge(M.ready, M.filled(t, "xnT"))
                        act.activation(m.xnT[p][:, :], m.M[:, 0:N], ACT.Copy).then_inc(xnT_act.sem, 1)
                    if s == turn_new + 1 and new is not None and not rope:
                        act.wait_ge(M.ready, M.filled(t, "proj"))
                        if exists(new - 1):
                            act.wait_ge(split_dve.sem, split_dve.at(new - 1, "rest"))
                        if bias:
                            act.activation(m.rc[:, 0:N], m.M[:, 0:N], ACT.Identity, bias=L.w["bA"])\
                               .then_inc(proj_act.sem, 1)
                            act.activation(m.rc[:, N:2 * N], m.M[:, N:2 * N], ACT.Identity, bias=L.w["bB"])\
                               .then_inc(proj_act.sem, 1)
                        else:
                            act.activation(m.rc[:, :], m.M[:, :], ACT.Copy).then_inc(proj_act.sem, 1)
                    if s == 5 and prev is not None and project:
                        act.wait_ge(M.ready, M.filled(t, "turnO"))
                        act.activation(m.oT[:, :], m.M[:, 0:N], ACT.Copy).then_inc(oT_act.sem, 1)
                    if s == split and new is not None:
                        ready = rope_pool if rope else proj_act
                        act.wait_ge(ready.sem, ready.at(new, ready.names[-1]))
                        if exists(new - 1):
                            act.wait_ge(parts_out.sem, parts_out.at(new - 1, "high"))
                        act.activation(m.parts[:, 0, :, :], m.rc[:, :].rearrange("p (o n) -> p o n", o=2), ACT.Copy)\
                           .then_inc(split_act.sem, 1)
                    if s == split + 1 and new is not None:
                        act.wait_ge(split_dve.sem, split_dve.at(new, "rest"))
                        if exists(new - 1):
                            act.wait_ge(parts_out.sem, parts_out.at(new - 1, "middle"))
                        act.activation(m.parts[:, 1, :, :], m.rest[:, :, :], ACT.Copy).then_inc(split_act.sem, 1)
            turns(act, body)

        @block.vector
        def _(dve):

            def body(t):
                p = t.parity
                q = (p + 1) % 2
                prev, cur, nxt, new = (t.batch(a) for a in (-1, 0, 1, 2))
                for s in range(SLICES):
                    if s == split + 1 and new is not None:
                        dve.wait_ge(split_act.sem, split_act.at(new, "high"))
                        if exists(new - 1):
                            dve.wait_ge(split_dve.sem, split_dve.at(new - 1, "low"))
                        dve.tensor_tensor(m.rest[:, :, :], m.rc[:, :].rearrange("p (o n) -> p o n", o=2),
                                          m.parts[:, 0, :, :], ALU.subtract).then_inc(split_dve.sem, 1)
                    if s == split + 2 and new is not None:
                        dve.wait_ge(split_act.sem, split_act.at(new, "middle"))
                        if exists(new - 1):
                            dve.wait_ge(parts_out.sem, parts_out.at(new - 1, "low"))
                        dve.tensor_tensor(m.parts[:, 2, :, :], m.rest[:, :, :], m.parts[:, 1, :, :], ALU.subtract)\
                           .then_inc(split_dve.sem, 1)
                    if s == 0 and new is not None:
                        if exists(new - 1):
                            dve.wait_ge(ln_pool.sem, ln_pool.at(new - 1, "rstd"))
                        for k in range(TT):
                            dve.bn_stats(m.stats[:, k, :], xtile(m.X, new, k, 1)).then_inc(ln_dve.sem, 1)
                        for k in range(TT):
                            dve.wait_ge(ln_dve.sem, ln_dve.at(new, f"stats{k}"))
                            own_wait(dve)
                            dve.bn_aggr(m.mean_var[:, k, :], m.stats[:, k, :]).then_inc(ln_dve.sem, 1)
                    if s == 1 and new is not None:
                        dve.wait_ge(ln_pool.sem, ln_pool.at(new, "rstd"))
                        if exists(new - 1):
                            dve.wait_ge(xnT_act.sem, xnT_act.at(new - 1, "xnT"))
                        for k in range(TT):
                            dve.tensor_scalar(m.xn[:, k, :], xtile(m.X, new, k, 1), m.mean_var[:, k, 0:1],
                                              m.rstd[:, k:k + 1], ALU.subtract, ALU.mult).then_inc(ln_dve.sem, 1)
                    for b, half in ((cur, 1), (nxt, 0)):
                        if b is None or s != SHIFT_SLICE[half]:
                            continue
                        dve.wait_ge(shift_act.sem, shift_act.at(b, f"half{half}"))
                        dve.scalar_tensor_tensor(m.shift[half][:, 1, :], m.M[0:8, 0:N], -1.0, m.shift[half][:, 0, :],
                                                 ALU.mult, ALU.subtract).then_inc(shift_dve.sem, 1)
                    for b, pair in ((cur, s + 6), (nxt, s - 2)):
                        if b is None or not 0 <= pair < HEADS // 2:
                            continue
                        for h in (2 * pair, 2 * pair + 1):
                            dve.wait_ge(score_pe.sem, score_pe.at(b, f"h{h}"))
                            if h % 8 == 0:
                                if exists(b - 1):
                                    dve.wait_ge(shift_dve.sem, shift_dve.at(b - 1, f"half{h // 8}"))
                            S = m.S[h % 2]
                            if causal:
                                dve.tensor_reduce(m.rowmax[:, 0, h:h + 1], S[:, 0:128], AX.X, ALU.max)
                                r = dve.tensor_reduce(m.rowmax[:, 1, h:h + 1], S[:, 128:384], AX.X, ALU.max)
                            else:
                                r = dve.tensor_reduce(m.rowmax[:, :, h:h + 1],
                                                      S[:, :].rearrange("p (k c) -> p k c", k=TT), AX.X, ALU.max)
                            r.then_inc(max_dve.sem, 1)
                    if nxt is not None:
                        F.vector(dve, nxt, q, s)
                    if s in (1, 2) and prev is not None:
                        k = s - 1
                        dve.wait_ge(M.ready, M.filled(t, f"turn{k}"))
                        if k == 0:
                            if exists(prev - 1) and project:
                                dve.wait_ge(oT_act.sem, oT_act.at(prev - 1, "oT"))
                            elif exists(prev - 1):
                                dve.wait_ge(fin_pool.sem, fin_pool.at(prev - 1, "gated"))
                        heads = m.M[:, :].rearrange("p (h w) -> p h w", w=32)
                        dve.reciprocal(m.rsum[:, k, :].unsqueeze(2), heads[:, :, HD:HD + 1]).then_inc(norm_dve.sem, 1)
                        dve.wait_ge(norm_dve.sem, norm_dve.at(prev, f"recip{k}"))
                        dve.tensor_tensor(m.o[:, k, :].rearrange("p (h d) -> p h d", d=HD), heads[:, :, 0:HD],
                                          m.rsum[:, k, :].unsqueeze(2).broadcast_to([P, HEADS, HD]), ALU.mult)\
                           .then_inc(norm_dve.sem, 1)
                    if s == turn_new + 1 and new is not None and rope:
                        for i in range(2):
                            dve.wait_ge(proj_pe.sem, proj_pe.at(new, proj_pe.names[i]))
                            if exists(new - 1):
                                dve.wait_ge(rope_pool.sem, rope_pool.at(new - 1, rope_pool.names[i]))
                            dve.tensor_tensor(m.turned[:, i, :], m.F[i][:, :], m.cossin[:, :], ALU.mult)\
                               .then_inc(rope_dve.sem, 1)
                    if s == 7 and prev is not None and project:
                        dve.wait_ge(M.ready, M.filled(t, "out"))
                        if exists(prev - 1):
                            dve.wait_ge(fin_pool.sem, fin_pool.at(prev - 1, "x"))
                        F.gate_ready(dve, prev)
                        dve.scalar_tensor_tensor(m.gated[:, :, :], m.M[:, 0:N].rearrange("p (k c) -> p k c", k=TT),
                                                 0.5, F.gate(prev, q), ALU.mult, ALU.mult)\
                           .then_inc(fin_dve.sem, 1)
            turns(dve, body)

        @block.gpsimd
        def _(pool):

            def body(t):
                prev, cur, nxt, new = (t.batch(a) for a in (-1, 0, 1, 2))
                if new is not None:
                    pool.wait_ge(ln_dve.sem, ln_dve.at(new, "mean1"))
                    own_wait(pool)
                    pool.tensor_scalar(m.var_eps[:, :], m.mean_var[:, :, 1], 1e-5, None, ALU.add)\
                        .then_inc(ln_pool.sem, 1)
                    pool.wait_ge(ln_pool.sem, ln_pool.at(new, "var"))
                    pool.tensor_tensor(m.rstd[:, :], m.var_eps[:, :], m.minus_half[:, 0:TT], ALU.pow)\
                        .then_inc(ln_pool.sem, 1)
                F.gpsimd(pool, nxt, (t.parity + 1) % 2)
                if new is not None and rope:
                    for i in range(2):
                        pool.wait_ge(rope_dve.sem, rope_dve.at(new, rope_dve.names[i]))
                        if i == 0 and exists(new - 1):
                            pool.wait_ge(split_dve.sem, split_dve.at(new - 1, "rest"))
                        pool.tensor_tensor(m.rc[:, N * i:N * i + N], m.turned[:, i, 0:N], m.turned[:, i, N:2 * N],
                                           ALU.add).then_inc(rope_pool.sem, 1)
                if prev is not None:
                    X = xtile(m.X, prev)
                    if project:
                        pool.wait_ge(fin_dve.sem, fin_dve.at(prev, "gated"))
                    else:
                        pool.wait_ge(norm_dve.sem, norm_dve.at(prev, "mul1"))
                        F.gate_ready(pool, prev)
                        if exists(prev - 1):
                            pool.wait_ge(fin_pool.sem, fin_pool.at(prev - 1, "x"))
                        pool.tensor_tensor(m.gated[:, :, :], m.o[:, :, :], F.gate(prev, (t.parity + 1) % 2), ALU.mult)\
                            .then_inc(fin_pool.sem, 1)
                        pool.wait_ge(fin_pool.sem, fin_pool.at(prev, "gated"))
                    pool.tensor_tensor(X, X, m.gated[:, :, :], ALU.add).then_inc(fin_pool.sem, 1)
            turns(pool, body)


def moe_layer(nc, m, w, tag):
    ctx = ExitStack()
    with ctx:
        def sem(name):
            return ctx.enter_context(nc.semaphore(f"{tag}_{name}"))

        E, K = w.experts, 8
        first = E - K
        ln_dve = Steps(sem("ln_dve"), "stats0 stats1 mean0 mean1 xn0 xn1 xr0 xr1")
        ln_pool = Steps(sem("ln_pool"), "var rstd sq mean2 meps r2")
        xT_act = Steps(sem("xT_act"), "xnT xrT")
        route_act = Steps(sem("route_act"), "act gT")
        route_dve = Steps(sem("route_dve"), "v vsum vrec max1 eq1 key1 top1 one1 less max2 eq2 key2 top2 one2 "
                          "onehots gates weight")
        in_pe = Steps(sem("in_pe"), [f"e{e}c{c}" for e in range(E) for c in range(2)])
        hid_act = Steps(sem("hid_act"), [f"e{e}c{c}" for e in range(E) for c in range(2)])
        outs = ["base"] + [f"e{e}" for e in range(first, E)]
        out_pe = Steps(sem("out_pe"), outs)
        acc_dve = Steps(sem("acc_dve"), ["base"] + [f"e{e}" for e in range(first, E)] + ["gate"])
        tanh_act = Steps(sem("tanh_act"), "tanh")
        M = BankJobs(sem("m_ready"), [("xnT", 1, xT_act, "xnT"), ("xrT", 1, xT_act, "xrT"),
                                      ("logit", 1, route_act, "act"), ("gT", 1, route_act, "gT")])
        IN = [m.S[0], m.S[1], m.T[0], m.T[1]]
        HR = 4

        def hidden_done(eng, b, e, c):
            if exists(b):
                eng.wait_ge(hid_act.sem, hid_act.at(b, f"e{e}c{c}"))

        def hid_free(eng, b, e):
            x = e - HR
            bb, x = (b, x) if x >= 0 else (b - 1, max(y for y in range(E) if y % HR == e % HR))
            if exists(bb):
                eng.wait_ge(out_pe.sem, out_pe.at(bb, "base" if x < first else f"e{x}"))

        block = ctx.enter_context(nc.Block())

        @block.tensor
        def _(pe):
            def experts_in(b, u, e):
                if e == 0:
                    pe.wait_ge(xT_act.sem, xT_act.at(b, xT_act.names[-1]))
                for c in range(2):
                    hidden_done(pe, b if e >= 2 else b - 1, (e - 2) % E, c)
                    bank = IN[(2 * e + c) % 4]
                    for i in range(2):
                        mm = pe.matmul(bank[:, N * i:N * i + N], w.W1[:, e, P * (2 * c + i):P * (2 * c + i) + P],
                                       w.xT[u], start=True, stop=True)
                    mm.then_inc(in_pe.sem, 1)

            def products_out(bank, e, start, stop):
                for k in range(TT):
                    for c in range(4):
                        mm = pe.matmul(bank[:, P * k:P * k + P], w.hT[e % HR][:, c, P * k:P * k + P],
                                       w.W2[:, e, c, :], start=(start and c == 0), stop=(stop and c == 3),
                                       skip_group_check=True)
                return mm

            def experts_out(b, u, i):
                prev = i - 2
                if exists(b if prev >= 0 else b - 1):
                    pe.wait_ge(acc_dve.sem, acc_dve.at(b if prev >= 0 else b - 1, (["base"] + [f"e{e}" for e in range(first, E)])[prev]))
                bank = m.F[(i + u) % 2]
                if i == 0:
                    pe.wait_ge(route_act.sem, route_act.at(b, "gT"))
                    for k in range(TT):
                        mm = pe.matmul(bank[:, P * k:P * k + P], w.gT[u][:, P * k:P * k + P], w.b2[:, :],
                                       start=True, stop=False, skip_group_check=True)
                        for e in range(first):
                            mm = pe.matmul(bank[:, P * k:P * k + P], m.ones[0:1, 0:P], w.b2s[:, e, :],
                                           start=False, stop=False, skip_group_check=True)
                        if k == 0:
                            hidden_done(pe, b, first - 1, 1)
                        for e in range(first):
                            for c in range(4):
                                mm = pe.matmul(bank[:, P * k:P * k + P], w.hT[e % HR][:, c, P * k:P * k + P],
                                               w.W2[:, e, c, :], start=False, stop=(e == first - 1 and c == 3),
                                               skip_group_check=True)
                else:
                    e = first + i - 1
                    hidden_done(pe, b, e, 1)
                    mm = products_out(bank, e, True, True)
                mm.then_inc(out_pe.sem, 1)

            def misc(t, b, u, i):
                if i == 0:
                    pe.wait_ge(ln_dve.sem, ln_dve.at(b, "xn1"))
                    free = M.freed(t, "xnT")
                    if free:
                        pe.wait_ge(*free)
                    for k in range(TT):
                        mm = pe.transpose(m.M[:, P * k:P * k + P], m.xn[:, k, :], m.ident[:, :])
                    mm.then_inc(M.ready, 1)
                if i == 1:
                    pe.wait_ge(ln_dve.sem, ln_dve.at(b, "xr1"))
                    free = M.freed(t, "xrT")
                    if free:
                        pe.wait_ge(*free)
                    for k in range(TT):
                        mm = pe.transpose(m.M[:, P * k:P * k + P], w.xr[:, k, :], m.ident[:, :])
                    mm.then_inc(M.ready, 1)
                if i == 2:
                    free = M.freed(t, "logit")
                    if free:
                        pe.wait_ge(*free)
                    for k in range(TT):
                        mm = pe.matmul(m.M[:, K * k:K * k + K], m.xnT[u][:, P * k:P * k + P], w.router[:, :],
                                       start=True, stop=True)
                    mm.then_inc(M.ready, 1)
                if i == 3:
                    pe.wait_ge(route_dve.sem, route_dve.at(b, "weight"))
                    free = M.freed(t, "gT")
                    if free:
                        pe.wait_ge(*free)
                    for k in range(TT):
                        mm = pe.transpose(m.M[0:K, P * k:P * k + P], w.weight[u][:, k, :], m.ident[:, :])
                    mm.then_inc(M.ready, 1)

            def body(t):
                cur, nxt = t.batch(0), t.batch(1)
                u = t.parity
                for e in range(E + 2):
                    if cur is not None:
                        if e < E:
                            experts_in(cur, u, e)
                        i = e - first - 1
                        if 0 <= i <= K:
                            experts_out(cur, u, i)
                    if nxt is not None and e in (3, 5, 6, 10):
                        misc(t, nxt, 1 - u, (3, 5, 6, 10).index(e))
            turns(pe, body)

        @block.scalar
        def _(act):
            def body(t):
                cur, nxt = t.batch(0), t.batch(1)
                u = t.parity
                for e in range(E + 2):
                    if cur is not None and e < E:
                        for c in range(2):
                            act.wait_ge(in_pe.sem, in_pe.at(cur, f"e{e}c{c}"))
                            if c == 0:
                                hid_free(act, cur, e)
                            for i in range(2):
                                a = act.activation(w.hT[e % HR][:, 2 * c + i, :], IN[(2 * e + c) % 4][:, N * i:N * i + N],
                                                   ACT.Gelu, bias=w.b1[:, e, 2 * c + i:2 * c + i + 1])
                            a.then_inc(hid_act.sem, 1)
                    if nxt is not None:
                        if e == 4:
                            act.wait_ge(M.ready, M.filled(t, "xnT"))
                            act.activation(m.xnT[1 - u][:, :], m.M[:, 0:N], ACT.Copy).then_inc(xT_act.sem, 1)
                        if e == 6:
                            act.wait_ge(M.ready, M.filled(t, "xrT"))
                            act.activation(w.xT[1 - u], m.M[:, 0:N], ACT.Copy).then_inc(xT_act.sem, 1)
                        if e == 7:
                            act.wait_ge(M.ready, M.filled(t, "logit"))
                            if exists(nxt - 1):
                                act.wait_ge(route_dve.sem, route_dve.at(nxt - 1, "weight"))
                            act.activation(w.v0[:, :, :], m.M[:, 0:2 * K].rearrange("p (k e) -> p k e", k=TT),
                                           ACT.Tanh, scale=0.5).then_inc(route_act.sem, 1)
                        if e == 11:
                            act.wait_ge(M.ready, M.filled(t, "gT"))
                            act.activation(w.gT[1 - u][:, :], m.M[0:K, 0:N], ACT.Copy).then_inc(route_act.sem, 1)
                if cur is not None:
                    act.wait_ge(acc_dve.sem, acc_dve.at(cur, f"e{E - 1}"))
                    act.activation(w.th, w.acc, ACT.Tanh, scale=0.5).then_inc(tanh_act.sem, 1)

            turns(act, body)

        @block.vector
        def _(dve):
            def top(b, n):
                v = w.v if n == 1 else w.v2
                dve.tensor_reduce(w.mx[:, :, :], v[:, :, :], AX.X, ALU.max).then_inc(route_dve.sem, 1)
                dve.wait_ge(route_dve.sem, route_dve.at(b, f"max{n}"))
                dve.tensor_tensor(w.eq[:, :, :], v[:, :, :], w.mx[:, :, :].broadcast_to([P, TT, K]), ALU.is_ge)\
                   .then_inc(route_dve.sem, 1)
                dve.wait_ge(route_dve.sem, route_dve.at(b, f"eq{n}"))
                dve.tensor_tensor(w.eq[:, :, :], w.eq[:, :, :], m.rank[:, :, :], ALU.mult).then_inc(route_dve.sem, 1)
                dve.wait_ge(route_dve.sem, route_dve.at(b, f"key{n}"))
                dve.tensor_reduce(w.mx[:, :, :], w.eq[:, :, :], AX.X, ALU.max).then_inc(route_dve.sem, 1)
                dve.wait_ge(route_dve.sem, route_dve.at(b, f"top{n}"))
                dve.tensor_tensor(w.one[:, :, K * (n - 1):K * n], w.eq[:, :, :],
                                  w.mx[:, :, :].broadcast_to([P, TT, K]), ALU.is_equal).then_inc(route_dve.sem, 1)
                dve.wait_ge(route_dve.sem, route_dve.at(b, f"one{n}"))

            def body(t):
                cur, nxt = t.batch(0), t.batch(1)
                u = t.parity
                for e in range(E + 2):
                    i = e - first - 2
                    if cur is not None and 0 <= i <= K:
                        accumulate(cur, u, i)
                    if nxt is not None:
                        misc(t, nxt, 1 - u, e)
                if cur is not None:
                    accumulate(cur, u, K)
                    dve.wait_ge(tanh_act.sem, tanh_act.at(cur, "tanh"))
                    dve.scalar_tensor_tensor(xtile(m.gate, cur), w.th, 1.0, w.acc, ALU.add, ALU.mult)\
                       .then_inc(acc_dve.sem, 1)

            def accumulate(b, u, i):
                name = "base" if i == 0 else f"e{first + i - 1}"
                dve.wait_ge(out_pe.sem, out_pe.at(b, name))
                F = m.F[(i + u) % 2][:, 0:N].rearrange("p (k c) -> p k c", k=TT)
                if i == 0:
                    if exists(b - 1):
                        dve.wait_ge(acc_dve.sem, acc_dve.at(b - 1, "gate"))
                    a = dve.tensor_tensor(w.acc, F, w.xk[u], ALU.add)
                else:
                    dve.wait_ge(acc_dve.sem, acc_dve.at(b, "base" if i == 1 else f"e{first + i - 2}"))
                    for k in range(TT):
                        a = dve.scalar_tensor_tensor(w.acc[:, k, :], F[:, k, :], w.weight[u][:, k, i - 1:i],
                                                     w.acc[:, k, :], ALU.mult, ALU.add)
                a.then_inc(acc_dve.sem, 1)

            def misc(t, b, u, e):
                if e == 0:
                    if exists(b - 1):
                        dve.wait_ge(ln_pool.sem, ln_pool.at(b - 1, "rstd"))
                    for k in range(TT):
                        dve.bn_stats(m.stats[:, k, :], xtile(m.X, b, k, 1)).then_inc(ln_dve.sem, 1)
                    for k in range(TT):
                        dve.wait_ge(ln_dve.sem, ln_dve.at(b, f"stats{k}"))
                        own_wait(dve)
                        dve.bn_aggr(m.mean_var[:, k, :], m.stats[:, k, :]).then_inc(ln_dve.sem, 1)
                if e == 1:
                    dve.wait_ge(ln_pool.sem, ln_pool.at(b, "rstd"))
                    if exists(b - 1):
                        dve.wait_ge(xT_act.sem, xT_act.at(b - 1, "xnT"))
                    for k in range(TT):
                        dve.tensor_scalar(m.xn[:, k, :], xtile(m.X, b, k, 1), m.mean_var[:, k, 0:1],
                                          m.rstd[:, k:k + 1], ALU.subtract, ALU.mult).then_inc(ln_dve.sem, 1)
                if e == 3:
                    dve.wait_ge(ln_pool.sem, ln_pool.at(b, "r2"))
                    dve.wait_ge(ln_dve.sem, ln_dve.at(b, "xn1"))
                    if exists(b - 2):
                        dve.wait_ge(acc_dve.sem, acc_dve.at(b - 2, "base"))
                    if exists(b - 1):
                        dve.wait_ge(xT_act.sem, xT_act.at(b - 1, "xrT"))
                    for k in range(TT):
                        dve.tensor_copy(w.xk[u][:, k, :], m.xn[:, k, :])
                        dve.tensor_scalar(w.xr[:, k, :], m.xn[:, k, :], w.r2[:, k:k + 1], None, ALU.mult)\
                           .then_inc(ln_dve.sem, 1)
                if e == 7:
                    R = route_dve
                    if exists(b - 1):
                        dve.wait_ge(R.sem, R.at(b - 1, R.names[-1]))
                    dve.wait_ge(route_act.sem, route_act.at(b, "act"))
                    dve.tensor_scalar(w.v[:, :, :], w.v0[:, :, :], 0.5, 0.5, ALU.mult, ALU.add).then_inc(R.sem, 1)
                    dve.wait_ge(R.sem, R.at(b, "v"))
                    dve.tensor_reduce(w.vsum[:, :, :], w.v[:, :, :], AX.X, ALU.add).then_inc(R.sem, 1)
                    dve.wait_ge(R.sem, R.at(b, "vsum"))
                    dve.reciprocal(w.vrec[:, :, :], w.vsum[:, :, :]).then_inc(R.sem, 1)
                    top(b, 1)
                    dve.scalar_tensor_tensor(w.v2[:, :, :], w.one[:, :, 0:K], -1e30, w.v[:, :, :], ALU.mult, ALU.add)\
                       .then_inc(R.sem, 1)
                    dve.wait_ge(R.sem, R.at(b, "less"))
                    top(b, 2)
                if e == 9:
                    R = route_dve
                    dve.tensor_tensor(w.ohs[:, :, :], w.one[:, :, 0:K], w.one[:, :, K:2 * K], ALU.add)\
                       .then_inc(R.sem, 1)
                    dve.wait_ge(R.sem, R.at(b, "onehots"))
                    dve.tensor_tensor(w.ohs[:, :, :], w.ohs[:, :, :], w.v[:, :, :], ALU.mult).then_inc(R.sem, 1)
                    dve.wait_ge(R.sem, R.at(b, "gates"))
                    if exists(b - 2):
                        dve.wait_ge(acc_dve.sem, acc_dve.at(b - 2, f"e{E - 1}"))
                    dve.tensor_tensor(w.weight[u][:, :, :], w.ohs[:, :, :], w.vrec[:, :, :].broadcast_to([P, TT, K]),
                                      ALU.mult).then_inc(R.sem, 1)
            turns(dve, body)

        @block.gpsimd
        def _(pool):
            def body(t):
                b = t.batch(1)
                if b is None:
                    return
                pool.wait_ge(ln_dve.sem, ln_dve.at(b, "mean1"))
                own_wait(pool)
                pool.tensor_scalar(m.var_eps[:, :], m.mean_var[:, :, 1], 1e-5, None, ALU.add).then_inc(ln_pool.sem, 1)
                pool.wait_ge(ln_pool.sem, ln_pool.at(b, "var"))
                pool.tensor_tensor(m.rstd[:, :], m.var_eps[:, :], m.minus_half[:, 0:TT], ALU.pow).then_inc(ln_pool.sem, 1)
                pool.wait_ge(ln_pool.sem, ln_pool.at(b, "rstd"))
                pool.tensor_tensor(w.sq[:, :], m.rstd[:, :], m.rstd[:, :], ALU.mult).then_inc(ln_pool.sem, 1)
                pool.wait_ge(ln_pool.sem, ln_pool.at(b, "sq"))
                pool.tensor_tensor(w.sq2[:, :], w.sq[:, :], m.mean_var[:, :, 1], ALU.mult).then_inc(ln_pool.sem, 1)
                pool.wait_ge(ln_pool.sem, ln_pool.at(b, "mean2"))
                own_wait(pool)
                pool.tensor_scalar(w.sq[:, :], w.sq2[:, :], float(np.finfo(np.float32).eps), None, ALU.add)\
                    .then_inc(ln_pool.sem, 1)
                pool.wait_ge(ln_pool.sem, ln_pool.at(b, "meps"))
                pool.tensor_tensor(w.r2[:, :], w.sq[:, :], m.minus_half[:, 0:TT], ALU.pow)\
                    .then_inc(ln_pool.sem, 1)
            turns(pool, body)


def recurrent_layer(nc, m, w, store=None):
    ctx = ExitStack()
    with ctx:
        def sem(name):
            return ctx.enter_context(nc.semaphore(f"l1_{name}"))

        E, C = 8, 64
        H = P
        ln_dve = Steps(sem("ln_dve"), "stats0 stats1 mean0 mean1 xn0 xn1")
        ln_pool = Steps(sem("ln_pool"), "var rstd")
        enc_act = Steps(sem("enc_act"), "xnT enc z cont r1 exp")
        enc_pool = Steps(sem("enc_pool"), "spikes keep take")
        scan_dve = Steps(sem("scan_dve"), "drive scan")
        route_dve = Steps(sem("route_dve"), "logit max shift max1 eq1 key1 top1 one1 less max2 eq2 key2 top2 one2 "
                          "onehots gates sum rec weight")
        gT_act = Steps(sem("gT_act"), "gT")
        in_pe = Steps(sem("in_pe"), [f"e{e}" for e in range(E)])
        hid = [Steps(sem(f"hid_{n}"), [f"e{e}" for e in range(i, E, 2)]) for i, n in enumerate(("act", "dve"))]
        out_pe = Steps(sem("out_pe"), [f"p{p}" for p in range(E // 2)])
        acc_dve = Steps(sem("acc_dve"), ["base"] + [f"e{e}" for e in range(E)])
        dec_act = Steps(sem("dec_act"), "outT spikes decoded tanh")
        dec_pool = Steps(sem("dec_pool"), "spikes var rstd x")
        dec_dve = Steps(sem("dec_dve"), "stats0 stats1 mean0 mean1 norm0 norm1 gain y gate gated")
        out_sp = Steps(sem("out_sp"), ["stored"], 16)
        M = BankJobs(sem("m_ready"), [("xnT", 1, enc_act, "xnT"), ("gT", 0, gT_act, "gT"), ("cont", 1, enc_act, "cont"),
                                      ("r1", 1, enc_act, "r1"), ("logit", 1, route_dve, "logit")])
        Z = BankJobs(sem("z_ready"), [("enc", 1, enc_act, "enc"), ("zh", 1, scan_dve, "drive")])
        Y = BankJobs(sem("y_ready"), [("outT", -1, dec_act, "outT"), ("c2s", -1, dec_act, "spikes"),
                                      ("dec", -1, dec_act, "decoded"), ("s", -1, dec_dve, "gated")])
        zb, yb, ob = m.S[0], m.T[0], m.O
        IN = [m.F[0], m.F[1], m.S[1], m.T[1]]

        block = ctx.enter_context(nc.Block())

        @block.sync
        def _(sp):
            if store is not None:
                def body(t):
                    b = t.batch(-1)
                    if b is not None:
                        sp.wait_ge(dec_pool.sem, dec_pool.at(b, "x"))
                        sp.dma_start(store[:, bass.ds(TT * b, TT), :], xtile(m.X, b)).then_inc(out_sp.sem, 16)
                turns(sp, body)
                if exists(B - 1):
                    sp.wait_ge(out_sp.sem, out_sp.at(B - 1, "stored"))

        @block.tensor
        def _(pe):
            def hidden(b, u, p):
                if p == 0:
                    pe.wait_ge(enc_act.sem, enc_act.at(b, "cont"))
                for e in (2 * p, 2 * p + 1):
                    if exists(b if e >= 4 else b - 1):
                        pe.wait_ge(hid[e % 2].sem, hid[e % 2].at(b if e >= 4 else b - 1, f"e{(e - 4) % E}"))
                    pe.matmul(IN[e % 4][:, 0:N], w.We1[:, e, :], w.contT[u], start=True, stop=True)\
                      .then_inc(in_pe.sem, 1)

            def outputs(b, u, p):
                pe.wait_ge(hid[0].sem, hid[0].at(b, f"e{2 * p}"))
                pe.wait_ge(hid[1].sem, hid[1].at(b, f"e{2 * p + 1}"))
                if exists(b if p else b - 1):
                    pe.wait_ge(acc_dve.sem, acc_dve.at(b if p else b - 1, f"e{(2 * p - 1) % E}"))
                if p == 0:
                    pe.wait_ge(gT_act.sem, gT_act.at(b, "gT"))
                    for k in range(TT):
                        pe.matmul(ob[:, 256 + C * k:256 + C * k + C], w.gT[:, P * k:P * k + P], w.be2[:, :],
                                  start=True, stop=True, skip_group_check=True)
                for k in range(TT):
                    for i in range(2):
                        c = C * (2 * k + i)
                        mm = pe.matmul(ob[:, c:c + C], w.hid[p % 2][:, i, P * k:P * k + P], w.We2[:, 2 * p + i, :],
                                       start=True, stop=True, skip_group_check=True)
                mm.then_inc(out_pe.sem, 1)

            def body(t):
                prev, cur, nxt = (t.batch(a) for a in (-1, 0, 1))
                u = t.parity
                q = 1 - u
                if prev is not None:
                    pe.wait_ge(acc_dve.sem, acc_dve.at(prev, f"e{E - 1}"))
                    free = Y.freed(t, "outT")
                    if free:
                        pe.wait_ge(*free)
                    own_wait(pe)
                    for k in range(TT):
                        mm = pe.transpose(yb[0:C, P * k:P * k + P], w.acc[q][:, C * k:C * k + C], m.ident[:, :])
                    mm.then_inc(Y.ready, 1)
                if cur is not None:
                    hidden(cur, u, 0)
                if nxt is not None:
                    pe.wait_ge(ln_dve.sem, ln_dve.at(nxt, "xn1"))
                    free = M.freed(t, "xnT")
                    if free:
                        pe.wait_ge(*free)
                    for k in range(TT):
                        mm = pe.transpose(m.M[:, P * k:P * k + P], m.xn[:, k, :], m.ident[:, :])
                    mm.then_inc(M.ready, 1)
                if cur is not None:
                    hidden(cur, u, 1)
                    pe.wait_ge(route_dve.sem, route_dve.at(cur, "weight"))
                    free = M.freed(t, "gT")
                    if free:
                        pe.wait_ge(*free)
                    for k in range(TT):
                        mm = pe.transpose(m.M[0:E, P * k:P * k + P], w.weight[u][:, k, :], m.ident[:, :])
                    mm.then_inc(M.ready, 1)
                if prev is not None:
                    pe.wait_ge(dec_act.sem, dec_act.at(prev, "outT"))
                    for c in range(2):
                        mm = pe.matmul(yb[:, N * c:N * c + N], w.c2s[:, P * c:P * c + P], w.outT[:, :],
                                       start=True, stop=True)
                    mm.then_inc(Y.ready, 1)
                if cur is not None:
                    outputs(cur, u, 0)
                    hidden(cur, u, 2)
                if nxt is not None:
                    free = Z.freed(t, "enc")
                    if free:
                        pe.wait_ge(*free)
                    pe.wait_ge(enc_act.sem, enc_act.at(nxt, "xnT"))
                    for c in range(2):
                        mm = pe.matmul(zb[:, N * c:N * c + N], w.enc[:, P * c:P * c + P], m.xnT[q][:, :],
                                       start=True, stop=True)
                    mm.then_inc(Z.ready, 1)
                if cur is not None:
                    outputs(cur, u, 1)
                    hidden(cur, u, 3)
                if nxt is not None:
                    free = Z.freed(t, "zh")
                    if free:
                        pe.wait_ge(*free)
                    for c, W in enumerate((w.Wz, w.Wh)):
                        mm = pe.matmul(zb[:, N * c:N * c + N], W[:, :], m.xnT[q][:, :], start=True, stop=True)
                    mm.then_inc(Z.ready, 1)
                if prev is not None:
                    pe.wait_ge(dec_pool.sem, dec_pool.at(prev, "spikes"))
                    free = Y.freed(t, "dec")
                    if free:
                        pe.wait_ge(*free)
                    for k in range(TT):
                        for c in range(2):
                            pe.matmul(yb[:, P * k:P * k + P], w.spikes2[:, c, P * k:P * k + P], w.dec[:, c, :],
                                      start=(c == 0), stop=False)
                        mm = pe.matmul(yb[:, P * k:P * k + P], m.ones[0:1, 0:P], w.dec_b[:, :], start=False, stop=True)
                    mm.then_inc(Y.ready, 1)
                if cur is not None:
                    outputs(cur, u, 2)
                if nxt is not None:
                    pe.wait_ge(enc_pool.sem, enc_pool.at(nxt, "spikes"))
                    free = M.freed(t, "cont")
                    if free:
                        pe.wait_ge(*free)
                    for c in range(2):
                        mm = pe.matmul(m.M[0:C, 0:N], w.s2c[:, c, :], w.spikes[:, c, :], start=(c == 0), stop=(c == 1))
                    mm.then_inc(M.ready, 1)
                if prev is not None:
                    pe.wait_ge(scan_dve.sem, scan_dve.at(prev, "scan"))
                    free = Y.freed(t, "s")
                    if free:
                        pe.wait_ge(*free)
                    for k in range(TT):
                        mm = pe.matmul(yb[:, P * k:P * k + P], w.hT[q][:, P * k:P * k + P], w.diffuse[:, :],
                                       start=True, stop=True)
                    mm.then_inc(Y.ready, 1)
                if cur is not None:
                    outputs(cur, u, 3)
                if nxt is not None:
                    free = M.freed(t, "r1")
                    if free:
                        pe.wait_ge(*free)
                    own_wait(pe)
                    pe.matmul(m.M[0:C, 0:N], w.rW1[:, :], w.contT[q], start=True, stop=True).then_inc(M.ready, 1)
                if nxt is not None:
                    free = M.freed(t, "logit")
                    if free:
                        pe.wait_ge(*free)
                    for k in range(TT):
                        mm = pe.matmul(m.M[:, E * k:E * k + E], w.r1T[:, P * k:P * k + P], w.rW2[:, :],
                                       start=True, stop=True)
                    mm.then_inc(M.ready, 1)
            turns(pe, body)

        @block.scalar
        def _(act):
            def relu(b, e):
                act.wait_ge(in_pe.sem, in_pe.at(b, f"e{e}"))
                if exists(b if e >= 4 else b - 1):
                    act.wait_ge(out_pe.sem, out_pe.at(b if e >= 4 else b - 1, f"p{(e // 2 - 2) % 4}"))
                act.activation(w.hid[e // 2 % 2][:, 0, :], IN[e % 4][:, 0:N], ACT.Relu, bias=w.be1[:, e:e + 1])\
                   .then_inc(hid[0].sem, 1)

            def body(t):
                prev, cur, nxt = (t.batch(a) for a in (-1, 0, 1))
                u, q = t.parity, 1 - t.parity
                if prev is not None:
                    act.wait_ge(Y.ready, Y.filled(t, "outT"))
                    act.activation(w.outT[0:C, :], yb[0:C, 0:N], ACT.Copy).then_inc(dec_act.sem, 1)
                if cur is not None:
                    relu(cur, 0)
                if nxt is not None:
                    act.wait_ge(M.ready, M.filled(t, "xnT"))
                    act.activation(m.xnT[q][:, :], m.M[:, 0:N], ACT.Copy).then_inc(enc_act.sem, 1)
                if cur is not None:
                    relu(cur, 2)
                    act.wait_ge(M.ready, M.filled(t, "gT"))
                    if exists(cur - 1):
                        act.wait_ge(out_pe.sem, out_pe.at(cur - 1, "p0"))
                    act.activation(w.gT[:, :], m.M[0:E, 0:N], ACT.Copy).then_inc(gT_act.sem, 1)
                if prev is not None:
                    act.wait_ge(Y.ready, Y.filled(t, "c2s"))
                    if exists(prev - 1):
                        act.wait_ge(dec_pool.sem, dec_pool.at(prev - 1, "spikes"))
                    for c in range(2):
                        a = act.activation(w.th2[:, c, :], yb[:, N * c:N * c + N], ACT.Tanh, scale=0.5,
                                           bias=w.c2s_b[:, c:c + 1])
                    a.then_inc(dec_act.sem, 1)
                if cur is not None:
                    relu(cur, 4)
                if nxt is not None:
                    act.wait_ge(Z.ready, Z.filled(t, "enc"))
                    if exists(nxt - 1):
                        act.wait_ge(enc_pool.sem, enc_pool.at(nxt - 1, "spikes"))
                    for c in range(2):
                        a = act.activation(w.th[:, c, :], zb[:, N * c:N * c + N], ACT.Tanh, scale=0.5,
                                           bias=w.enc_b[:, c:c + 1])
                    a.then_inc(enc_act.sem, 1)
                if cur is not None:
                    relu(cur, 6)
                if nxt is not None:
                    act.wait_ge(Z.ready, Z.filled(t, "zh"))
                    if exists(nxt - 1):
                        act.wait_ge(enc_pool.sem, enc_pool.at(nxt - 1, "take"))
                    act.activation(w.zth[:, :], zb[:, 0:N], ACT.Tanh, scale=0.5, bias=w.bz[:, :])\
                       .then_inc(enc_act.sem, 1)
                if prev is not None:
                    act.wait_ge(Y.ready, Y.filled(t, "dec"))
                    if exists(prev - 1):
                        act.wait_ge(dec_dve.sem, dec_dve.at(prev - 1, "norm1"))
                    act.activation(w.dth[:, :, :], yb[:, 0:N].rearrange("p (k c) -> p k c", k=TT), ACT.Tanh, scale=0.5)\
                       .then_inc(dec_act.sem, 1)
                if nxt is not None:
                    act.wait_ge(M.ready, M.filled(t, "cont"))
                    act.activation(w.contT[q][0:C, :], m.M[0:C, 0:N], ACT.Identity, bias=w.s2c_b[:, :])\
                       .then_inc(enc_act.sem, 1)
                    act.wait_ge(M.ready, M.filled(t, "r1"))
                    act.activation(w.r1T[:, :], m.M[0:C, 0:N], ACT.Tanh, bias=w.rb1[:, :]).then_inc(enc_act.sem, 1)
                if prev is not None:
                    act.wait_ge(dec_dve.sem, dec_dve.at(prev, "y"))
                    act.activation(w.gth[:, :, :], w.y[:, :, :], ACT.Tanh, scale=0.5).then_inc(dec_act.sem, 1)
                if nxt is not None:
                    act.wait_ge(route_dve.sem, route_dve.at(nxt, "shift"))
                    act.activation(w.v[:, :, :], w.v0[:, :, :], ACT.Exp).then_inc(enc_act.sem, 1)
            turns(act, body)

        @block.vector
        def _(dve):
            def relu(b, e):
                dve.wait_ge(in_pe.sem, in_pe.at(b, f"e{e}"))
                if exists(b if e >= 4 else b - 1):
                    dve.wait_ge(out_pe.sem, out_pe.at(b if e >= 4 else b - 1, f"p{(e // 2 - 2) % 4}"))
                dve.tensor_scalar(w.hid[e // 2 % 2][:, 1, :], IN[e % 4][:, 0:N], w.be1[:, e:e + 1], 0.0, ALU.add, ALU.max)\
                   .then_inc(hid[1].sem, 1)

            def accumulate(b, u, p):
                for i in range(2):
                    e = 2 * p + i
                    if i == 0:
                        dve.wait_ge(out_pe.sem, out_pe.at(b, f"p{p}"))
                    if e == 0:
                        dve.tensor_copy(w.acc[u][:, 0:TT * C], ob[:, 256:256 + TT * C]).then_inc(acc_dve.sem, 1)
                    dve.wait_ge(acc_dve.sem, acc_dve.at(b, f"e{e - 1}" if e else "base"))
                    for k in range(TT):
                        acc = w.acc[u][:, C * k:C * k + C]
                        a = dve.scalar_tensor_tensor(acc, ob[:, C * (2 * k + i):C * (2 * k + i) + C],
                                                     w.weight[u][:, k, e:e + 1], acc, ALU.mult, ALU.add)
                    a.then_inc(acc_dve.sem, 1)

            R = route_dve

            def top(b, n):
                v = w.v if n == 1 else w.v2
                dve.tensor_reduce(w.mx[:, :, :], v[:, :, :], AX.X, ALU.max).then_inc(R.sem, 1)
                dve.wait_ge(R.sem, R.at(b, f"max{n}"))
                dve.tensor_tensor(w.eq[:, :, :], v[:, :, :], w.mx[:, :, :].broadcast_to([P, TT, E]), ALU.is_ge)\
                   .then_inc(R.sem, 1)
                dve.wait_ge(R.sem, R.at(b, f"eq{n}"))
                dve.tensor_tensor(w.eq[:, :, :], w.eq[:, :, :], m.rank[:, :, :], ALU.mult).then_inc(R.sem, 1)
                dve.wait_ge(R.sem, R.at(b, f"key{n}"))
                dve.tensor_reduce(w.mx[:, :, :], w.eq[:, :, :], AX.X, ALU.max).then_inc(R.sem, 1)
                dve.wait_ge(R.sem, R.at(b, f"top{n}"))
                dve.tensor_tensor(w.one[:, :, E * (n - 1):E * n], w.eq[:, :, :],
                                  w.mx[:, :, :].broadcast_to([P, TT, E]), ALU.is_equal).then_inc(R.sem, 1)
                dve.wait_ge(R.sem, R.at(b, f"one{n}"))

            def route(b, u, t):
                dve.wait_ge(M.ready, M.filled(t, "logit"))
                if exists(b - 1):
                    dve.wait_ge(R.sem, R.at(b - 1, "weight"))
                dve.tensor_tensor(w.v0[:, :, :], m.M[:, 0:TT * E].rearrange("p (k e) -> p k e", k=TT), w.rb2[:, :, :],
                                  ALU.add).then_inc(R.sem, 1)
                dve.wait_ge(R.sem, R.at(b, "logit"))
                dve.tensor_reduce(w.mx[:, :, :], w.v0[:, :, :], AX.X, ALU.max).then_inc(R.sem, 1)
                dve.wait_ge(R.sem, R.at(b, "max"))
                dve.tensor_tensor(w.v0[:, :, :], w.v0[:, :, :], w.mx[:, :, :].broadcast_to([P, TT, E]), ALU.subtract)\
                   .then_inc(R.sem, 1)
                dve.wait_ge(enc_act.sem, enc_act.at(b, "exp"))
                top(b, 1)
                dve.scalar_tensor_tensor(w.v2[:, :, :], w.one[:, :, 0:E], MASKED, w.v[:, :, :], ALU.mult, ALU.add)\
                   .then_inc(R.sem, 1)
                dve.wait_ge(R.sem, R.at(b, "less"))
                top(b, 2)
                dve.tensor_tensor(w.ohs[:, :, :], w.one[:, :, 0:E], w.one[:, :, E:2 * E], ALU.add).then_inc(R.sem, 1)
                dve.wait_ge(R.sem, R.at(b, "onehots"))
                dve.tensor_tensor(w.ohs[:, :, :], w.ohs[:, :, :], w.v[:, :, :], ALU.mult).then_inc(R.sem, 1)
                dve.wait_ge(R.sem, R.at(b, "gates"))
                dve.tensor_reduce(w.mx[:, :, :], w.ohs[:, :, :], AX.X, ALU.add).then_inc(R.sem, 1)
                dve.wait_ge(R.sem, R.at(b, "sum"))
                dve.reciprocal(w.vrec[:, :, :], w.mx[:, :, :]).then_inc(R.sem, 1)
                dve.wait_ge(R.sem, R.at(b, "rec"))
                dve.tensor_tensor(w.weight[u][:, :, :], w.ohs[:, :, :], w.vrec[:, :, :].broadcast_to([P, TT, E]),
                                  ALU.mult).then_inc(R.sem, 1)

            def body(t):
                prev, cur, nxt, new = (t.batch(a) for a in (-1, 0, 1, 2))
                u, q = t.parity, 1 - t.parity
                if cur is not None:
                    relu(cur, 1)
                    relu(cur, 3)
                    accumulate(cur, u, 0)
                    relu(cur, 5)
                if new is not None:
                    if exists(new - 1):
                        dve.wait_ge(ln_pool.sem, ln_pool.at(new - 1, "rstd"))
                    if exists(new - 1):
                        dve.wait_ge(ln_dve.sem, ln_dve.at(new - 1, "xn1"))
                    for k in range(TT):
                        dve.bn_stats(m.stats[:, k, :], xtile(m.X, new, k, 1)).then_inc(ln_dve.sem, 1)
                    for k in range(TT):
                        dve.wait_ge(ln_dve.sem, ln_dve.at(new, f"stats{k}"))
                        own_wait(dve)
                        dve.bn_aggr(m.mean_var[:, k, :], m.stats[:, k, :]).then_inc(ln_dve.sem, 1)
                if cur is not None:
                    accumulate(cur, u, 1)
                    relu(cur, 7)
                if nxt is not None:
                    dve.wait_ge(Z.ready, Z.filled(t, "zh"))
                    dve.wait_ge(enc_pool.sem, enc_pool.at(nxt, "take"))
                    if exists(nxt - 1):
                        dve.wait_ge(scan_dve.sem, scan_dve.at(nxt - 1, "scan"))
                    dve.scalar_tensor_tensor(w.drive[:, :], zb[:, N:2 * N], w.bh[:, :], w.take[:, :], ALU.add, ALU.mult)\
                       .then_inc(scan_dve.sem, 1)
                if prev is not None:
                    D_ = dec_dve
                    dve.wait_ge(dec_act.sem, dec_act.at(prev, "decoded"))
                    if exists(prev - 1):
                        dve.wait_ge(dec_pool.sem, dec_pool.at(prev - 1, "rstd"))
                    for k in range(TT):
                        dve.bn_stats(w.stats[:, k, :], w.dth[:, k, :]).then_inc(D_.sem, 1)
                    for k in range(TT):
                        dve.wait_ge(D_.sem, D_.at(prev, f"stats{k}"))
                        own_wait(dve)
                        dve.bn_aggr(w.mean_var[:, k, :], w.stats[:, k, :]).then_inc(D_.sem, 1)
                if cur is not None:
                    accumulate(cur, u, 2)
                if nxt is not None:
                    if prev is not None:
                        dve.wait_ge(Y.ready, Y.filled(t, "s"))
                    dve.wait_ge(scan_dve.sem, scan_dve.at(nxt, "drive"))
                    dve.tensor_tensor_scan(w.hT[q], w.keep, w.drive, 0.0, ALU.mult, ALU.add)\
                       .then_inc(scan_dve.sem, 1)
                if new is not None:
                    dve.wait_ge(ln_pool.sem, ln_pool.at(new, "rstd"))
                    if nxt is not None:
                        dve.wait_ge(M.ready, M.filled(t, "xnT"))
                    for k in range(TT):
                        dve.tensor_scalar(m.xn[:, k, :], xtile(m.X, new, k, 1), m.mean_var[:, k, 0:1],
                                          m.rstd[:, k:k + 1], ALU.subtract, ALU.mult).then_inc(ln_dve.sem, 1)
                if prev is not None:
                    dve.wait_ge(dec_pool.sem, dec_pool.at(prev, "rstd"))
                    for k in range(TT):
                        dve.tensor_scalar(w.yn[:, k, :], w.dth[:, k, :], w.mean_var[:, k, 0:1], w.rstd[:, k:k + 1],
                                          ALU.subtract, ALU.mult).then_inc(D_.sem, 1)
                    dve.wait_ge(D_.sem, D_.at(prev, "norm1"))
                    dve.tensor_tensor(w.yn[:, :, :], w.yn[:, :, :], w.ln_g[:, :].unsqueeze(1).broadcast_to([P, TT, D]),
                                      ALU.mult).then_inc(D_.sem, 1)
                    dve.wait_ge(D_.sem, D_.at(prev, "gain"))
                    dve.tensor_tensor(w.y[:, :, :], w.yn[:, :, :], w.ln_b[:, :].unsqueeze(1).broadcast_to([P, TT, D]),
                                      ALU.add).then_inc(D_.sem, 1)
                if cur is not None:
                    accumulate(cur, u, 3)
                if prev is not None:
                    dve.wait_ge(dec_act.sem, dec_act.at(prev, "tanh"))
                    dve.scalar_tensor_tensor(w.gate[:, :, :], w.gth[:, :, :], 1.0, w.y[:, :, :], ALU.add, ALU.mult)\
                       .then_inc(D_.sem, 1)
                    dve.wait_ge(D_.sem, D_.at(prev, "gate"))
                    dve.wait_ge(Y.ready, Y.filled(t, "s"))
                    if exists(prev - 1):
                        dve.wait_ge(dec_pool.sem, dec_pool.at(prev - 1, "x"))
                    dve.scalar_tensor_tensor(m.gated[:, :, :], yb[:, 0:N].rearrange("p (k c) -> p k c", k=TT), 0.5,
                                             w.gate[:, :, :], ALU.mult, ALU.mult).then_inc(D_.sem, 1)
                if nxt is not None:
                    route(nxt, q, t)
            turns(dve, body)

        @block.gpsimd
        def _(pool):
            def body(t):
                prev, cur, nxt, new = (t.batch(a) for a in (-1, 0, 1, 2))
                if prev is not None:
                    pool.wait_ge(dec_act.sem, dec_act.at(prev, "spikes"))
                    own_wait(pool)
                    pool.tensor_scalar(w.spikes2[:, :, :], w.th2[:, :, :], 0.5, 0.5, ALU.mult, ALU.add)\
                        .then_inc(dec_pool.sem, 1)
                if nxt is not None:
                    pool.wait_ge(enc_act.sem, enc_act.at(nxt, "enc"))
                    own_wait(pool)
                    pool.tensor_scalar(w.spikes[:, :, :], w.th[:, :, :], 0.5, 0.5, ALU.mult, ALU.add)\
                        .then_inc(enc_pool.sem, 1)
                if new is not None:
                    pool.wait_ge(ln_dve.sem, ln_dve.at(new, "mean1"))
                    own_wait(pool)
                    pool.tensor_scalar(m.var_eps[:, :], m.mean_var[:, :, 1], 1e-5, None, ALU.add)\
                        .then_inc(ln_pool.sem, 1)
                    pool.wait_ge(ln_pool.sem, ln_pool.at(new, "var"))
                    pool.tensor_tensor(m.rstd[:, :], m.var_eps[:, :], m.minus_half[:, 0:TT], ALU.pow)\
                        .then_inc(ln_pool.sem, 1)
                if nxt is not None:
                    pool.wait_ge(enc_act.sem, enc_act.at(nxt, "z"))
                    if exists(nxt - 1):
                        pool.wait_ge(scan_dve.sem, scan_dve.at(nxt - 1, "scan"))
                    own_wait(pool)
                    pool.tensor_scalar(w.keep[:, :], w.zth[:, :], -0.5, 0.5, ALU.mult, ALU.add)\
                        .then_inc(enc_pool.sem, 1)
                    pool.tensor_scalar(w.take[:, :], w.zth[:, :], 0.5, 0.5, ALU.mult, ALU.add)\
                        .then_inc(enc_pool.sem, 1)
                if prev is not None:
                    pool.wait_ge(dec_dve.sem, dec_dve.at(prev, "mean1"))
                    own_wait(pool)
                    pool.tensor_scalar(w.var_eps[:, :], w.mean_var[:, :, 1], 4e-5, None, ALU.add)\
                        .then_inc(dec_pool.sem, 1)
                    pool.wait_ge(dec_pool.sem, dec_pool.at(prev, "var"))
                    pool.tensor_tensor(w.rstd[:, :], w.var_eps[:, :], m.minus_half[:, 0:TT], ALU.pow)\
                        .then_inc(dec_pool.sem, 1)
                    pool.wait_ge(dec_dve.sem, dec_dve.at(prev, "gated"))
                    X = xtile(m.X, prev)
                    pool.tensor_tensor(X, X, m.gated[:, :, :], ALU.add).then_inc(dec_pool.sem, 1)
            turns(pool, body)



SLOTS_OF_EXPERT = 2 * CAPACITY
XROWS = 8 * SLOTS_OF_EXPERT
ST = SLOTS_OF_EXPERT // P


def dispatch_layer(nc, m, w):
    ctx = ExitStack()
    with ctx:
        def sem(name):
            return ctx.enter_context(nc.semaphore(f"l3d_{name}"))

        K, G = 8, w.G
        ln_dve = Steps(sem("ln_dve"), [f"{x}{k}" for x in ("stats", "mean", "xn") for k in range(w.G)])
        ln_pool = Steps(sem("ln_pool"), "var rstd")
        xT_act = Steps(sem("xT_act"), "xnT")
        exp_act = Steps(sem("exp_act"), "exp")
        R = Steps(sem("route_dve"), "logit max shift vsum vrec max1 eq1 key1 top1 one1 less max2 eq2 key2 top2 one2 "
                  "place keep chosen slots slot kept spare0 spare1 index gather gates0 gates1 gate weight counts")
        xT_pe = Steps(sem("xT_pe"), "xnT")
        sent = Steps(sem("sent"), ["rows"], 16 * 2 * G)
        M = BankJobs(sem("m_ready"), [("logit", 0, R, "logit"), ("count", 0, R, "keep")],
                     count=B * TT // G)

        block = ctx.enter_context(nc.Block())

        @block.tensor
        def _(pe):
            def body(t):
                cur, nxt = t.batch(0), t.batch(1)
                u = t.parity
                if cur is not None:
                    pe.wait_ge(xT_act.sem, xT_act.at(cur, "xnT"))
                    free = M.freed(t, "logit")
                    if free:
                        pe.wait_ge(*free)
                    for k in range(G):
                        mm = pe.matmul(m.M[:, K * k:K * k + K], w.xnT[u][:, P * k:P * k + P], w.router[:, :],
                                       start=True, stop=True)
                    mm.then_inc(M.ready, 1)
                    pe.wait_ge(R.sem, R.at(cur, "one2"))
                    for k in range(G):
                        pe.matmul(m.M[:, 16 * k:16 * k + 16], m.upto[:, :], w.g_one[:, k, :], start=True, stop=False)
                        for j in range(k):
                            pe.matmul(m.M[:, 16 * k:16 * k + 16], m.ones[:, :], w.g_one[:, j, :], start=False, stop=False)
                        mm = pe.matmul(m.M[:, 16 * k:16 * k + 16], m.ones[:, :], w.counts[:, :], start=False, stop=True)
                    mm.then_inc(M.ready, 1)
                if nxt is not None:
                    pe.wait_ge(ln_dve.sem, ln_dve.at(nxt, f"xn{G - 1}"))
                    if exists(nxt - 1):
                        pe.wait_ge(xT_act.sem, xT_act.at(nxt - 1, "xnT"))
                    for k in range(G):
                        mm = pe.transpose(m.S[0][:, P * k:P * k + P], w.xs[1 - u][:, k, :], m.ident[:, :])
                    mm.then_inc(xT_pe.sem, 1)
            turns(pe, body, count=B * TT // G, start=-1)

        @block.scalar
        def _(act):
            def body(t):
                cur, nxt = t.batch(0), t.batch(1)
                if cur is not None:
                    act.wait_ge(R.sem, R.at(cur, "shift"))
                    act.activation(w.g_v[:, :, :], w.g_v0[:, :, :], ACT.Exp).then_inc(exp_act.sem, 1)
                if nxt is not None:
                    act.wait_ge(xT_pe.sem, xT_pe.at(nxt, "xnT"))
                    act.activation(w.xnT[1 - t.parity], m.S[0][:, :], ACT.Copy).then_inc(xT_act.sem, 1)
            turns(act, body, count=B * TT // G, start=-1)

        @block.vector
        def _(dve):
            def top(b, n):
                v = w.g_v if n == 1 else w.g_v2
                dve.tensor_reduce(w.g_mx[:, :, :], v[:, :, :], AX.X, ALU.max).then_inc(R.sem, 1)
                dve.wait_ge(R.sem, R.at(b, f"max{n}"))
                dve.tensor_tensor(w.g_eq[:, :, :], v[:, :, :], w.g_mx[:, :, :].broadcast_to([P, G, K]), ALU.is_ge)\
                   .then_inc(R.sem, 1)
                dve.wait_ge(R.sem, R.at(b, f"eq{n}"))
                dve.tensor_tensor(w.g_eq[:, :, :], w.g_eq[:, :, :], m.rank[:, 0:1, :].broadcast_to([P, G, K]), ALU.mult).then_inc(R.sem, 1)
                dve.wait_ge(R.sem, R.at(b, f"key{n}"))
                dve.tensor_reduce(w.g_mx[:, :, :], w.g_eq[:, :, :], AX.X, ALU.max).then_inc(R.sem, 1)
                dve.wait_ge(R.sem, R.at(b, f"top{n}"))
                dve.tensor_tensor(w.g_one[:, :, K * (n - 1):K * n], w.g_eq[:, :, :],
                                  w.g_mx[:, :, :].broadcast_to([P, G, K]), ALU.is_equal).then_inc(R.sem, 1)
                dve.wait_ge(R.sem, R.at(b, f"one{n}"))

            def choose(b, t):
                dve.wait_ge(M.ready, M.filled(t, "logit"))
                if exists(b - 1):
                    dve.wait_ge(R.sem, R.at(b - 1, "counts"))
                dve.tensor_tensor(w.g_v0[:, :, :], m.M[:, 0:G * K].rearrange("p (k e) -> p k e", k=G),
                                  w.router_b[:, :, :].broadcast_to([P, G, K]), ALU.add).then_inc(R.sem, 1)
                dve.wait_ge(R.sem, R.at(b, "logit"))
                dve.tensor_reduce(w.g_mx[:, :, :], w.g_v0[:, :, :], AX.X, ALU.max).then_inc(R.sem, 1)
                dve.wait_ge(R.sem, R.at(b, "max"))
                dve.tensor_tensor(w.g_v0[:, :, :], w.g_v0[:, :, :], w.g_mx[:, :, :].broadcast_to([P, G, K]),
                                  ALU.subtract).then_inc(R.sem, 1)
                dve.wait_ge(exp_act.sem, exp_act.at(b, "exp"))
                dve.tensor_reduce(w.g_vsum[:, :, :], w.g_v[:, :, :], AX.X, ALU.add).then_inc(R.sem, 1)
                dve.wait_ge(R.sem, R.at(b, "vsum"))
                dve.reciprocal(w.g_vrec[:, :, :], w.g_vsum[:, :, :]).then_inc(R.sem, 1)
                top(b, 1)
                dve.scalar_tensor_tensor(w.g_v2[:, :, :], w.g_one[:, :, 0:K], MASKED, w.g_v[:, :, :], ALU.mult, ALU.add)\
                   .then_inc(R.sem, 1)
                dve.wait_ge(R.sem, R.at(b, "less"))
                top(b, 2)

            def place(b, u, t):
                counts = m.M[:, 0:16 * G].rearrange("p (k e) -> p k e", k=G)
                dve.wait_ge(M.ready, M.filled(t, "count"))
                dve.tensor_tensor(w.place[:, :, :], counts, m.first_slot[:, 0:1, :].broadcast_to([P, G, 2 * K]), ALU.add).then_inc(R.sem, 1)
                dve.scalar_tensor_tensor(w.g_kept[:, :, :], counts, float(CAPACITY) + 0.5, w.g_one[:, :, :],
                                         ALU.is_le, ALU.mult).then_inc(R.sem, 1)
                dve.tensor_reduce(w.cnt2[:, :].unsqueeze(2), w.g_one[:, :, :].rearrange("p k e -> p e k"), AX.X, ALU.add)\
                   .then_inc(R.sem, 1)
                dve.wait_ge(R.sem, R.at(b, "keep"))
                dve.tensor_tensor(w.place[:, :, :], w.place[:, :, :], w.g_kept[:, :, :], ALU.mult).then_inc(R.sem, 1)
                dve.wait_ge(R.sem, R.at(b, "slots"))
                by_choice = "p k (c e) -> p (k c) e"
                dve.tensor_reduce(w.slot[:, :], w.place[:, :, :].rearrange(by_choice, c=2), AX.X, ALU.add)\
                   .then_inc(R.sem, 1)
                dve.tensor_reduce(w.is_kept[:, :], w.g_kept[:, :, :].rearrange(by_choice, c=2), AX.X, ALU.max)\
                   .then_inc(R.sem, 1)
                dve.wait_ge(R.sem, R.at(b, "kept"))
                dve.tensor_tensor(w.is_kept[:, :], w.is_kept[:, :], m.spare[:, 0:1].broadcast_to([P, 2 * G]), ALU.mult).then_inc(R.sem, 1)
                dve.wait_ge(R.sem, R.at(b, "spare0"))
                dve.tensor_tensor(w.is_kept[:, :], m.spare[:, 0:1].broadcast_to([P, 2 * G]), w.is_kept[:, :], ALU.subtract).then_inc(R.sem, 1)
                dve.wait_ge(R.sem, R.at(b, "spare1"))
                dve.tensor_tensor(w.index[u][:, :], w.is_kept[:, :], w.slot[:, :], ALU.add).then_inc(R.sem, 1)
                dve.tensor_copy(w.slots[:, bass.ds(2 * G * b, 2 * G)], w.slot[:, :]).then_inc(R.sem, 1)
                for c in range(2):
                    kept = w.g_kept[:, :, K * c:K * c + K]
                    dve.tensor_tensor(kept, kept, w.g_v[:, :, :], ALU.mult).then_inc(R.sem, 1)
                dve.wait_ge(R.sem, R.at(b, "gates1"))
                dve.tensor_reduce(w.share[:, :], w.g_kept[:, :, :].rearrange(by_choice, c=2), AX.X, ALU.add)\
                   .then_inc(R.sem, 1)
                dve.wait_ge(R.sem, R.at(b, "gate"))
                dve.tensor_tensor(w.shares[:, bass.ds(2 * G * b, 2 * G)].rearrange("p (k c) -> p k c", c=2),
                                  w.share[:, :].rearrange("p (k c) -> p k c", c=2),
                                  w.g_vrec[:, :, :].broadcast_to([P, G, 2]), ALU.mult).then_inc(R.sem, 1)
                dve.tensor_tensor(w.counts[:, :], w.counts[:, :], w.cnt2[:, :], ALU.add).then_inc(R.sem, 1)

            def body(t):
                cur, nxt = t.batch(0), t.batch(1)
                u = t.parity
                if nxt is not None:
                    if exists(nxt - 1):
                        dve.wait_ge(ln_pool.sem, ln_pool.at(nxt - 1, "rstd"))
                    if exists(nxt - 1):
                        dve.wait_ge(ln_dve.sem, ln_dve.at(nxt - 1, f"xn{G - 1}"))
                    for k in range(G):
                        dve.bn_stats(w.gstats[:, k, :], m.X[:, bass.ds(G * nxt + k, 1), :]).then_inc(ln_dve.sem, 1)
                    for k in range(G):
                        dve.wait_ge(ln_dve.sem, ln_dve.at(nxt, f"stats{k}"))
                        own_wait(dve)
                        dve.bn_aggr(w.gmean_var[:, k, :], w.gstats[:, k, :]).then_inc(ln_dve.sem, 1)
                if cur is not None:
                    choose(cur, t)
                if nxt is not None:
                    dve.wait_ge(ln_pool.sem, ln_pool.at(nxt, "rstd"))
                    if exists(nxt - 2):
                        dve.wait_ge(sent.sem, sent.at(nxt - 2, "rows"))
                    for k in range(G):
                        dve.tensor_scalar(w.xs[1 - u][:, k, :], m.X[:, bass.ds(G * nxt + k, 1), :], w.gmean_var[:, k, 0:1],
                                          w.grstd[:, k:k + 1], ALU.subtract, ALU.mult).then_inc(ln_dve.sem, 1)
                if cur is not None:
                    place(cur, u, t)
            turns(dve, body, count=B * TT // G, start=-1)

        @block.gpsimd
        def _(pool):
            def body(t):
                cur, nxt = t.batch(0), t.batch(1)
                if nxt is not None:
                    pool.wait_ge(ln_dve.sem, ln_dve.at(nxt, f"mean{G - 1}"))
                    own_wait(pool)
                    pool.tensor_scalar(w.gvar_eps[:, :], w.gmean_var[:, :, 1], 1e-5, None, ALU.add)\
                        .then_inc(ln_pool.sem, 1)
                    pool.wait_ge(ln_pool.sem, ln_pool.at(nxt, "var"))
                    pool.tensor_tensor(w.grstd[:, :], w.gvar_eps[:, :], m.minus_half[:, 0:G], ALU.pow)\
                        .then_inc(ln_pool.sem, 1)
                if cur is not None:
                    pool.wait_ge(R.sem, R.at(cur, "index"))
                    if exists(cur - 1):
                        pool.wait_ge(sent.sem, sent.at(cur - 1, "rows"))
                    own_wait(pool)
                    for k in range(G):
                        for c in range(2):
                            pool.indirect_dma_start(
                                m.sorted_x, bass.IndirectOffsetOnAxis(ap=w.index[t.parity][:, 2 * k + c:2 * k + c + 1],
                                                                      axis=0),
                                w.xs[t.parity][:, k, :], None, bounds_check=XROWS - 1, oob_is_err=False).then_inc(sent.sem, 16)
            turns(pool, body, count=B * TT // G, start=-1)
            pool.wait_ge(sent.sem, sent.at(B * TT // G - 1, "rows"))


def experts_layer(nc, m, w, W1, W2, b1, b2):
    ctx = ExitStack()
    with ctx:
        def sem(name):
            return ctx.enter_context(nc.semaphore(f"l3e_{name}"))

        E, C, S4 = 8, 4, 4 * P
        loaded = Steps(sem("loaded"), ["expert"], 16 * 5)
        xT_pe = Steps(sem("xT_pe"), "x")
        xT_act, xT_dve = Steps(sem("xT_act"), "x"), Steps(sem("xT_dve"), "x")
        h_pe = Steps(sem("h_pe"), [f"c{c}" for c in range(C)])
        h_act = Steps(sem("h_act"), [f"c{c}" for c in range(C)])
        h_dve = Steps(sem("h_dve"), [f"c{c}" for c in range(C)])
        y_pe = Steps(sem("y_pe"), "y")
        y_dve = Steps(sem("y_dve"), "y")
        stored = Steps(sem("stored"), ["y"], 16)

        block = ctx.enter_context(nc.Block())

        @block.sync
        def _(sp):
            def body(t):
                e = t.batch(1)
                if e is not None:
                    v = w.ex[(t.parity + 1) % 2]
                    if exists(e - 2):
                        sp.wait_ge(y_dve.sem, y_dve.at(e - 2, "y"))
                    if exists(e - 1):
                        sp.wait_ge(loaded.sem, loaded.at(e - 1, "expert"))
                    sp.dma_start(v.x, m.sorted_x[bass.ds(SLOTS_OF_EXPERT * e, SLOTS_OF_EXPERT), :]
                                 .rearrange("(s p) d -> p s d", p=P)).then_inc(loaded.sem, 16)
                    sp.dma_start(v.W1, W1[:, bass.ds(e, 1), :].rearrange("p a n -> p (a n)")).then_inc(loaded.sem, 16)
                    sp.dma_start(v.b1, b1[:, bass.ds(e, 1), :].rearrange("p a n -> p (a n)")).then_inc(loaded.sem, 16)
                    sp.dma_start(v.W2, W2[:, bass.ds(e, 1), :, :].rearrange("p a c n -> p (a c n)"))\
                      .then_inc(loaded.sem, 16)
                    sp.dma_start(v.b2, b2[bass.ds(e, 1), :].broadcast_to([P, D])).then_inc(loaded.sem, 16)
                e = t.batch(-1)
                if e is not None:
                    sp.wait_ge(y_dve.sem, y_dve.at(e, "y"))
                    own_wait(sp)
                    if exists(e - 1):
                        sp.wait_ge(stored.sem, stored.at(e - 1, "y"))
                    sp.dma_start(m.sorted_y[bass.ds(SLOTS_OF_EXPERT * e, SLOTS_OF_EXPERT), :]
                                 .rearrange("(s p) d -> p s d", p=P), w.ex[(t.parity + 1) % 2].y)\
                      .then_inc(stored.sem, 16)
            turns(sp, body, count=E, start=-1)
            sp.wait_ge(stored.sem, stored.at(E - 1, "y"))

        @block.tensor
        def _(pe):
            def body(t):
                cur, nxt = t.batch(0), t.batch(1)
                u = t.parity
                if cur is not None:
                    v = w.ex[u]
                    for c in range(C):
                        if c == 0:
                            pe.wait_ge(xT_act.sem, xT_act.at(cur, "x"))
                            pe.wait_ge(xT_dve.sem, xT_dve.at(cur, "x"))
                        if exists(cur if c >= 2 else cur - 1):
                            pe.wait_ge(h_act.sem, h_act.at(cur if c >= 2 else cur - 1, f"c{(c - 2) % C}"))
                            pe.wait_ge(h_dve.sem, h_dve.at(cur if c >= 2 else cur - 1, f"c{(c - 2) % C}"))
                        W = v.W1[:, P * c:P * c + P]
                        pe.matmul(m.T[c % 2][:, :], W, v.xT[:, 0:S4], start=True, stop=True)
                        pe.matmul(m.F[c % 2][:, 0:P], W, v.xT[:, S4:S4 + P], start=True, stop=True)\
                          .then_inc(h_pe.sem, 1)
                if nxt is not None:
                    pe.wait_ge(loaded.sem, loaded.at(nxt, "expert"))
                    if exists(nxt - 1):
                        pe.wait_ge(xT_act.sem, xT_act.at(nxt - 1, "x"))
                        pe.wait_ge(xT_dve.sem, xT_dve.at(nxt - 1, "x"))
                    for s in range(ST):
                        bank = m.S[s // 4]
                        mm = pe.transpose(bank[:, P * (s % 4):P * (s % 4) + P], w.ex[1 - u].x[:, s, :], m.ident[:, :])
                    mm.then_inc(xT_pe.sem, 1)
                if cur is not None:
                    pe.wait_ge(h_act.sem, h_act.at(cur, f"c{C - 1}"))
                    pe.wait_ge(h_dve.sem, h_dve.at(cur, f"c{C - 1}"))
                    if exists(cur - 1):
                        pe.wait_ge(y_dve.sem, y_dve.at(cur - 1, "y"))
                    for s in range(ST):
                        bank = (m.O, m.M)[s // 4]
                        for c in range(C):
                            mm = pe.matmul(bank[:, P * (s % 4):P * (s % 4) + P], w.h[u][:, c, P * s:P * s + P],
                                           v.W2[:, P * c:P * c + P], start=(c == 0), stop=(c == C - 1))
                    mm.then_inc(y_pe.sem, 1)
            turns(pe, body, count=E, start=-1)

        @block.scalar
        def _(act):
            def body(t):
                cur, nxt = t.batch(0), t.batch(1)
                u = t.parity
                if cur is not None:
                    for c in range(C):
                        act.wait_ge(h_pe.sem, h_pe.at(cur, f"c{c}"))
                        act.activation(w.h[u][:, c, 0:S4], m.T[c % 2][:, :], ACT.Relu, bias=w.ex[u].b1[:, c:c + 1])\
                           .then_inc(h_act.sem, 1)
                if nxt is not None:
                    act.wait_ge(xT_pe.sem, xT_pe.at(nxt, "x"))
                    act.activation(w.ex[1 - u].xT[:, 0:S4], m.S[0][:, :], ACT.Copy).then_inc(xT_act.sem, 1)
            turns(act, body, count=E, start=-1)

        @block.vector
        def _(dve):
            def body(t):
                cur, nxt = t.batch(0), t.batch(1)
                u = t.parity
                if cur is not None:
                    for c in range(C):
                        dve.wait_ge(h_pe.sem, h_pe.at(cur, f"c{c}"))
                        dve.tensor_scalar(w.h[u][:, c, S4:S4 + P], m.F[c % 2][:, 0:P], w.ex[u].b1[:, c:c + 1], 0.0,
                                          ALU.add, ALU.max).then_inc(h_dve.sem, 1)
                if nxt is not None:
                    dve.wait_ge(xT_pe.sem, xT_pe.at(nxt, "x"))
                    dve.tensor_copy(w.ex[1 - u].xT[:, S4:S4 + P], m.S[1][:, 0:P]).then_inc(xT_dve.sem, 1)
                if cur is not None:
                    v = w.ex[u]
                    dve.wait_ge(y_pe.sem, y_pe.at(cur, "y"))
                    if exists(cur - 2):
                        dve.wait_ge(stored.sem, stored.at(cur - 2, "y"))
                    dve.tensor_tensor(v.y[:, 0:4, :], m.O[:, :].rearrange("p (s d) -> p s d", d=D),
                                      v.b2.unsqueeze(1).broadcast_to([P, 4, D]), ALU.add)
                    dve.tensor_tensor(v.y[:, 4, :], m.M[:, 0:P], v.b2, ALU.add).then_inc(y_dve.sem, 1)
            turns(dve, body, count=E, start=-1)



class Memory:

    def __init__(self, nc, ctx):
        def sb(name, shape, dt=F32):
            return ctx.enter_context(nc.sbuf_tensor(name, shape, dt))

        def bank(name):
            return ctx.enter_context(nc.psum_tensor(name, [P, 512], F32))

        self.X = sb("X", [P, B * TT, D])
        self.xnT = [sb(f"xnT{u}", [P, N]) for u in range(2)]
        self.xn = sb("xn", [P, TT, D])
        self.stats = sb("stats", [P, TT, 6])
        self.mean_var = sb("mean_var", [P, TT, 2])
        self.var_eps = sb("var_eps", [P, TT])
        self.rstd = sb("rstd", [P, TT])
        self.rc = sb("rc", [P, 2 * N])
        self.turned = sb("turned", [P, 2, 2 * N])
        self.rest = sb("rest", [P, 2, N])
        self.parts = sb("parts", [P, 3, 2, N], BF16)
        self.parts_dram = nc.dram_tensor("parts_dram", [2, 2, 3, HD, HEADS * N], BF16, kind="Internal").ap()
        self.stack = [[sb(f"stack{o}{u}", [P, HEADS, N], BF16) for u in range(2)] for o in range(2)]
        self.rowmax = sb("rowmax", [P, TT, HEADS])
        self.shift = [sb(f"shift{i}", [HEADS // 2, 2, N], BF16) for i in range(2)]
        self.prob = sb("prob", [P, PRING, 512])
        self.vaug = [sb(f"vaug{u}", [P, TT, HEADS, 32]) for u in range(2)]
        self.oTn = [sb(f"oTn{u}", [P, GROUPS, N]) for u in range(2)]
        self.rsum = sb("rsum", [P, TT, HEADS])
        self.o = sb("o", [P, TT, D])
        self.oT = sb("oT", [P, N])
        self.gated = sb("gated", [P, TT, D])
        self.gate = sb("gate", [P, B * TT, D])
        self.W1 = sb("W1", [P, 10, 512])
        self.W2 = sb("W2", [P, 10, 4, P])
        self.ident = sb("ident", [P, P])
        self.ident_b = sb("ident_b", [P, P], BF16)
        self.tri = self.prob[:, 3, 0:2 * P].rearrange("p (k n) -> p k n", k=2)
        self.tri2 = sb("tri2", [P, 2, 2, P], BF16)
        self.cossin = sb("cossin", [P, 2 * N])
        self.upto = sb("upto", [P, P])
        self.first_slot = sb("first_slot", [P, TT, 16])
        self.spare = sb("spare", [P, 2 * TT])
        self.zeros = sb("zeros", [P, 1, D])
        self.sorted_x = nc.dram_tensor("sorted_x", [XROWS, D], F32, kind="Internal").ap()
        self.sorted_y = nc.dram_tensor("sorted_y", [XROWS, D], F32, kind="Internal").ap()
        self.rank = sb("rank", [P, TT, 8])
        self.ones = sb("ones", [P, P])
        self.minus_half = sb("minus_half", [P, 16])
        self.S = [bank(f"S{i}") for i in range(2)]
        self.T = [bank(f"T{i}") for i in range(2)]
        self.O = bank("O")
        self.M = bank("M")
        self.F = [bank(f"F{i}") for i in range(2)]


class Gated:

    def gate(self, b, u):
        return xtile(self.m.gate, b)


class SwigluFfn(Gated):

    CHUNKS = 3
    STAGE = {1: 0, 3: 1, 5: 2, 7: 3}

    def __init__(self, w):
        self.w = w

    def open(self, nc, sem, m, xnT_act):
        self.m, self.xnT_act = m, xnT_act
        c = range(self.CHUNKS)
        self.pe = Steps(sem("ffn_pe"), [f"in{i}" for i in c] + ["out"])
        self.act = Steps(sem("ffn_act"), [f"tanh{i}" for i in c] + ["tanh"])
        self.dve = Steps(sem("ffn_dve"), [f"{x}{i}" for i in c for x in ("silu", "hid")] + ["gate"])
        return self

    def bank_free(self, pe, b, i):
        steps = [f"hid{k}" for k in range(self.CHUNKS)] + ["gate"]
        if exists(b if i >= 2 else b - 1):
            pe.wait_ge(self.dve.sem, self.dve.at(b if i >= 2 else b - 1, steps[i - 2]))

    def tensor(self, pe, b, u, s):
        s = self.STAGE.get(s, -1)
        if s < 0:
            return
        m, n = self.m, self.CHUNKS
        if s == 0:
            pe.wait_ge(self.xnT_act.sem, self.xnT_act.at(b, "xnT"))
        if s < n:
            self.bank_free(pe, b, s)
            for i in range(2):
                mm = pe.matmul(m.F[s % 2][:, N * i:N * i + N], self.w.gate_up[:, i, P * s:P * s + P], m.xnT[u][:, :],
                               start=True, stop=True)
            mm.then_inc(self.pe.sem, 1)
        if s == n:
            self.bank_free(pe, b, n)
            pe.wait_ge(self.dve.sem, self.dve.at(b, f"hid{n - 1}"))
            for k in range(TT):
                for c in range(n):
                    mm = pe.matmul(m.F[n % 2][:, P * k:P * k + P], self.w.hid[:, c, P * k:P * k + P],
                                   self.w.down[:, c, :], start=(c == 0), stop=(c == n - 1))
            mm.then_inc(self.pe.sem, 1)

    def scalar(self, act, b, u, s):
        s = self.STAGE.get(s, -1)
        if s < 0:
            return
        m, n = self.m, self.CHUNKS
        if s < n:
            act.wait_ge(self.pe.sem, self.pe.at(b, f"in{s}"))
            if exists(b if s else b - 1):
                act.wait_ge(self.dve.sem, self.dve.at(b if s else b - 1, f"silu{s - 1}" if s else "gate"))
            act.activation(self.w.th[:, :], m.F[s % 2][:, 0:N], ACT.Tanh, scale=0.5).then_inc(self.act.sem, 1)
        if s == n:
            act.wait_ge(self.pe.sem, self.pe.at(b, "out"))
            act.wait_ge(self.dve.sem, self.dve.at(b, f"silu{n - 1}"))
            act.activation(self.w.th[:, :], m.F[n % 2][:, 0:N], ACT.Tanh, scale=0.5).then_inc(self.act.sem, 1)

    def vector(self, dve, b, u, s):
        s = self.STAGE.get(s, -1)
        if s < 0:
            return
        m, n = self.m, self.CHUNKS
        if s < n:
            F = m.F[s % 2]
            dve.wait_ge(self.act.sem, self.act.at(b, f"tanh{s}"))
            if exists(b if s else b - 1):
                dve.wait_ge(self.dve.sem, self.dve.at(b if s else b - 1, f"hid{(s - 1) % n}"))
            dve.scalar_tensor_tensor(self.w.silu[:, :], self.w.th[:, :], 1.0, F[:, 0:N], ALU.add, ALU.mult)\
               .then_inc(self.dve.sem, 1)
            dve.wait_ge(self.dve.sem, self.dve.at(b, f"silu{s}"))
            if s == 0:
                if exists(b - 1):
                    dve.wait_ge(self.pe.sem, self.pe.at(b - 1, "out"))
            dve.scalar_tensor_tensor(self.w.hid[:, s, :], self.w.silu[:, :], 0.5, F[:, N:2 * N], ALU.mult, ALU.mult)\
               .then_inc(self.dve.sem, 1)
        if s == n:
            dve.wait_ge(self.act.sem, self.act.at(b, "tanh"))
            dve.scalar_tensor_tensor(self.gate(b, u), self.w.th[:, :].rearrange("p (k c) -> p k c", k=TT), 1.0,
                                     m.F[n % 2][:, 0:N].rearrange("p (k c) -> p k c", k=TT), ALU.add, ALU.mult)\
               .then_inc(self.dve.sem, 1)

    def gpsimd(self, pool, b, u):
        pass

    def gate_ready(self, eng, b):
        eng.wait_ge(self.dve.sem, self.dve.at(b, "gate"))


class Holder:
    pass


def layer0(nc, ctx, load, m):
    def sb(name, shape, dt=F32):
        return ctx.enter_context(nc.sbuf_tensor(name, shape, dt))

    w = Holder()
    w.w = {}
    for key, src in (("A", "L0_attn_WkT"), ("B", "L0_attn_WqT"), ("V", "L0_attn_WvT"), ("O", "L0_attn_WoT")):
        t = sb(f"l0_{key}", [P, P])
        load(t[:, :], src)
        w.w[key] = t[:, :]
    w.bA, w.bB, w.bv = (sb(f"l0_{x}", [P, 1]) for x in ("bA", "bB", "bv"))
    load(w.bA[:, :], "L0_attn_bk", col=True)
    load(w.bB[:, :], "L0_attn_bq", col=True)
    load(w.bv[:, :], "L0_attn_bv", col=True)
    w.w["bA"], w.w["bB"] = w.bA[:, :], w.bB[:, :]
    w.bo = sb("l0_bo", [1, P])
    load(w.bo[:, :], "L0_attn_bo", row=True)
    w.w["bo"] = w.bo2 = sb("l0_bo2", [1, P])
    w.w["bo"] = w.bo2[:, :]
    w.ints = m.prob[:, 0:3, 0:384].bitcast(I32)
    load(w.ints[:, 0, :], "L0_ffn_w_gateT")
    load(w.ints[:, 1, :], "L0_ffn_w_upT")
    load(w.ints[:, 2, :].rearrange("p (c n) -> p c n", c=3), "L0_ffn_w_downT", chunks=3)
    w.gate_up = sb("l0_gate_up", [P, 2, 384])
    w.down = sb("l0_down", [P, 3, P])
    w.th, w.silu, w.hid = sb("l0_th", [P, N]), sb("l0_silu", [P, N]), sb("l0_hid", [P, 3, N])
    return w


def layer1(nc, ctx, load, m, w2):
    def sb(name, shape, src, **how):
        t = ctx.enter_context(nc.sbuf_tensor(f"l1_{name}", shape, F32))
        load(t[:, :] if len(shape) == 2 else t[:, :, :], src, **how)
        return t

    w = Holder()
    w.Wz, w.Wh = sb("Wz", [P, P], "L1_attn_Wz"), sb("Wh", [P, P], "L1_attn_Wh")
    w.bz, w.bh = sb("bz", [P, 1], "L1_attn_bz", col=True), sb("bh", [P, 1], "L1_attn_bh", col=True)
    w.diffuse = sb("diffuse", [P, P], "L1_attn_log_D", every=True)
    w.lap = sb("lap", [P, P], "const_lap")
    w.enc, w.enc_b = sb("enc", [P, N], "L1_ffn_enc_W"), sb("enc_b", [P, 2], "L1_ffn_enc_b")
    w.s2c, w.s2c_b = sb("s2c", [P, 2, 64], "L1_ffn_s2c_W"), sb("s2c_b", [64, 1], "L1_ffn_s2c_b", col=True)
    w.rW1, w.We1, w.c2s = (ctx.enter_context(nc.sbuf_tensor(f"l1_{x}", [P] + shape, F32))
                           for x, shape in (("rW1", [64]), ("We1", [8, P]), ("c2s", [N])))
    load(w.rW1[0:64, :], "L1_ffn_rW1")
    load(w.We1[0:64, :, :], "L1_ffn_We1")
    load(w.c2s[0:64, :], "L1_ffn_c2s_W")
    w.rb1 = sb("rb1", [64, 1], "L1_ffn_rb1", col=True)
    w.rW2 = sb("rW2", [64, 8], "L1_ffn_rW2")
    w.rb2 = ctx.enter_context(nc.sbuf_tensor("l1_rb2", [P, TT, 8], F32))
    for k in range(TT):
        load(w.rb2[:, k, :], "L1_ffn_rb2", every=True)
    w.be1 = sb("be1", [P, 8], "L1_ffn_be1T")
    w.We2, w.be2 = sb("We2", [P, 8, 64], "L1_ffn_We2"), sb("be2", [8, 64], "L1_ffn_be2")
    w.c2s_b = sb("c2s_b", [P, 2], "L1_ffn_c2s_b")
    w.dec, w.dec_b = sb("dec", [P, 2, P], "L1_ffn_dec_W"), sb("dec_b", [1, P], "L1_ffn_dec_b", row=True)
    w.ln_g, w.ln_b = sb("ln_g", [P, P], "L1_ffn_ln_g", every=True), sb("ln_b", [P, P], "L1_ffn_ln_b", every=True)
    w.v0, w.v, w.v2, w.eq, w.one, w.ohs = w2.v0, w2.v, w2.v2, w2.eq, w2.one, w2.ohs
    w.mx, w.vrec, w.weight = w2.mx, w2.vrec, w2.weight
    pair = [m.prob[:, i, :].rearrange("p (a n) -> p a n", a=2) for i in range(PRING)]
    w.th, w.spikes, w.th2, w.spikes2 = pair[0:4]
    w.hid = pair[4:6]
    w.zth, w.keep, w.take, w.drive = (m.prob[:, 6 + i // 2, N * (i % 2):N * (i % 2) + N] for i in range(4))
    w.hT = [m.oTn[u][:, 0, :] for u in range(2)]
    w.contT = [m.oTn[u][:, 1, :] for u in range(2)]
    w.r1T, w.outT = m.oTn[0][0:64, 2, :], m.oTn[1][:, 2, :]
    w.acc = [m.rest[:, u, :] for u in range(2)]
    w.dth, w.yn, w.y, w.gth = (m.turned[:, i // 2, N * (i % 2):N * (i % 2) + N].rearrange("p (k c) -> p k c", k=TT)
                               for i in range(4))
    w.gate = m.oTn[0][:, 3, :].rearrange("p (k c) -> p k c", k=TT)
    w.gT = m.oT[0:8, :]
    w.stats, w.mean_var = w2.stats, w2.mean_var
    w.var_eps, w.rstd = w2.var_eps, w2.rstd
    return w


def layer1_weights(nc, ctx, m, w):
    s_exp = ctx.enter_context(nc.semaphore("l1w_exp"))
    s_mul = ctx.enter_context(nc.semaphore("l1w_mul"))
    with nc.Block() as block:
        @block.scalar
        def _(act):
            act.activation(m.xn[:, 0, :], w.diffuse[:, :], ACT.Exp).then_inc(s_exp, 1)

        @block.vector
        def _(dve):
            for a in (w.rW1[64:P, :], w.We1[64:P, :, :], w.c2s[64:P, :], w.contT[0][64:P, :], w.contT[1][64:P, :],
                      w.outT[64:P, :]):
                dve.memset(a, 0.0)
            for b in (w.bz, w.enc_b, w.c2s_b):
                dve.tensor_scalar(b[:, :], b[:, :], 0.5, None, ALU.mult)
            dve.wait_ge(s_exp, 1)
            dve.tensor_tensor(m.xn[:, 1, :], m.xn[:, 0, :], w.lap[:, :], ALU.mult).then_inc(s_mul, 1)
            dve.wait_ge(s_mul, 1)
            dve.tensor_tensor(w.diffuse[:, :], m.xn[:, 1, :], m.ident[:, :], ALU.add)


class Precomputed(Gated):

    def open(self, nc, sem, m, xnT_act):
        self.m = m
        return self

    def tensor(self, pe, b, u, s):
        pass

    scalar = vector = tensor

    def gpsimd(self, pool, b, u):
        pass

    def gate_ready(self, eng, b):
        pass


class GatheredFfn(Gated):

    def __init__(self, w):
        self.w = w

    def open(self, nc, sem, m, xnT_act):
        self.m = m
        self.pool = Steps(sem("ffn_pool"), "slots shares")
        self.rows = Steps(sem("ffn_rows"), ["in"], 16 * 2 * TT)
        self.dve = Steps(sem("ffn_dve"), "first second gate")
        self.act = Steps(sem("ffn_act"), "tanh")
        return self

    def tensor(self, pe, b, u, s):
        pass

    def scalar(self, act, b, u, s):
        if s == 5:
            act.wait_ge(self.dve.sem, self.dve.at(b, "second"))
            act.activation(self.w.mix_th, self.w.mix, ACT.Tanh, scale=0.5).then_inc(self.act.sem, 1)

    def vector(self, dve, b, u, s):
        w = self.w
        if s == 4:
            dve.wait_ge(self.rows.sem, self.rows.at(b, "in"))
            if exists(b - 1):
                dve.wait_ge(self.dve.sem, self.dve.at(b - 1, "gate"))
            for k in range(TT):
                a = dve.tensor_scalar(w.mix[:, k, :], w.rows[u][:, 2 * k, :], w.share_of[u][:, 2 * k:2 * k + 1], None,
                                      ALU.mult)
            a.then_inc(self.dve.sem, 1)
            dve.wait_ge(self.dve.sem, self.dve.at(b, "first"))
            for k in range(TT):
                a = dve.scalar_tensor_tensor(w.mix[:, k, :], w.rows[u][:, 2 * k + 1, :],
                                             w.share_of[u][:, 2 * k + 1:2 * k + 2], w.mix[:, k, :], ALU.mult, ALU.add)
            a.then_inc(self.dve.sem, 1)
        if s == 6:
            dve.wait_ge(self.act.sem, self.act.at(b, "tanh"))
            dve.scalar_tensor_tensor(self.gate(b, u), w.mix_th, 1.0, w.mix, ALU.add, ALU.mult)\
               .then_inc(self.dve.sem, 1)

    def gpsimd(self, pool, b, u):
        if b is None:
            return
        w = self.w
        if exists(b - 2):
            pool.wait_ge(self.dve.sem, self.dve.at(b - 2, "second"))
            own_wait(pool)
        pool.tensor_copy(w.slot_of[u][:, :], w.slots[:, bass.ds(2 * TT * b, 2 * TT)]).then_inc(self.pool.sem, 1)
        pool.tensor_copy(w.share_of[u][:, :], w.shares[:, bass.ds(2 * TT * b, 2 * TT)]).then_inc(self.pool.sem, 1)
        pool.wait_ge(self.pool.sem, self.pool.at(b, "shares"))
        if exists(b - 1):
            pool.wait_ge(self.rows.sem, self.rows.at(b - 1, "in"))
        own_wait(pool)
        for i in range(2 * TT):
            pool.indirect_dma_start(w.rows[u][:, i, :], None, self.m.sorted_y,
                                    bass.IndirectOffsetOnAxis(ap=w.slot_of[u][:, i:i + 1], axis=0))\
                .then_inc(self.rows.sem, 16)

    def gate_ready(self, eng, b):
        eng.wait_ge(self.dve.sem, self.dve.at(b, "gate"))


def moe_weights(nc, ctx, m, tag, experts):
    def sb(name, shape, dt=F32):
        return ctx.enter_context(nc.sbuf_tensor(f"{tag}_{name}", shape, dt))

    w, K = Holder(), 8
    first = experts - K
    w.experts = experts
    w.W1, w.W2 = m.W1[:, 0:experts, :], m.W2[:, 0:experts, :, :]
    w.b1 = sb("b1", [P, experts, 4])
    w.router, w.b2 = sb("router", [P, K]), sb("b2", [K, P])
    w.v0, w.v, w.v2, w.eq = (sb(x, [P, TT, K]) for x in ("v0", "v", "v2", "eq"))
    w.mx, w.vsum, w.vrec = (sb(x, [P, TT, 1]) for x in ("mx", "vsum", "vrec"))
    w.one, w.ohs = sb("one", [P, TT, 2 * K]), sb("onehots", [P, TT, K])
    w.weight = [sb(f"weight{u}", [P, TT, K]) for u in range(2)]
    w.gT = [sb(f"gT{u}", [K, N]) for u in range(2)]
    w.hT = [m.prob[:, 2 * r:2 * r + 2, :].rearrange("p a (b n) -> p (a b) n", b=2) for r in range(4)]
    tiles = [m.rc[:, N * i:N * i + N] for i in range(2)] + [m.rest[:, 0, :]]
    w.acc, w.th, w.xr = (t.rearrange("p (k c) -> p k c", k=TT) for t in tiles)
    w.stats, w.mean_var = sb("stats", [P, TT, 6]), sb("mean_var", [P, TT, 2])
    w.var_eps, w.rstd = sb("var_eps", [P, TT]), sb("rstd", [P, TT])
    w.xT = [m.turned[:, 0, N * u:N * u + N] for u in range(2)]
    w.xk = [m.turned[:, 1, N * u:N * u + N].rearrange("p (k c) -> p k c", k=TT) for u in range(2)]
    w.sq, w.sq2, w.r2 = sb("sq", [P, TT]), sb("sq2", [P, TT]), sb("r2", [P, TT])
    w.b2s = sb("b2s", [1, first, P])
    w.g = sb("g", [P, 2])
    return w


def layer3(nc, ctx, load, m):
    def sb(name, shape, dt=F32):
        return ctx.enter_context(nc.sbuf_tensor(f"l3_{name}", shape, dt))

    w = Holder()
    w.router, w.router_b = sb("router", [P, 8]), sb("router_b", [P, 1, 8])
    load(w.router[:, :], "L3_ffn_gate_wT")
    load(w.router_b[:, 0, :], "L3_ffn_gate_b", every=True)
    w.cnt2, w.counts = sb("chosen", [P, 16]), sb("counts", [P, 16])
    w.G = G = 4
    w.slot, w.is_kept, w.share = (sb(x, [P, 2 * G]) for x in ("slot", "is_kept", "share"))
    w.index = [sb(f"index{u}", [P, 2 * G], I32) for u in range(2)]
    w.g_v0, w.g_v, w.g_v2, w.g_eq = (sb(f"g_{x}", [P, G, 8]) for x in ("v0", "v", "v2", "eq"))
    w.g_one, w.g_kept, w.place = (sb(f"g_{x}", [P, G, 16]) for x in ("one", "kept", "place"))
    w.g_mx, w.g_vsum, w.g_vrec = (sb(f"g_{x}", [P, G, 1]) for x in ("mx", "vsum", "vrec"))
    w.gstats, w.gmean_var = sb("g_stats", [P, G, 6]), sb("g_mean_var", [P, G, 2])
    w.gvar_eps, w.grstd = sb("g_var_eps", [P, G]), sb("g_rstd", [P, G])
    w.xnT = [m.rc[:, :], m.rest[:, :, :].rearrange("p a n -> p (a n)")]
    w.slots, w.shares = sb("slots", [P, 2 * B * TT], I32), sb("shares", [P, 2 * B * TT])
    w.slot_of = [sb(f"slot_of{u}", [P, 4], I32) for u in range(2)]
    w.share_of = [sb(f"share_of{u}", [P, 4]) for u in range(2)]
    w.xs = [m.turned[:, u, :].rearrange("p (k c) -> p k c", k=G) for u in range(2)]
    free1 = m.W1[:, :, :].rearrange("p e n -> p (e n)")
    free2 = m.W2[:, :, :, :].rearrange("p e c n -> p (e c n)")
    rows = ST * D
    w.ex = []
    for u in range(2):
        x = Holder()
        x.W1, x.W2 = free1[:, 512 * u:512 * u + 512], free2[:, 512 * u:512 * u + 512]
        x.x, x.xT, x.y = (free1[:, 1024 + rows * (2 * i + u):1024 + rows * (2 * i + u + 1)] for i in range(3))
        x.x, x.y = (a.rearrange("p (s d) -> p s d", d=D) for a in (x.x, x.y))
        x.b2 = free2[:, 1024 + D * u:1024 + D * u + D]
        x.b1 = free2[:, 1280 + 4 * u:1280 + 4 * u + 4]
        w.ex.append(x)
    w.h = [a.rearrange("p (c n) -> p c n", c=4) for a in
           (free2[:, 1536:1536 + 4 * rows], m.prob[:, :, :].rearrange("p a n -> p (a n)")[:, 0:4 * rows])]
    w.rows = [m.W1[:, u, :].rearrange("p (i d) -> p i d", d=D) for u in range(2)]
    w.mix, w.mix_th = (m.W1[:, 2, N * i:N * i + N].rearrange("p (k d) -> p k d", d=D) for i in range(2))
    w.w = {}
    for key, src in (("A", "L3_attn_W_qT"), ("Ar", "L3_attn_W_qTs"), ("B", "L3_attn_W_kT"), ("Br", "L3_attn_W_kTs"),
                     ("V", "L3_attn_W_vT"), ("O", "L3_attn_W_oT")):
        t = ctx.enter_context(nc.sbuf_tensor(f"l3_{key}", [P, P], F32))
        load(t[:, :], src)
        w.w[key] = t[:, :]
    return w


def layer2(nc, ctx, load, m):
    w = moe_weights(nc, ctx, m, "l2", 10)

    def sb(name, shape, dt=F32):
        return ctx.enter_context(nc.sbuf_tensor(f"l2_{name}", shape, dt))
    load(w.W1[:, 0:2, :], "L2_ffn_W1_s")
    load(w.W1[:, 2:10, :], "L2_ffn_W1_r")
    load(w.W2[:, 0:2, :, :], "L2_ffn_W2_s")
    load(w.W2[:, 2:10, :, :], "L2_ffn_W2_r")
    load(w.b1[:, 0:2, :], "L2_ffn_b1_s")
    load(w.b1[:, 2:10, :], "L2_ffn_b1_r")
    load(w.router[:, :], "L2_ffn_centroids")
    load(w.b2[:, :], "L2_ffn_b2_r")
    load(w.b2s[:, :, :].rearrange("a e n -> a (e n)"), "L2_ffn_b2_s", row=True)
    load(w.g[:, 0:1], "L2_ffn_g_shared", col=True)
    load(w.g[:, 1:2], "L2_ffn_g_routed", col=True)
    w.dq = m.prob[0:32, 4, 0:128]
    w.uqT = m.prob[0:32, 4, 128:256]
    w.dkv = m.prob[0:32, 4, 256:384]
    w.uk = m.prob[:, 5, 128:160]
    w.uv = m.prob[:, 5, 160:192]
    w.oT = m.prob[:, 5, 192:320]
    load(w.dq[:, :], "L2_attn_W_dq", stage="layer2")
    load(w.uqT[:, :], "L2_attn_W_uqT", stage="layer2")
    load(w.dkv[:, :], "L2_attn_W_dkv", stage="layer2")
    load(w.uk[:, :], "L2_attn_W_uk", stage="layer2")
    load(w.uv[:, :], "L2_attn_W_uv", stage="layer2")
    load(w.oT[:, :], "L2_attn_W_oT", stage="layer2")
    w.qT = m.prob[:, 5, 320:448]
    w.keffT = m.prob[0:32, 4, 384:512]
    w.veff = m.prob[0:32, 5, 0:128]
    w.w = {k: sb(k, [P, P]) for k in "ABV"}
    w.w = {k: t[:, :] for k, t in w.w.items()}
    return w


def layer2_weights(nc, ctx, m, w, factors):
    def sem(name):
        return ctx.enter_context(nc.semaphore(f"l2w_{name}"))
    s_pe, s_dve, s_factors = sem("pe"), sem("dve"), sem("factors")
    with nc.Block() as block:
        @block.sync
        def _(sp):
            for dst, src in factors:
                sp.dma_start(dst, src).then_inc(s_factors, 16)

        @block.tensor
        def _(pe):
            pe.wait_ge(s_factors, 16 * len(factors))
            pe.matmul(m.S[0][:, 0:P], w.dq[:, :], w.uqT[:, :], start=True, stop=True).then_inc(s_pe, 1)
            pe.matmul(m.S[1][:, 0:P], w.uqT[:, :], w.dq[:, :], start=True, stop=True).then_inc(s_pe, 1)
            pe.matmul(m.T[0][0:32, 0:P], w.uv[:, :], w.oT[:, :], start=True, stop=True).then_inc(s_pe, 1)
            pe.wait_ge(s_dve, 3)
            pe.matmul(m.T[1][0:32, 0:P], w.uk[:, :], w.qT[:, :], start=True, stop=True).then_inc(s_pe, 1)
            pe.matmul(m.F[0][:, 0:P], w.dkv[:, :], w.veff[:, :], start=True, stop=True).then_inc(s_pe, 1)
            pe.wait_ge(s_dve, 4)
            pe.matmul(m.F[1][:, 0:P], w.dkv[:, :], w.keffT[:, :], start=True, stop=True).then_inc(s_pe, 1)

        @block.vector
        def _(dve):
            moves = [(w.w["A"], m.S[0][:, 0:P]), (w.qT[:, :], m.S[1][:, 0:P]), (w.veff[:, :], m.T[0][0:32, 0:P]),
                     (w.keffT[:, :], m.T[1][0:32, 0:P]), (w.w["V"], m.F[0][:, 0:P]), (w.w["B"], m.F[1][:, 0:P])]
            for i, (dst, src) in enumerate(moves):
                dve.wait_ge(s_pe, i + 1)
                dve.tensor_scalar(dst, src, 0.5 if i == 4 else 1.0, None, ALU.mult).then_inc(s_dve, 1)
            dve.tensor_scalar(w.W1[:, 0:2, :], w.W1[:, 0:2, :], w.g[:, 0:1], None, ALU.mult)
            dve.tensor_scalar(w.W1[:, 2:10, :], w.W1[:, 2:10, :], w.g[:, 1:2], None, ALU.mult)


def build(nc, args, layers):
    ctx = ExitStack()
    with ctx:
        m = Memory(nc, ctx)
        loads = {"first": [], "later": [], "layer2": []}

        def load(dst, name, col=False, row=False, every=False, chunks=None, stage="first"):
            src = args[name]
            if every:
                src = src.rearrange("(a p) -> a p", a=1).broadcast_to([P, src.shape[0]])
            if col:
                src = src.rearrange("(p a) -> p a", a=1)
            if row:
                src = src.rearrange("(a p) -> a p", a=1)
            if chunks:
                src = src.rearrange("(c p) n -> p c n", c=chunks)
            loads[stage].append((dst, src))

        def load_later(dst, name, **how):
            load(dst, name, **{"stage": "later", **how})

        load(m.ident[:, :], "const_ident")
        load(m.tri[:, :, :], "const_tri")
        load(m.cossin[:, :], "const_cossin")
        load(m.upto[:, :], "const_upto")
        load(m.rank[:, :, :], "const_rank")
        load(m.first_slot[:, :, :], "const_first_slot")
        load(m.spare[:, :], "const_spare")
        load(m.X[:, :, :], "x_tiles")
        w0 = layer0(nc, ctx, load, m)
        w2 = layer2(nc, ctx, load_later, m)
        w1 = layer1(nc, ctx, load_later, m, w2)
        w3 = layer3(nc, ctx, load_later, m)
        s_later = ctx.enter_context(nc.semaphore("s_later"))
        s_load = ctx.enter_context(nc.semaphore("s_load"))
        s_zero_stack = ctx.enter_context(nc.semaphore("s_zero_stack"))
        s_prep = ctx.enter_context(nc.semaphore("s_prep"))
        s_bias = ctx.enter_context(nc.semaphore("s_bias"))
        s_zero = ctx.enter_context(nc.semaphore("sorted_x_zeroed"))

        def zero_sorted(eng):
            eng.dma_start(m.sorted_x.rearrange("(p s) d -> p s d", p=P),
                          m.zeros[:, :, :].broadcast_to([P, XROWS // P, D])).then_inc(s_zero, 16)

        with nc.Block() as block:
            @block.sync
            def _(sp):
                for dst, src in loads["first"]:
                    sp.dma_start(dst, src).then_inc(s_load, 16)

            @block.scalar
            def _(act):
                for dst, src in loads["later"]:
                    act.dma_start(dst, src).then_inc(s_later, 16)

            @block.tensor
            def _(pe):
                pe.wait_ge(s_load, 16 * len(loads["first"]))
                pe.matmul(m.M[0:1, 0:P], w0.bv[:, :], w0.w["O"], start=True, stop=True).then_inc(s_bias, 1)

            @block.gpsimd
            def _(pool):
                for o in range(2):
                    pool.memset(m.stack[o][1][:, :, :].rearrange("p h n -> p (h n)").bitcast(U32), 0)\
                        .then_inc(s_zero_stack, 1)

            @block.vector
            def _(dve):
                dve.memset(m.ones[:, :], 1.0)
                dve.memset(m.zeros[:, 0, :], 0.0)
                dve.memset(m.minus_half[:, :], -0.5)
                dve.memset(w3.counts[:, :], 0.0)
                for o in range(2):
                    dve.memset(m.stack[o][0][:, :, :].rearrange("p h n -> p (h n)").bitcast(U32), 0)
                for u in range(2):
                    dve.memset(m.vaug[u][:, :, :, :].rearrange("p a b c -> p (a b c)"), 0.0).then_inc(s_prep, 1)
                dve.wait_ge(s_prep, 2)
                dve.wait_ge(s_zero_stack, 2)
                for u in range(2):
                    dve.memset(m.stack[1][u][SHIFT_ROW:SHIFT_ROW + 2, :, :].rearrange("p h n -> p (h n)"), 1.0)
                    dve.memset(m.vaug[u][:, :, :, HD:HD + 1], 1.0)
                dve.wait_ge(s_load, 16 * len(loads["first"]))
                dve.tensor_scalar(w0.gate_up[:, :, :], w0.ints[:, 0:2, :], float(np.float32(1 / 127.0)), None, ALU.mult)
                dve.tensor_scalar(w0.down[:, :, :].rearrange("p c n -> p (c n)"), w0.ints[:, 2, :],
                                  float(np.float32(1 / 127.0)), None, ALU.mult)
                dve.tensor_copy(m.ident_b[:, :], m.ident[:, :])
                for k in range(2):
                    for i in range(2):
                        dve.tensor_copy(m.tri2[:, k, i, :], m.tri[:, k, :])
                dve.wait_ge(s_bias, 1)
                dve.tensor_tensor(w0.bo2[:, :], m.M[0:1, 0:P], w0.bo[:, :], ALU.add).then_inc(s_prep, 1)
        if 0 in layers:
            attention_layer(nc, m, w0, "l0", causal=False, scale=float(1 / np.float32(np.sqrt(128))), bias=True,
                            rope=False, project=True, ffn=SwigluFfn(w0), store=args["out"] if layers[-1] == 0 else None)
        with nc.Block() as block:
            @block.vector
            def _(dve):
                dve.wait_ge(s_later, 16 * len(loads["later"]))
        layer1_weights(nc, ctx, m, w1)
        if 1 in layers:
            recurrent_layer(nc, m, w1, store=args["out"] if layers[-1] == 1 else None)
        layer2_weights(nc, ctx, m, w2, loads["layer2"])
        if 2 in layers:
            moe_layer(nc, m, w2, "l2f")
            attention_layer(nc, m, w2, "l2", causal=True, scale=float(1 / np.sqrt(np.float32(HD))), bias=False,
                            rope=False, project=False, ffn=Precomputed(), store=args["out"] if layers[-1] == 2 else None,
                            prefetch=zero_sorted)
        if 3 in layers:
            with nc.Block() as block:
                @block.sync
                def _(sp):
                    if 2 not in layers:
                        zero_sorted(sp)
                    sp.wait_ge(s_zero, 16)
            dispatch_layer(nc, m, w3)
            experts_layer(nc, m, w3, args["L3_ffn_W1"], args["L3_ffn_W2"], args["L3_ffn_b1"], args["L3_ffn_b2"])
            attention_layer(nc, m, w3, "l3", causal=True, scale=float(1 / np.sqrt(np.float32(HD))), bias=False,
                            rope=True, project=True, ffn=GatheredFfn(w3), store=args["out"])


_HOST = {
    "L0_attn_WqT": ("L0_attn_Wq", "T"), "L0_attn_WkT": ("L0_attn_Wk", "T"), "L0_attn_WvT": ("L0_attn_Wv", "T"),
    "L0_attn_WoT": ("L0_attn_Wo", "T"), "L0_attn_bq": ("L0_attn_bq", ""), "L0_attn_bk": ("L0_attn_bk", ""),
    "L0_attn_bv": ("L0_attn_bv", ""), "L0_attn_bo": ("L0_attn_bo", ""),
    "L0_ffn_w_gateT": ("L0_ffn_w_gate", "T"), "L0_ffn_w_upT": ("L0_ffn_w_up", "T"),
    "L0_ffn_w_downT": ("L0_ffn_w_down", "T"),
    **{n: (n, "") for n in "L1_attn_Wz L1_attn_Wh L1_attn_bz L1_attn_bh L1_attn_log_D L1_ffn_enc_W L1_ffn_s2c_b "
       "L1_ffn_rW1 L1_ffn_rb1 L1_ffn_rW2 L1_ffn_rb2 L1_ffn_be2 L1_ffn_c2s_W L1_ffn_dec_b L1_ffn_ln_g "
       "L1_ffn_ln_b".split()},
    **{n: (n, "chunks") for n in ("L1_ffn_enc_b", "L1_ffn_c2s_b", "L1_ffn_s2c_W", "L1_ffn_dec_W")},
    "L1_ffn_We1": ("L1_ffn_We1", "W1"), "L1_ffn_We2": ("L1_ffn_We2", "W1"), "L1_ffn_be1T": ("L1_ffn_be1", "T"),
    "L2_attn_W_dq": ("L2_attn_W_dq", ""), "L2_attn_W_uqT": ("L2_attn_W_uq", "T"),
    "L2_attn_W_dkv": ("L2_attn_W_dkv", ""), "L2_attn_W_uk": ("L2_attn_W_uk", ""),
    "L2_attn_W_uv": ("L2_attn_W_uv", ""), "L2_attn_W_oT": ("L2_attn_W_o", "T"),
    "L2_ffn_centroids": ("L2_ffn_centroids", ""), "L2_ffn_b2_r": ("L2_ffn_b2_r", ""),
    "L2_ffn_b2_s": ("L2_ffn_b2_s", "flat"), "L2_ffn_g_shared": ("L2_ffn_g_shared", ""),
    "L2_ffn_g_routed": ("L2_ffn_g_routed", ""),
    "L2_ffn_W1_s": ("L2_ffn_W1_s", "W1"), "L2_ffn_W1_r": ("L2_ffn_W1_r", "W1"),
    "L2_ffn_W2_s": ("L2_ffn_W2_s", "W2"), "L2_ffn_W2_r": ("L2_ffn_W2_r", "W2"),
    "L2_ffn_b1_s": ("L2_ffn_b1_s", "b1"), "L2_ffn_b1_r": ("L2_ffn_b1_r", "b1"),
    "L3_ffn_W1": ("L3_ffn_W1", "W1"), "L3_ffn_W2": ("L3_ffn_W2", "W2"), "L3_ffn_b1": ("L3_ffn_b1", "b1"),
    "L3_ffn_b2": ("L3_ffn_b2", ""), "L3_ffn_gate_wT": ("L3_ffn_gate_w", "T"), "L3_ffn_gate_b": ("L3_ffn_gate_b", ""),
    "L3_attn_W_qT": ("L3_attn_W_q", "T"), "L3_attn_W_qTs": ("L3_attn_W_q", "swap"),
    "L3_attn_W_kT": ("L3_attn_W_k", "T"), "L3_attn_W_kTs": ("L3_attn_W_k", "swap"),
    "L3_attn_W_vT": ("L3_attn_W_v", "T"), "L3_attn_W_oT": ("L3_attn_W_o", "T"),
}


def laid_out(a, how):
    if how == "T":
        return a.T
    if how == "swap":
        return a.reshape(P // 2, 2, P)[:, ::-1].reshape(P, P).T
    if how == "W1":
        return a.transpose(1, 0, 2)
    if how == "W2":
        return a.reshape(a.shape[0], 4, P, D).transpose(2, 0, 1, 3)
    if how == "b1":
        return a.reshape(a.shape[0], 4, P).transpose(2, 0, 1)
    if how == "chunks":
        return np.moveaxis(a.reshape((2, P) + a.shape[1:]), 0, 1)
    return a.reshape(-1) if how == "flat" else a


def constants():
    f = np.arange(P)
    tri = np.stack([np.where(f[None, :] > f[:, None], MASKED, 0.0), np.where(f[:, None] > f[None, :], MASKED, 0.0)], 1)
    inv = np.float32(10000.0) ** (np.float32(-2.0) * np.arange(HD // 2, dtype=np.float32) / np.float32(HD))
    ang = np.arange(N, dtype=np.float32)[None, :] * inv.astype(np.float32)[(f % HD) // 2][:, None]
    sign = np.where(f % 2 == 0, -1.0, 1.0)[:, None]
    return {
        "const_ident": np.eye(P, dtype=np.float32),
        "const_upto": (f[:, None] <= f[None, :]).astype(np.float32),
        "const_rank": np.ascontiguousarray(np.broadcast_to(8.0 - np.arange(8, dtype=np.float32), (P, TT, 8))),
        "const_lap": sum(np.roll(np.eye(P, dtype=np.float32), i, 1) for i in (1, -1))
        - np.float32(2.0) * np.eye(P, dtype=np.float32),
        "const_first_slot": np.ascontiguousarray(np.broadcast_to(
            (np.arange(8)[None, :] * SLOTS_OF_EXPERT + np.arange(2)[:, None] * CAPACITY - 1).reshape(16)
            .astype(np.float32), (P, TT, 16))),
        "const_spare": np.ascontiguousarray(np.broadcast_to(
            (XROWS + f)[:, None].astype(np.float32), (P, 2 * TT))),
        "const_tri": tri.astype(np.float32),
        "const_cossin": np.concatenate([np.cos(ang), sign * np.sin(ang)], 1).astype(np.float32),
    }


def host_arrays(inputs):
    arrays = dict(constants())
    x = np.asarray(inputs["L0_attn_x"]).reshape(B * TT, P, D)
    arrays["x_tiles"] = np.ascontiguousarray(x.transpose(1, 0, 2))
    for name, (src, how) in _HOST.items():
        a = np.asarray(inputs[src])
        arrays[name] = np.ascontiguousarray(laid_out(a, how))
    return arrays


LAYERS = (0, 1, 2, 3)


def kernel(**inputs):
    import concourse.bacc as bacc
    from concourse.bass_utils import run_bass_kernel_spmd

    nc = bacc.Bacc("TRN2", target_bir_lowering=False, num_devices=1)
    arrays = host_arrays(inputs)
    args = {k: nc.dram_tensor(k, a.shape, mybir.dt.from_np(a.dtype), kind="ExternalInput").ap()
            for k, a in arrays.items()}
    args["out"] = nc.dram_tensor("out", [P, B * TT, D], F32, kind="ExternalOutput").ap()
    build(nc, args, LAYERS)
    got = run_bass_kernel_spmd(nc, [arrays], core_ids=[0]).results[0]["out"]
    return np.ascontiguousarray(got.transpose(1, 0, 2)).reshape(B, N, D)
```
